# Optimizing a Trainium2 kernel written in Bass

```python
import numpy as np
import jax
import jax.numpy as jnp

def _softmax(x, axis=-1):
    return jax.nn.softmax(x, axis=axis)

def _gelu(x):
    return jax.nn.gelu(x, approximate=True)

def _silu(x):
    return jax.nn.silu(x)

def _sigmoid(x):
    return jax.nn.sigmoid(x)

def _layernorm(x, axis=-1, eps=1e-05):
    m = jnp.mean(x, axis=axis, keepdims=True)
    v = jnp.var(x, axis=axis, keepdims=True)
    return (x - m) / jnp.sqrt(v + eps)

def _scatter_add(tgt, idx, src, axis=0):
    return tgt.at[idx].add(src)

def _segment_sum(src, seg, n):
    return jax.ops.segment_sum(src, seg, n)
kernel_name = 'mk_audio_tower_d1_tok_audfeat256_r4_fa98e5'

def setup_inputs(seed: int=0):
    np.random.seed(seed)
    _w = jnp.asarray

    def _rec_inputs():
        import jax
        import jax.numpy as jnp
        _rk = jax.random.key(seed)
        x = -0.00197248 + 1.00072 * jax.random.normal(jax.random.fold_in(_rk, 1), (32, 1, 10240), jnp.float32)
        return x
    x = _rec_inputs()

    def _L0_tok_setup():
        import jax, jax.numpy as jnp
        import numpy as np
        B, L = (4, 10240)
        C = 128
        DMLP = 512
        TEMP = 1e-05
        EPS = 1e-05
        FACTOR = 2

        def _conv(x, w, b, stride, pad):
            x = jnp.pad(x, ((0, 0), (0, 0), (pad, pad)), mode='reflect')
            y = jax.lax.conv_general_dilated(x, w, (stride,), 'VALID', dimension_numbers=('NCH', 'OIH', 'NCH'))
            return y + b[None, :, None]

        def _cnorm(x, g, b):
            m = jnp.mean(x, axis=1, keepdims=True)
            v = jnp.var(x, axis=1, keepdims=True, ddof=1)
            return (x - m) * jax.lax.rsqrt(v + EPS) * g[None, :, None] + b[None, :, None]

        def _forward(x, conv0_w, conv0_b, conv1_w, conv1_b, conv2_w, conv2_b, conv3_w, conv3_b, n0_w, n0_b, n1_w, n1_b, n2_w, n2_b, n3_w, n3_b, n4_w, n4_b, mlp_w1, mlp_b1, mlp_w2, mlp_b2, mlp_w3, mlp_b3):
            h = jax.nn.relu(_cnorm(_conv(x, conv0_w, conv0_b, 5, 3), n0_w, n0_b))
            h = jax.nn.relu(_cnorm(_conv(h, conv1_w, conv1_b, 4, 2), n1_w, n1_b))
            h = jax.nn.relu(_cnorm(_conv(h, conv2_w, conv2_b, 2, 1), n2_w, n2_b))
            h = jax.nn.relu(_cnorm(_conv(h, conv3_w, conv3_b, 2, 1), n3_w, n3_b))
            f = jnp.transpose(h, (0, 2, 1))
            T = f.shape[1]
            z = jax.nn.gelu(f @ mlp_w1 + mlp_b1, approximate=False)
            z = jax.nn.gelu(z @ mlp_w2 + mlp_b2, approximate=False)
            imp = jax.nn.sigmoid((z @ mlp_w3 + mlp_b3)[..., 0]) + TEMP
            imp = imp / jnp.sum(imp, axis=1, keepdims=True) * (T / FACTOR)
            Tn = T // FACTOR
            cs = jnp.cumsum(imp, axis=1)
            p = jnp.maximum(cs[:, :, None] - jnp.arange(Tn, dtype=cs.dtype)[None, None, :], 0.0)
            pc = jnp.pad(p, ((0, 0), (0, 0), (0, 1)))
            d = pc[:, :, :-1] - pc[:, :, 1:]
            wmat = d - jnp.pad(d, ((0, 0), (1, 0), (0, 0)))[:, :-1, :]
            pooled = jnp.einsum('btn,btc->bnc', wmat, f)
            out = jnp.transpose(pooled, (0, 2, 1))
            return jax.nn.relu(_cnorm(out, n4_w, n4_b))
        key = jax.random.key(seed)
        ks = jax.random.split(key, 8)

        def w(k, shape, fan_in):
            return jax.random.normal(k, shape, jnp.float32) / np.float32(np.sqrt(fan_in))
        inp = {'x': jax.random.normal(ks[0], (B, 1, L), jnp.float32), 'conv0_w': w(ks[1], (C, 1, 10), 10), 'conv0_b': jnp.zeros(C, jnp.float32), 'conv1_w': w(ks[2], (C, C, 8), C * 8), 'conv1_b': jnp.zeros(C, jnp.float32), 'conv2_w': w(ks[3], (C, C, 4), C * 4), 'conv2_b': jnp.zeros(C, jnp.float32), 'conv3_w': w(ks[4], (C, C, 4), C * 4), 'conv3_b': jnp.zeros(C, jnp.float32), 'mlp_w1': w(ks[5], (C, DMLP), C), 'mlp_b1': jnp.zeros(DMLP, jnp.float32), 'mlp_w2': w(ks[6], (DMLP, DMLP), DMLP), 'mlp_b2': jnp.zeros(DMLP, jnp.float32), 'mlp_w3': w(ks[7], (DMLP, 1), DMLP), 'mlp_b3': jnp.zeros(1, jnp.float32)}
        for i in range(5):
            inp[f'n{i}_w'] = jnp.ones(C, jnp.float32)
            inp[f'n{i}_b'] = jnp.zeros(C, jnp.float32)
        return inp
    _L0_tok_all = _L0_tok_setup()
    _L0_tok_in = {k: v for k, v in _L0_tok_all.items() if k in ('conv0_w', 'conv0_b', 'conv1_w', 'conv1_b', 'conv2_w', 'conv2_b', 'conv3_w', 'conv3_b', 'n0_w', 'n0_b', 'n1_w', 'n1_b', 'n2_w', 'n2_b', 'n3_w', 'n3_b', 'n4_w', 'n4_b', 'mlp_w1', 'mlp_b1', 'mlp_w2', 'mlp_b2', 'mlp_w3', 'mlp_b3')}
    del _L0_tok_all

    def _L0_attn_setup():
        import jax, jax.numpy as jnp
        import numpy as np
        B, T, D = (4, 512, 64)
        W_LORA, A_LORA, G_LORA = (64, 64, 128)
        DECAY_SCALE = -0.6065306597126334
        EPS = D * 1e-05

        def _forward(x, x_mix, W_r, W_k, W_v, W_o, A_w, B_w, b_w, A_a, B_a, b_a, A_g, B_g, k_k, k_a, r_k, gn_w, gn_b):
            b, t, d = x.shape
            shifted = jnp.pad(x, ((0, 0), (1, 0), (0, 0)))[:, :-1]
            delta = shifted - x
            xr, xw, xk, xv, xa, xg = [x + delta * x_mix[i] for i in range(6)]
            r = xr @ W_r
            w = DECAY_SCALE * jax.nn.sigmoid(jnp.tanh(xw @ A_w) @ B_w + b_w)
            k = xk @ W_k
            v = xv @ W_v
            a = jax.nn.sigmoid(xa @ A_a @ B_a + b_a)
            g = jax.nn.sigmoid(xg @ A_g) @ B_g
            kk = k * k_k
            kk = kk / jnp.maximum(jnp.linalg.norm(kk, axis=-1, keepdims=True), 1e-12)
            k = k * (1.0 + (a - 1.0) * k_a)
            decay = jnp.exp(w)

            def step(S, inp):
                r_t, dec_t, k_t, v_t, kk_t, a_t = inp
                b_t = kk_t * a_t
                sa = jnp.einsum('bvk,bk->bv', S, -kk_t)
                S = S * dec_t[:, None, :] + sa[:, :, None] * b_t[:, None, :] + v_t[:, :, None] * k_t[:, None, :]
                o_t = jnp.einsum('bvk,bk->bv', S, r_t)
                return (S, o_t)
            tm = lambda z: jnp.swapaxes(z, 0, 1)
            S0 = jnp.zeros((b, d, d), x.dtype)
            _, o = jax.lax.scan(step, S0, (tm(r), tm(decay), tm(k), tm(v), tm(kk), tm(a)))
            o = jnp.swapaxes(o, 0, 1)
            mu = jnp.mean(o, axis=-1, keepdims=True)
            var = jnp.var(o, axis=-1, keepdims=True)
            o = (o - mu) * jax.lax.rsqrt(var + EPS) * gn_w + gn_b
            o = o + jnp.sum(r * k * r_k, axis=-1, keepdims=True) * v
            return o * g @ W_o
        key = jax.random.key(seed)
        ks = jax.random.split(key, 20)
        n = jax.random.normal
        p = {}
        p['x'] = n(ks[0], (B, T, D), jnp.float32)
        p['x_mix'] = n(ks[1], (6, D), jnp.float32) * 0.1
        s = 1.0 / np.sqrt(D).astype(np.float32)
        p['W_r'] = n(ks[2], (D, D), jnp.float32) * s
        p['W_k'] = n(ks[3], (D, D), jnp.float32) * s
        p['W_v'] = n(ks[4], (D, D), jnp.float32) * s
        p['W_o'] = n(ks[5], (D, D), jnp.float32) * s
        p['A_w'] = n(ks[6], (D, W_LORA), jnp.float32) * s
        p['B_w'] = n(ks[7], (W_LORA, D), jnp.float32) / np.sqrt(W_LORA).astype(np.float32)
        p['b_w'] = n(ks[8], (D,), jnp.float32) * 0.5
        p['A_a'] = n(ks[9], (D, A_LORA), jnp.float32) * s
        p['B_a'] = n(ks[10], (A_LORA, D), jnp.float32) / np.sqrt(A_LORA).astype(np.float32)
        p['b_a'] = n(ks[11], (D,), jnp.float32) * 0.1
        p['A_g'] = n(ks[12], (D, G_LORA), jnp.float32) * s
        p['B_g'] = n(ks[13], (G_LORA, D), jnp.float32) / np.sqrt(G_LORA).astype(np.float32)
        p['k_k'] = n(ks[14], (D,), jnp.float32) * 0.5 + 0.85
        p['k_a'] = n(ks[15], (D,), jnp.float32) * 0.1 + 1.0
        p['r_k'] = n(ks[16], (D,), jnp.float32) * 0.1
        p['gn_w'] = jnp.ones((D,), jnp.float32)
        p['gn_b'] = jnp.zeros((D,), jnp.float32)
        return p
    _L0_attn_all = _L0_attn_setup()
    _L0_attn_in = {k: v for k, v in _L0_attn_all.items() if k in ('x_mix', 'W_r', 'W_k', 'W_v', 'W_o', 'A_w', 'B_w', 'b_w', 'A_a', 'B_a', 'b_a', 'A_g', 'B_g', 'k_k', 'k_a', 'r_k', 'gn_w', 'gn_b')}
    del _L0_attn_all

    def _L0_ffn_setup():
        import jax, jax.numpy as jnp
        import numpy as np
        DIM = 64
        HEADS = 8
        NUM_KEYS = 64
        NUM_KV = NUM_KEYS ** 2
        PK_TOPK = 16
        FINAL_TOPK = 16
        DIM_KEY = DIM // 2
        P = 2

        def _pk(x, Wq_pk, pk_keys):
            b, n, _ = x.shape
            q = (x @ Wq_pk).reshape(b, n, P, HEADS, DIM_KEY).transpose(2, 0, 1, 3, 4)
            sim = jnp.einsum('pbnhd,pkhd->pbnhk', q, pk_keys)
            scores, idx = jax.lax.top_k(sim, PK_TOPK)
            idx0 = idx[0]
            idx1 = idx[1] * NUM_KEYS
            index = (idx0[..., :, None] + idx1[..., None, :]).reshape(b, n, HEADS, PK_TOPK * PK_TOPK)
            score = (scores[0][..., :, None] + scores[1][..., None, :]).reshape(b, n, HEADS, PK_TOPK * PK_TOPK)
            final_scores, pk_idx = jax.lax.top_k(score, FINAL_TOPK)
            final_indices = jnp.take_along_axis(index, pk_idx, axis=-1)
            final_scores = jax.nn.softmax(final_scores, axis=-1)
            return (final_scores, final_indices)
        key = jax.random.key(seed)
        ks = jax.random.split(key, 7)
        b, n = (2, 256)
        std = 0.02
        x = jax.random.normal(ks[0], (b, n, DIM), dtype=jnp.float32)
        Wq_pk = jax.random.normal(ks[1], (DIM, P * HEADS * DIM_KEY), dtype=jnp.float32) * std
        pk_keys = jax.random.normal(ks[2], (P, NUM_KEYS, HEADS, DIM_KEY), dtype=jnp.float32) * std
        Wq = jax.random.normal(ks[3], (DIM, HEADS * DIM), dtype=jnp.float32) * std
        keys_table = jax.random.normal(ks[4], (NUM_KV * HEADS, DIM), dtype=jnp.float32) * std
        values_table = jax.random.normal(ks[5], (NUM_KV * HEADS, DIM), dtype=jnp.float32) * std
        Wo = jax.random.normal(ks[6], (DIM * HEADS, DIM), dtype=jnp.float32) * std
        return {'x': x, 'Wq_pk': Wq_pk, 'pk_keys': pk_keys, 'Wq': Wq, 'keys_table': keys_table, 'values_table': values_table, 'Wo': Wo}
    _L0_ffn_all = _L0_ffn_setup()
    _L0_ffn_in = {k: v for k, v in _L0_ffn_all.items() if k in ('Wq_pk', 'pk_keys', 'Wq', 'keys_table', 'values_table', 'Wo')}
    del _L0_ffn_all
    return {'x': x, 'L0_tok_conv0_w': _L0_tok_in['conv0_w'], 'L0_tok_conv0_b': _L0_tok_in['conv0_b'], 'L0_tok_conv1_w': _L0_tok_in['conv1_w'], 'L0_tok_conv1_b': _L0_tok_in['conv1_b'], 'L0_tok_conv2_w': _L0_tok_in['conv2_w'], 'L0_tok_conv2_b': _L0_tok_in['conv2_b'], 'L0_tok_conv3_w': _L0_tok_in['conv3_w'], 'L0_tok_conv3_b': _L0_tok_in['conv3_b'], 'L0_tok_n0_w': _L0_tok_in['n0_w'], 'L0_tok_n0_b': _L0_tok_in['n0_b'], 'L0_tok_n1_w': _L0_tok_in['n1_w'], 'L0_tok_n1_b': _L0_tok_in['n1_b'], 'L0_tok_n2_w': _L0_tok_in['n2_w'], 'L0_tok_n2_b': _L0_tok_in['n2_b'], 'L0_tok_n3_w': _L0_tok_in['n3_w'], 'L0_tok_n3_b': _L0_tok_in['n3_b'], 'L0_tok_n4_w': _L0_tok_in['n4_w'], 'L0_tok_n4_b': _L0_tok_in['n4_b'], 'L0_tok_mlp_w1': _L0_tok_in['mlp_w1'], 'L0_tok_mlp_b1': _L0_tok_in['mlp_b1'], 'L0_tok_mlp_w2': _L0_tok_in['mlp_w2'], 'L0_tok_mlp_b2': _L0_tok_in['mlp_b2'], 'L0_tok_mlp_w3': _L0_tok_in['mlp_w3'], 'L0_tok_mlp_b3': _L0_tok_in['mlp_b3'], 'L0_attn_x_mix': _L0_attn_in['x_mix'], 'L0_attn_W_r': _L0_attn_in['W_r'], 'L0_attn_W_k': _L0_attn_in['W_k'], 'L0_attn_W_v': _L0_attn_in['W_v'], 'L0_attn_W_o': _L0_attn_in['W_o'], 'L0_attn_A_w': _L0_attn_in['A_w'], 'L0_attn_B_w': _L0_attn_in['B_w'], 'L0_attn_b_w': _L0_attn_in['b_w'], 'L0_attn_A_a': _L0_attn_in['A_a'], 'L0_attn_B_a': _L0_attn_in['B_a'], 'L0_attn_b_a': _L0_attn_in['b_a'], 'L0_attn_A_g': _L0_attn_in['A_g'], 'L0_attn_B_g': _L0_attn_in['B_g'], 'L0_attn_k_k': _L0_attn_in['k_k'], 'L0_attn_k_a': _L0_attn_in['k_a'], 'L0_attn_r_k': _L0_attn_in['r_k'], 'L0_attn_gn_w': _L0_attn_in['gn_w'], 'L0_attn_gn_b': _L0_attn_in['gn_b'], 'L0_ffn_Wq_pk': _L0_ffn_in['Wq_pk'], 'L0_ffn_pk_keys': _L0_ffn_in['pk_keys'], 'L0_ffn_Wq': _L0_ffn_in['Wq'], 'L0_ffn_keys_table': _L0_ffn_in['keys_table'], 'L0_ffn_values_table': _L0_ffn_in['values_table'], 'L0_ffn_Wo': _L0_ffn_in['Wo']}

def reference(x, L0_tok_conv0_w, L0_tok_conv0_b, L0_tok_conv1_w, L0_tok_conv1_b, L0_tok_conv2_w, L0_tok_conv2_b, L0_tok_conv3_w, L0_tok_conv3_b, L0_tok_n0_w, L0_tok_n0_b, L0_tok_n1_w, L0_tok_n1_b, L0_tok_n2_w, L0_tok_n2_b, L0_tok_n3_w, L0_tok_n3_b, L0_tok_n4_w, L0_tok_n4_b, L0_tok_mlp_w1, L0_tok_mlp_b1, L0_tok_mlp_w2, L0_tok_mlp_b2, L0_tok_mlp_w3, L0_tok_mlp_b3, L0_attn_x_mix, L0_attn_W_r, L0_attn_W_k, L0_attn_W_v, L0_attn_W_o, L0_attn_A_w, L0_attn_B_w, L0_attn_b_w, L0_attn_A_a, L0_attn_B_a, L0_attn_b_a, L0_attn_A_g, L0_attn_B_g, L0_attn_k_k, L0_attn_k_a, L0_attn_r_k, L0_attn_gn_w, L0_attn_gn_b, L0_ffn_Wq_pk, L0_ffn_pk_keys, L0_ffn_Wq, L0_ffn_keys_table, L0_ffn_values_table, L0_ffn_Wo):
    import jax
    import jax.numpy as jnp

    def _L0_tok_ref(x, conv0_w, conv0_b, conv1_w, conv1_b, conv2_w, conv2_b, conv3_w, conv3_b, n0_w, n0_b, n1_w, n1_b, n2_w, n2_b, n3_w, n3_b, n4_w, n4_b, mlp_w1, mlp_b1, mlp_w2, mlp_b2, mlp_w3, mlp_b3):
        import jax, jax.numpy as jnp
        import numpy as np
        B, L = (4, 10240)
        C = 128
        DMLP = 512
        TEMP = 1e-05
        EPS = 1e-05
        FACTOR = 2

        def _conv(x, w, b, stride, pad):
            x = jnp.pad(x, ((0, 0), (0, 0), (pad, pad)), mode='reflect')
            y = jax.lax.conv_general_dilated(x, w, (stride,), 'VALID', dimension_numbers=('NCH', 'OIH', 'NCH'))
            return y + b[None, :, None]

        def _cnorm(x, g, b):
            m = jnp.mean(x, axis=1, keepdims=True)
            v = jnp.var(x, axis=1, keepdims=True, ddof=1)
            return (x - m) * jax.lax.rsqrt(v + EPS) * g[None, :, None] + b[None, :, None]

        def _forward(x, conv0_w, conv0_b, conv1_w, conv1_b, conv2_w, conv2_b, conv3_w, conv3_b, n0_w, n0_b, n1_w, n1_b, n2_w, n2_b, n3_w, n3_b, n4_w, n4_b, mlp_w1, mlp_b1, mlp_w2, mlp_b2, mlp_w3, mlp_b3):
            h = jax.nn.relu(_cnorm(_conv(x, conv0_w, conv0_b, 5, 3), n0_w, n0_b))
            h = jax.nn.relu(_cnorm(_conv(h, conv1_w, conv1_b, 4, 2), n1_w, n1_b))
            h = jax.nn.relu(_cnorm(_conv(h, conv2_w, conv2_b, 2, 1), n2_w, n2_b))
            h = jax.nn.relu(_cnorm(_conv(h, conv3_w, conv3_b, 2, 1), n3_w, n3_b))
            f = jnp.transpose(h, (0, 2, 1))
            T = f.shape[1]
            z = jax.nn.gelu(f @ mlp_w1 + mlp_b1, approximate=False)
            z = jax.nn.gelu(z @ mlp_w2 + mlp_b2, approximate=False)
            imp = jax.nn.sigmoid((z @ mlp_w3 + mlp_b3)[..., 0]) + TEMP
            imp = imp / jnp.sum(imp, axis=1, keepdims=True) * (T / FACTOR)
            Tn = T // FACTOR
            cs = jnp.cumsum(imp, axis=1)
            p = jnp.maximum(cs[:, :, None] - jnp.arange(Tn, dtype=cs.dtype)[None, None, :], 0.0)
            pc = jnp.pad(p, ((0, 0), (0, 0), (0, 1)))
            d = pc[:, :, :-1] - pc[:, :, 1:]
            wmat = d - jnp.pad(d, ((0, 0), (1, 0), (0, 0)))[:, :-1, :]
            pooled = jnp.einsum('btn,btc->bnc', wmat, f)
            out = jnp.transpose(pooled, (0, 2, 1))
            return jax.nn.relu(_cnorm(out, n4_w, n4_b))
        return _forward(x, conv0_w, conv0_b, conv1_w, conv1_b, conv2_w, conv2_b, conv3_w, conv3_b, n0_w, n0_b, n1_w, n1_b, n2_w, n2_b, n3_w, n3_b, n4_w, n4_b, mlp_w1, mlp_b1, mlp_w2, mlp_b2, mlp_w3, mlp_b3)

    def _L0_attn_ref(x, x_mix, W_r, W_k, W_v, W_o, A_w, B_w, b_w, A_a, B_a, b_a, A_g, B_g, k_k, k_a, r_k, gn_w, gn_b):
        import jax, jax.numpy as jnp
        import numpy as np
        B, T, D = (4, 512, 64)
        W_LORA, A_LORA, G_LORA = (64, 64, 128)
        DECAY_SCALE = -0.6065306597126334
        EPS = D * 1e-05

        def _forward(x, x_mix, W_r, W_k, W_v, W_o, A_w, B_w, b_w, A_a, B_a, b_a, A_g, B_g, k_k, k_a, r_k, gn_w, gn_b):
            b, t, d = x.shape
            shifted = jnp.pad(x, ((0, 0), (1, 0), (0, 0)))[:, :-1]
            delta = shifted - x
            xr, xw, xk, xv, xa, xg = [x + delta * x_mix[i] for i in range(6)]
            r = xr @ W_r
            w = DECAY_SCALE * jax.nn.sigmoid(jnp.tanh(xw @ A_w) @ B_w + b_w)
            k = xk @ W_k
            v = xv @ W_v
            a = jax.nn.sigmoid(xa @ A_a @ B_a + b_a)
            g = jax.nn.sigmoid(xg @ A_g) @ B_g
            kk = k * k_k
            kk = kk / jnp.maximum(jnp.linalg.norm(kk, axis=-1, keepdims=True), 1e-12)
            k = k * (1.0 + (a - 1.0) * k_a)
            decay = jnp.exp(w)

            def step(S, inp):
                r_t, dec_t, k_t, v_t, kk_t, a_t = inp
                b_t = kk_t * a_t
                sa = jnp.einsum('bvk,bk->bv', S, -kk_t)
                S = S * dec_t[:, None, :] + sa[:, :, None] * b_t[:, None, :] + v_t[:, :, None] * k_t[:, None, :]
                o_t = jnp.einsum('bvk,bk->bv', S, r_t)
                return (S, o_t)
            tm = lambda z: jnp.swapaxes(z, 0, 1)
            S0 = jnp.zeros((b, d, d), x.dtype)
            _, o = jax.lax.scan(step, S0, (tm(r), tm(decay), tm(k), tm(v), tm(kk), tm(a)))
            o = jnp.swapaxes(o, 0, 1)
            mu = jnp.mean(o, axis=-1, keepdims=True)
            var = jnp.var(o, axis=-1, keepdims=True)
            o = (o - mu) * jax.lax.rsqrt(var + EPS) * gn_w + gn_b
            o = o + jnp.sum(r * k * r_k, axis=-1, keepdims=True) * v
            return o * g @ W_o
        return _forward(x, x_mix, W_r, W_k, W_v, W_o, A_w, B_w, b_w, A_a, B_a, b_a, A_g, B_g, k_k, k_a, r_k, gn_w, gn_b)

    def _L0_ffn_ref(x, Wq_pk, pk_keys, Wq, keys_table, values_table, Wo):
        import jax, jax.numpy as jnp
        import numpy as np
        DIM = 64
        HEADS = 8
        NUM_KEYS = 64
        NUM_KV = NUM_KEYS ** 2
        PK_TOPK = 16
        FINAL_TOPK = 16
        DIM_KEY = DIM // 2
        P = 2

        def _pk(x, Wq_pk, pk_keys):
            b, n, _ = x.shape
            q = (x @ Wq_pk).reshape(b, n, P, HEADS, DIM_KEY).transpose(2, 0, 1, 3, 4)
            sim = jnp.einsum('pbnhd,pkhd->pbnhk', q, pk_keys)
            scores, idx = jax.lax.top_k(sim, PK_TOPK)
            idx0 = idx[0]
            idx1 = idx[1] * NUM_KEYS
            index = (idx0[..., :, None] + idx1[..., None, :]).reshape(b, n, HEADS, PK_TOPK * PK_TOPK)
            score = (scores[0][..., :, None] + scores[1][..., None, :]).reshape(b, n, HEADS, PK_TOPK * PK_TOPK)
            final_scores, pk_idx = jax.lax.top_k(score, FINAL_TOPK)
            final_indices = jnp.take_along_axis(index, pk_idx, axis=-1)
            final_scores = jax.nn.softmax(final_scores, axis=-1)
            return (final_scores, final_indices)
        b, n, d = x.shape
        q = (x @ Wq).reshape(b, n, HEADS, DIM) * DIM ** (-0.5)
        kv_scores, indices = _pk(x, Wq_pk, pk_keys)
        offsets = jnp.arange(HEADS, dtype=indices.dtype) * NUM_KV
        ind = indices + offsets[None, None, :, None]
        k = jnp.einsum('bnhk,bnhkd->bnhd', kv_scores, keys_table[ind])
        v = jnp.einsum('bnhk,bnhkd->bnhd', kv_scores, values_table[ind])
        sim = jnp.einsum('bihd,bjhd->bhij', q, k)
        neg = -jnp.finfo(sim.dtype).max
        causal = jnp.tril(jnp.ones((n, n), dtype=bool))
        sim = jnp.where(causal, sim, neg)
        attn = jax.nn.softmax(sim, axis=-1)
        out = jnp.einsum('bhij,bjhd->bhid', attn, v)
        out = out.transpose(0, 2, 1, 3).reshape(b, n, HEADS * DIM)
        return out @ Wo
    h = _L0_tok_ref(x, L0_tok_conv0_w, L0_tok_conv0_b, L0_tok_conv1_w, L0_tok_conv1_b, L0_tok_conv2_w, L0_tok_conv2_b, L0_tok_conv3_w, L0_tok_conv3_b, L0_tok_n0_w, L0_tok_n0_b, L0_tok_n1_w, L0_tok_n1_b, L0_tok_n2_w, L0_tok_n2_b, L0_tok_n3_w, L0_tok_n3_b, L0_tok_n4_w, L0_tok_n4_b, L0_tok_mlp_w1, L0_tok_mlp_b1, L0_tok_mlp_w2, L0_tok_mlp_b2, L0_tok_mlp_w3, L0_tok_mlp_b3)
    h = h + _L0_attn_ref(_layernorm(h, axis=-1), L0_attn_x_mix, L0_attn_W_r, L0_attn_W_k, L0_attn_W_v, L0_attn_W_o, L0_attn_A_w, L0_attn_B_w, L0_attn_b_w, L0_attn_A_a, L0_attn_B_a, L0_attn_b_a, L0_attn_A_g, L0_attn_B_g, L0_attn_k_k, L0_attn_k_a, L0_attn_r_k, L0_attn_gn_w, L0_attn_gn_b)
    h = h + _L0_ffn_ref(_layernorm(h, axis=-1), L0_ffn_Wq_pk, L0_ffn_pk_keys, L0_ffn_Wq, L0_ffn_keys_table, L0_ffn_values_table, L0_ffn_Wo)
    return h

_drawn_inputs = setup_inputs


def setup_inputs(seed=0):
    import zlib

    import numpy as np

    out = dict(_drawn_inputs(seed))
    spreads = {'L0_tok_conv0_b': (0.0, 0.1),
     'L0_tok_conv1_b': (0.0, 0.1),
     'L0_tok_conv2_b': (0.0, 0.1),
     'L0_tok_conv3_b': (0.0, 0.1),
     'L0_tok_n0_w': (1.0, 0.2),
     'L0_tok_n0_b': (0.0, 0.1),
     'L0_tok_n1_w': (1.0, 0.2),
     'L0_tok_n1_b': (0.0, 0.1),
     'L0_tok_n2_w': (1.0, 0.2),
     'L0_tok_n2_b': (0.0, 0.1),
     'L0_tok_n3_w': (1.0, 0.2),
     'L0_tok_n3_b': (0.0, 0.1),
     'L0_tok_n4_w': (1.0, 0.2),
     'L0_tok_n4_b': (0.0, 0.1),
     'L0_tok_mlp_b1': (0.0, 0.1),
     'L0_tok_mlp_b2': (0.0, 0.1),
     'L0_attn_gn_w': (1.0, 0.2),
     'L0_attn_gn_b': (0.0, 0.1)}
    factors = {'L0_ffn_Wq_pk': 8.0,
     'L0_ffn_pk_keys': 8.0,
     'L0_ffn_Wq': 64.0,
     'L0_ffn_keys_table': 64.0,
     'L0_ffn_values_table': 8.0,
     'L0_ffn_Wo': 8.0}
    for name, (base, spread) in spreads.items():
        noise = np.random.default_rng([zlib.crc32(name.encode()), seed]).standard_normal(out[name].shape)
        drawn = base * np.exp(spread * noise) if base else spread * noise
        out[name] = jnp.asarray(drawn.astype(out[name].dtype))
    for name, factor in factors.items():
        out[name] = (out[name] * factor).astype(out[name].dtype)
    return out
```

```python
import concourse.bass as bass
from concourse import mybir
from contextlib import ExitStack

F32 = mybir.dt.float32
U32 = mybir.dt.uint32
ALU = mybir.AluOpType
ACT = mybir.ActivationFunctionType
AX = mybir.AxisListType

BATCH = 32
WAVE = 10240
C = 128
P = 128
D = 64
T0, T1, T2, T3 = 2048, 512, 256, 128
K0, S0, PAD0 = 10, 5, 3
FR = T0 // P
WIN = S0 * (FR - 1) + K0
MLP = 512
MC = MLP // P
HEADS = 8
NKEY = 64
TOPK = 16
LORA = 64
DECAY = -0.6065306597126334
RECTS = [(0, 1, 16), (1, 2, 8), (2, 4, 5), (4, 8, 3), (8, 16, 1)]
NCAND = sum((b - a) * n for a, b, n in RECTS)
LEVELS = 6
NGB = 4
EPS = 1e-5
GN_EPS = D * 1e-5
LOWEST = -3.0e38
FUTURE = 1.0e30

CONST = {}
_at = 0
for _name, _n in (("ident", P), ("mean_sq", P), ("ones", P), ("center", P), ("upto", P), ("before", P),
                  ("shift_diff", P), ("neg_iota", D), ("cand_iota", NCAND), ("head_base", HEADS * TOPK),
                  ("tri", 4 * P), ("pair", P), ("pair_t", P), ("merge_t", LEVELS * P), ("future", P)):
    CONST[_name] = (_at, _n)
    _at += _n
NCONST = _at

STACK = {"r": (0, 64, 0), "k": (64, 64, 2), "w": (128, 64, 1), "a": (192, 64, 4), "v": (256, 64, 3), "g": (320, 128, 5)}
NSTACK = 448


def constants():
    import numpy as np
    s, t = np.arange(P)[:, None], np.arange(P)[None, :]
    out = np.zeros((P, NCONST), np.float32)

    def put(name, a):
        at, n = CONST[name]
        out[:, at:at + n] = np.reshape(a, (a.shape[0], n)) if a.ndim > 1 else a

    put("ident", (s == t) * 1.0)
    put("mean_sq", np.full((P, P), 1.0 / (C - 1)))
    put("ones", np.ones((P, P)))
    put("center", (s == t) - 1.0 / C)
    put("upto", (s <= t) * 1.0)
    put("before", (s < t) * 1.0)
    put("shift_diff", (s == t - 1) * 1.0 - (s == t))
    put("neg_iota", -np.arange(D) * 1.0)
    put("cand_iota", np.arange(NCAND) * 1.0)
    put("head_base", np.repeat(np.arange(HEADS) * NKEY * NKEY, TOPK) * 1.0)
    put("tri", np.concatenate([-1.0 * (s < t), 1.0 * (s <= t), -1.0 * (s < t), 1.0 * (s <= t)], 1))
    put("pair", -1.0 * ((s % 2 == 1) & (t == s - 1)))
    put("pair_t", 1.0 * ((t % 2 == 1) & (s == t - 1)))
    merges = []
    for lv in range(1, LEVELS + 1):
        half = 2 ** lv
        merges.append(1.0 * ((s // (2 * half) == t // (2 * half)) & (t % (2 * half) >= half) & (s % (2 * half) < half)))
    put("merge_t", np.concatenate(merges, 1))
    put("future", FUTURE * (t > s))
    return out


def tower(nc, x, consts, w0, w1, w2, w3, cvec, mw1, mw2, mw3, mb12, mb3, stack, mix, bw, ba, bg, vec64,
          wo_attn, gn, wqpk, keys, wq, table, wo_ffn, out):
    ctx = ExitStack()
    with ctx:
        def sb(name, shape, dt=F32):
            return ctx.enter_context(nc.sbuf_tensor(name, shape, dt))

        def sem(name):
            return ctx.enter_context(nc.semaphore(name))

        cst = sb("cst", [P, NCONST])

        def const(name, a=0, b=None, rows=P):
            at, n = CONST[name]
            return cst[0:rows, at + a:at + (n if b is None else b)]

        conv0_w = sb("conv0_w", [WIN, FR, C])
        conv_w = {1: sb("conv1_w", [C, 8, C]), 2: sb("conv2_w", [C, 4, C]), 3: sb("conv3_w", [C, 4, C])}
        wmean = sb("wmean", [P, FR])
        chan = sb("chan", [C, 14])
        cbias = sb("cbias", [C, 4])
        mlp1 = sb("mlp1", [C, MLP])
        mlp2 = sb("mlp2", [P, MC, MLP])
        mlp3 = sb("mlp3", [P, MC])
        mlpb = sb("mlpb", [P, 2 * MC + 1])
        half_b3 = sb("half_b3", [P, 1])
        proj = sb("proj", [P, NSTACK])
        mixc = sb("mixc", [P, 6])
        lora_w = sb("lora_w", [LORA, D])
        lora_a = sb("lora_a", [LORA, D])
        lora_g = sb("lora_g", [P, D])
        v64 = sb("v64", [D, 5])
        v64h = sb("v64h", [D, 3])
        attn_wo = sb("attn_wo", [D, D])
        gnb = sb("gnb", [P, 2, D])
        qpk = sb("qpk", [32, 2, HEADS, D])
        pkk = sb("pkk", [32, 2, HEADS, NKEY])
        route_w = sb("route_w", [D, HEADS, 2, NKEY])
        ffn_wq = sb("ffn_wq", [D, HEADS * D])
        ffn_wo = sb("ffn_wo", [P, HEADS, D])
        eps = sb("eps", [P, 2])

        window = sb("window", [P, WIN])
        window_t = sb("window_t", [WIN, P])
        square = sb("square", [P, 2, 512])
        logv = sb("logv", [P, 512])
        rstd = sb("rstd", [P, 2, 512])
        normed = sb("normed", [P, 2, 512])
        h0 = sb("h0", [C, 4, T1 + 1])
        h1 = sb("h1", [C, T1 + 2])
        h2 = sb("h2", [C, T2 + 2])
        h3 = sb("h3", [C, T3])
        z1 = sb("z1", [P, MC, T3])
        z2 = sb("z2", [P, MC, T3])
        imp = sb("imp", [P, 2])
        total = sb("total", [P, 1])
        cums = sb("cums", [P, 2])
        ramp = sb("ramp", [P, 2, D + 1])
        dramp = sb("dramp", [P, D + 1])
        wmat = sb("wmat", [P, D])
        feat = sb("feat", [P, C])
        tok = sb("tok", [C, D])

        res = sb("res", [P, D])
        stats = sb("stats", [P, 6])
        mv = sb("mv", [P, 2])
        mlog = sb("mlog", [P, 1])
        mrstd = sb("mrstd", [P, 1])
        ln = sb("ln", [P, D])
        xd = sb("xd", [P, P])
        rk = sb("rk", [D, 2, P])
        val = sb("val", [P, D])
        tanh_w = sb("tanh_w", [LORA, P])
        lin_a = sb("lin_a", [LORA, P])
        sig_g = sb("sig_g", [P, P])
        sig_wa = sb("sig_wa", [D, 2, P])
        gate = sb("gate", [P, D])
        cdec = sb("cdec", [D, P + 1])
        mid = sb("mid", [D, 2])
        dec_up = sb("dec_up", [D, P + 1])
        dec_dn = sb("dec_dn", [D, P])
        kkr = sb("kkr", [D, P])
        kks = sb("kks", [D, P])
        kkn = sb("kkn", [D, P])
        kk = sb("kk", [D, P])
        kb = sb("kb", [D, P])
        kfac = sb("kfac", [D, P])
        k2 = sb("k2", [D, P])
        rk2 = sb("rk2", [D, P])
        left = sb("left", [D, 2, P])
        right = sb("right", [D, 2, P])
        tri = sb("tri", [P, 4, P])
        offs = sb("offs", [P, LEVELS, P])
        inv = sb("inv", [P, 2, P])
        prod = sb("prod", [P, P])
        rhs0 = sb("rhs0", [P, D])
        sol1 = sb("sol1", [P, D])
        offsol = sb("offsol", [P, D])
        sa = sb("sa", [P, D])
        bonus = sb("bonus", [P, 1])
        og = sb("og", [P, 2, D])
        og_t = sb("og_t", [D, P])
        x2 = sb("x2", [D, P])

        sims = sb("sims", [P, HEADS, 2, NKEY])
        top = sb("top", [P, 2, HEADS, 2, TOPK])
        topi = sb("topi", [P, HEADS, 2, TOPK], U32)
        cand = sb("cand", [P, 2, HEADS, NCAND])
        fin = sb("fin", [P, HEADS, TOPK])
        finp = sb("finp", [P, HEADS, TOPK], U32)
        pick = sb("pick", [P, HEADS, TOPK, NCAND])
        rowf = sb("rowf", [P, HEADS * TOPK])
        fexp = sb("fexp", [P, HEADS, TOPK])
        fsum = sb("fsum", [P, HEADS])
        w_next = sb("w_next", [P, HEADS, TOPK])
        i_next = sb("i_next", [P, HEADS * TOPK], U32)

        rows = sb("rows", [P, HEADS * TOPK], U32)
        weight = sb("weight", [P, HEADS, TOPK])
        res_h = sb("res_h", [P, D])
        x2_h = sb("x2_h", [D, P])
        got = sb("got", [P, NGB, TOPK, P])
        diag = sb("diag", [P, 2, TOPK, P])
        qt = sb("qt", [D, P])
        kvt = sb("kvt", [P, P])
        vw = sb("vw", [P, D])
        neg = sb("neg", [P, P])
        nmax = sb("nmax", [P, 1])
        ex = sb("ex", [P, P])
        esum = sb("esum", [P, 1])
        erec = sb("erec", [P, 1])
        prob = sb("prob", [P, P])
        prob_t = sb("prob_t", [P, P])
        res_o = sb("res_o", [P, D])

        bank = [ctx.enter_context(nc.psum_tensor(f"bank{i}", [P, 512], F32)) for i in range(8)]
        conv_bank, var_bank = (bank[0], bank[1]), bank[2]
        mx, my = bank[3], bank[4]
        kv_bank, sc_bank, y_bank = bank[5], bank[6], bank[7]

        s_loaded = sem("s_loaded")
        s_cleared = sem("s_cleared")
        s_centred = sem("s_centred")
        s_setup_pe = sem("s_setup_pe")
        s_setup_done = sem("s_setup_done")
        s_wave = sem("s_wave")
        s_window_ps = sem("s_window_ps")
        s_window_t = sem("s_window_t")
        s_conv0 = sem("s_conv0")
        s_sq0 = sem("s_sq0")
        s_var0 = sem("s_var0")
        s_log0 = sem("s_log0")
        s_rstd0 = sem("s_rstd0")
        s_norm0 = sem("s_norm0")
        s_h0 = sem("s_h0")
        s_pad = sem("s_pad")
        s_conv = sem("s_conv")
        s_sq = sem("s_sq")
        s_var = sem("s_var")
        s_log = sem("s_log")
        s_rstd = sem("s_rstd")
        s_norm = sem("s_norm")
        s_h = sem("s_h")
        s_z1p, s_z1, s_z2p, s_z2 = sem("s_z1p"), sem("s_z1"), sem("s_z2p"), sem("s_z2")
        s_z3p, s_imp_t, s_imp = sem("s_z3p"), sem("s_imp_t"), sem("s_imp")
        s_cums = sem("s_cums")
        s_ramp = sem("s_ramp")
        s_feat_ps, s_feat = sem("s_feat_ps"), sem("s_feat")
        s_mdve = sem("s_mdve")
        s_mact = sem("s_mact")
        s_mpe = sem("s_mpe")
        s_route = sem("s_route")
        s_simcp = sem("s_simcp")
        s_fexp = sem("s_fexp")
        s_rows = sem("s_rows")
        s_handed = sem("s_handed")
        s_got = [sem(f"s_got{i}") for i in range(NGB)]
        s_diag = sem("s_diag")
        s_q_ps = sem("s_q_ps")
        s_q = sem("s_q")
        s_kv_ps = sem("s_kv_ps")
        s_kv = sem("s_kv")
        s_score = sem("s_score")
        s_vw = sem("s_vw")
        s_neg = sem("s_neg")
        s_exp = sem("s_exp")
        s_erec = sem("s_erec")
        s_prob = sem("s_prob")
        s_prob_ps = sem("s_prob_ps")
        s_prob_t = sem("s_prob_t")
        s_y = sem("s_y")
        s_waited = sem("s_waited")
        s_out = sem("s_out")
        s_stored = sem("s_stored")

        block = ctx.enter_context(nc.Block())

        def wait_apart(eng, sem, value):
            eng.wait_ge(sem, value)
            if not isinstance(value, int):
                eng.sem_inc(s_waited, 1)

        def level_bank(n):
            return conv_bank[(0, 1, 0, 0)[n]]

        LEN = (T1, T2, T3, D)
        V = {}
        for n, k in enumerate(("stats", "mean", "ln", "rk", "val", "sig_g", "sig_wa", "cdec", "mid", "kkr", "kks",
                               "nrm", "rnrm", "kk", "kb", "kfac", "k2", "left_k", "left_r", "right_b", "right_k", "rk2", "tri",
                               "inv0", "inv0b", "invt0", "invt0b", "offs", "bonus",
                               "p0", "t0", "p1", "t1", "p2", "t2", "p3", "t3", "p4", "t4",
                               "rhs0", "sol1", "offsol", "sa", "ostats", "omean", "on", "ow", "ob", "obonus", "og",
                               "res", "stats2", "mean2", "ln2"), 1):
            V[k] = n
        A = {}
        for n, k in enumerate(("log", "rstd", "xd", "tanh_w", "lin_a", "tanh_g", "tanh_sw", "tanh_sa", "gate",
                               "dec_up", "dec_dn", "nrm", "olog", "orstd", "og_t", "log2", "rstd2", "x2"), 1):
            A[k] = n
        E = {}
        for n, k in enumerate(("xd", "proj", "lora", "ss", "tri", "p0", "t0", "p1", "t1", "p2", "t2", "p3", "t3", "p4", "t4",
                               "rhs0", "sol1", "offsol", "sol2", "o", "og_t", "wo", "x2", "sims"), 1):
            E[k] = n
        NV, NA, NE = len(V), len(A), len(E)
        R = {k: n for n, k in enumerate((
            "top8_0", "rep_0", "top16_0", "idx_0", "top8_1", "rep_1", "top16_1", "idx_1", "keys", "cands",
            "fin8", "rep_f", "fin16", "fidx", "shift", "pick", "rowsel", "rowf", "i_next", "fsum", "frec", "w_next"), 1)}
        NROUTE = len(R)
        SLOTS = [((), (0,), ()), ((), (1,), ()), ((), (2,), ()), ((), (3, 4), ()),
                 ((0,), (), (0,)), ((1,), (), (1,)), ((2, 3), (), (2,)), ((4, 5), (), (3,))]

        def pipeline(eng, tokenizer, mixer, route, head, head_out, hand_rows, hand_rest):
            def step(tb, mb, hb):
                for slot, (tparts, mparts, rparts) in enumerate(SLOTS):
                    if mb is not None:
                        for part in mparts:
                            mixer(mb, part)
                        for part in rparts:
                            route(mb, part)
                    if tb is not None:
                        for part in tparts:
                            tokenizer(tb, part)
                    if hb is not None:
                        if slot:
                            head_out(hb, slot - 1)
                        head(hb, slot)
                if mb is not None:
                    hand_rows(mb)
                if hb is not None:
                    head_out(hb, HEADS - 1)
                if mb is not None:
                    hand_rest(mb)

            step(0, None, None)
            step(1, 0, None)
            step(2, 1, 0)
            with eng.Fori(1, BATCH - 2) as b:
                step(b + 2, b + 1, b)
            step(None, BATCH - 1, BATCH - 2)
            step(None, None, BATCH - 1)

        def nothing(b, part=None):
            pass

        LOADS = [(cst[:, :], consts), (chan[:, :], cvec), (mlp1[:, :], mw1),
                 (mlp2[:, :, :], mw2.rearrange("(k p) n -> p k n", p=P)),
                 (mlp3[:, :], mw3), (mlpb[:, 0:2 * MC], mb12), (mlpb[:, 2 * MC:], mb3.broadcast_to([P, 1])),
                 (proj[0:D, :], stack), (proj[D:P, :], stack),
                 (lora_w[:, :], bw), (lora_a[:, :], ba), (lora_g[:, :], bg), (v64[:, :], vec64),
                 (attn_wo[:, :], wo_attn), (gnb[:, :, :], gn.rearrange("(o a) d -> o a d", o=1).broadcast_to([P, 2, D])),
                 (qpk[:, :, :, :], wqpk), (pkk[:, :, :, :], keys), (ffn_wq[:, :], wq),
                 (ffn_wo[D:P, :, :], wo_ffn.rearrange("(h d) n -> d h n", d=D)),
                 (conv_w[1][:, :, :], w1), (conv_w[2][:, :, :], w2), (conv_w[3][:, :, :], w3)]
        NLOADS = len(LOADS) + FR + 1

        @block.sync
        def _(sp):
            for dst, src in LOADS:
                sp.dma_start(dst, src).then_inc(s_loaded, 16)
            sp.wait_ge(s_cleared, 2)
            for j in range(FR):
                sp.dma_start(conv0_w[S0 * j:S0 * j + K0, j, :], w0).then_inc(s_loaded, 16)
            sp.dma_start(mixc[D:P, :], mix).then_inc(s_loaded, 16)

            def load_wave(b):
                n = S0 * FR
                sp.dma_start(window[:, 0:n], x[bass.ds(b, 1), 0:P * n].rearrange("o (p n) -> (o p) n", p=P)).then_inc(s_wave, 16)
                sp.dma_start(window[:, n:WIN], x[bass.ds(b, 1), n:(P + 1) * n].rearrange("o (p n) -> (o p) n", p=P)[:, 0:WIN - n]).then_inc(s_wave, 16)

            def store(b):
                sp.wait_ge(s_out, b + 1)
                sp.dma_start(out[bass.ds(b, 1), :, :].rearrange("o c d -> (o c) d"), res_o[:, :]).then_inc(s_stored, 16)

            load_wave(0)
            sp.wait_ge(s_window_ps, 1)
            load_wave(1)
            sp.wait_ge(s_window_ps, 2)
            load_wave(2)
            with sp.Fori(0, BATCH - 3) as b:
                sp.wait_ge(s_window_ps, b + 3)
                load_wave(b + 3)
                store(b)
            for b in range(BATCH - 3, BATCH):
                store(b)
            sp.wait_ge(s_stored, 16 * BATCH)

        @block.gpsimd
        def _(pool):
            nc.gpsimd.memset(conv0_w[:, :, :], 0.0).then_inc(s_cleared, 1)
            nc.gpsimd.memset(mixc[:, :], 1.0).then_inc(s_cleared, 1)

            def gathers(b):
                wait_apart(pool, s_rows, b + 1)
                for h in range(HEADS):
                    g = h % NGB
                    if h >= NGB or not isinstance(b, int):
                        wait_apart(pool, s_kv_ps, b * HEADS + h - NGB + 1)
                    for k in range(TOPK):
                        pool.indirect_dma_start(got[:, g, k, :], None, table,
                                                bass.IndirectOffsetOnAxis(ap=rows[:, h * TOPK + k:h * TOPK + k + 1], axis=0)
                                                ).then_inc(s_got[g], 16)

            gathers(0)
            with pool.Fori(1, BATCH) as b:
                gathers(b)

        @block.tensor
        def _(pe):
            mm, tr = nc.tensor.matmul, nc.tensor.transpose
            pe.wait_ge(s_loaded, 16 * NLOADS)
            mm(mx[:, 0:4], const("center"), chan[:, 0:4], start=True, stop=True).then_inc(s_setup_pe, 1)
            for n in range(2 * HEADS):
                h, p = n // 2, n % 2
                last = mm(conv_bank[n // 8][0:D, (n % 8) * NKEY:(n % 8 + 1) * NKEY], qpk[:, p, h, :], pkk[:, p, h, :], start=True, stop=True)
            last.then_inc(s_setup_pe, 1)
            pe.wait_ge(s_setup_done, 1)

            def variance0(b, r):
                pe.wait_ge(s_sq0, b * 4 + r + 1)
                if r >= 1:
                    pe.wait_ge(s_log0, b * 4 + r)
                mm(var_bank[:, :], const("mean_sq"), square[:, r % 2, :], start=True, stop=True).then_inc(s_var0, 1)

            def variance(b, n):
                pe.wait_ge(s_sq, b * 4 + n + 1)
                mm(var_bank[:, 0:LEN[n]], const("mean_sq"), square[:, n % 2, 0:LEN[n]], start=True, stop=True).then_inc(s_var, 1)

            def tokenizer(b, part):
                if part == 0:
                    pe.wait_ge(s_wave, 32 * (b + 1))
                    if not isinstance(b, int) or b > 0:
                        pe.wait_ge(s_log, b * 4)
                    tr(var_bank[0:WIN, 0:P], window[:, :], const("ident")).then_inc(s_window_ps, 1)
                    pe.wait_ge(s_window_t, b + 1)
                    for r in range(4):
                        if r >= 2:
                            pe.wait_ge(s_norm0, b * 4 + r - 1)
                        for q in range(4):
                            j = 4 * (q + (r < 2)) + r - 2
                            last = mm(conv_bank[r % 2][:, q:512:4], conv0_w[:, j, :], window_t[:, :], start=True, stop=True)
                        last.then_inc(s_conv0, 1)
                        if r >= 1:
                            variance0(b, r - 1)
                    variance0(b, 3)
                elif part <= 3:
                    n = part
                    pe.wait_ge(s_pad, b * 3 + n)
                    taps = 8 if n == 1 else 4
                    ps = level_bank(n - 1)[:, 0:LEN[n - 1]]
                    for k in range(taps):
                        if n == 1:
                            rhs = h0[:, k % 4, k // 4:k // 4 + T1]
                        else:
                            rhs = (h1 if n == 2 else h2)[:, k:k + 2 * LEN[n - 1] - 1:2]
                        last = mm(ps, conv_w[n][:, k, :], rhs, start=k == 0, stop=k == taps - 1)
                    last.then_inc(s_conv, 1)
                    variance(b, n - 1)
                elif part == 4:
                    pe.wait_ge(s_h, b * 4 + 3)
                    for m in range(MC):
                        last = mm(conv_bank[1][:, m * P:(m + 1) * P], mlp1[:, m * P:(m + 1) * P], h3[:, :], start=True, stop=True)
                    last.then_inc(s_z1p, 1)
                    pe.wait_ge(s_z1, b + 1)
                    for m in range(MC):
                        for k in range(MC):
                            last = mm(conv_bank[0][:, m * P:(m + 1) * P], mlp2[:, k, m * P:(m + 1) * P], z1[:, k, :], start=k == 0, stop=k == MC - 1)
                    last.then_inc(s_z2p, 1)
                    mm(conv_bank[1][:, 0:P], h3[:, :], const("center"), start=True, stop=True).then_inc(s_feat_ps, 1)
                    pe.wait_ge(s_z2, b + 1)
                    for k in range(MC):
                        last = mm(var_bank[:, 0:1], z2[:, k, :], mlp3[:, k:k + 1], start=k == 0, stop=k == MC - 1)
                    last.then_inc(s_z3p, 1)
                else:
                    pe.wait_ge(s_imp, b + 1)
                    mm(var_bank[:, 1:2], const("upto"), imp[:, 1:2], start=True, stop=True)
                    mm(var_bank[:, 2:3], const("before"), imp[:, 1:2], start=True, stop=True)
                    mm(var_bank[:, 3:4], const("ones"), imp[:, 1:2], start=True, stop=True).then_inc(s_cums, 1)
                    pe.wait_ge(s_feat, b + 1)
                    pe.wait_ge(s_ramp, b * 6 + 6)
                    mm(conv_bank[0][:, 0:D], feat[:, :], wmat[:, :], start=True, stop=True).then_inc(s_conv, 1)
                    variance(b, 3)

            def mixer(b, part):
                dve = lambda k: pe.wait_ge(s_mdve, b * NV + V[k])
                act = lambda k: pe.wait_ge(s_mact, b * NA + A[k])

                def levels(a, z):
                    for lv in range(a, z):
                        dve("bonus" if lv == 0 else f"t{lv - 1}")
                        mm(my[:, 256:384], offs[:, lv, :], inv[:, 0, :], start=True, stop=True).then_inc(s_mpe, 1)
                        dve(f"p{lv}")
                        mm(mx[:, 0:P], inv[:, 1, :], prod[:, :], start=True, stop=True)
                        mm(mx[:, P:2 * P], prod[:, :], inv[:, 1, :], start=True, stop=True).then_inc(s_mpe, 1)

                if part == 0:
                    dve("ln")
                    mm(mx[0:D, 0:P], ln[:, :], const("ident"), start=True, stop=True)
                    mm(mx[D:P, 0:P], ln[:, :], const("shift_diff"), start=True, stop=True).then_inc(s_mpe, 1)
                    act("xd")
                    for n, k in enumerate("rkwa"):
                        at, w, _ = STACK[k]
                        mm(my[0:D, n * P:(n + 1) * P], proj[:, at:at + w], xd[:, :], start=True, stop=True)
                    at, w, _ = STACK["g"]
                    mm(mx[:, P:2 * P], proj[:, at:at + w], xd[:, :], start=True, stop=True)
                    at, w, _ = STACK["v"]
                    mm(mx[:, 2 * P:2 * P + D], xd[:, :], proj[:, at:at + w], start=True, stop=True).then_inc(s_mpe, 1)
                    wait_apart(pe, s_mdve, b * NV + V["sig_g"])
                    mm(mx[0:D, 0:P], lora_w[:, :], tanh_w[:, :], start=True, stop=True)
                    mm(mx[0:D, 320:448], lora_a[:, :], lin_a[:, :], start=True, stop=True)
                    mm(mx[:, 448:512], sig_g[:, :], lora_g[:, :], start=True, stop=True).then_inc(s_mpe, 1)
                    wait_apart(pe, s_mdve, b * NV + V["kks"])
                    mm(my[0:D, 384:512], const("ones", 0, D, rows=D), kks[:, :], start=True, stop=True).then_inc(s_mpe, 1)
                elif part == 1:
                    dve("rk2")
                    act("gate")
                    mm(mx[:, 0:256], right[:, 0, :], left[:, :, :].rearrange("p a t -> p (a t)"), start=True, stop=True)
                    mm(mx[:, 256:512], right[:, 1, :], left[:, :, :].rearrange("p a t -> p (a t)"), start=True, stop=True)
                    mm(my[:, 0:P], left[:, 0, :], right[:, 0, :], start=True, stop=True)
                    mm(my[:, P:P + 1], rk2[:, :], v64[:, 4:5], start=True, stop=True).then_inc(s_mpe, 1)
                    levels(0, 2)
                elif part == 2:
                    levels(2, 4)
                elif part == 3:
                    levels(4, 5)
                    mm(my[:, 384:448], tri[:, 2, :], val[:, :], start=True, stop=True).then_inc(s_mpe, 1)
                    dve("rhs0")
                    mm(my[:, 448:512], inv[:, 1, :], rhs0[:, :], start=True, stop=True).then_inc(s_mpe, 1)
                    dve("sol1")
                    mm(mx[:, 256:320], offs[:, LEVELS - 1, :], sol1[:, :], start=True, stop=True).then_inc(s_mpe, 1)
                    dve("offsol")
                    mm(mx[:, 320:384], inv[:, 1, :], offsol[:, :], start=True, stop=True).then_inc(s_mpe, 1)
                    dve("sa")
                    mm(mx[:, 384:448], tri[:, 1, :], sa[:, :], start=True, stop=False)
                    mm(mx[:, 384:448], tri[:, 3, :], val[:, :], start=False, stop=True).then_inc(s_mpe, 1)
                else:
                    wait_apart(pe, s_mdve, b * NV + V["og"])
                    tr(my[0:D, 256:384], og[:, 1, :], const("ident")).then_inc(s_mpe, 1)
                    wait_apart(pe, s_mact, b * NA + A["og_t"])
                    mm(my[:, 384:448], og_t[:, :], attn_wo[:, :], start=True, stop=True).then_inc(s_mpe, 1)
                    wait_apart(pe, s_mdve, b * NV + V["ln2"])
                    tr(mx[0:D, 0:P], ln[:, :], const("ident")).then_inc(s_mpe, 1)
                    act("x2")
                    rw = route_w[:, :, :, :].rearrange("p h s k -> p (h s k)")
                    mm(my[:, :], x2[:, :], rw[:, 0:512], start=True, stop=True)
                    mm(mx[:, :], x2[:, :], rw[:, 512:1024], start=True, stop=True).then_inc(s_mpe, 1)

            def head(b, h):
                n = b * HEADS + h
                if h == 0:
                    wait_apart(pe, s_handed, b + 1)
                mm(sc_bank[0:D, 384:512], ffn_wq[:, h * D:(h + 1) * D], x2_h[:, :], start=True, stop=True).then_inc(s_q_ps, 1)
                pe.wait_ge(s_diag, n + 1)
                pe.wait_ge(s_got[h % NGB], (b * (HEADS // NGB) + h // NGB + 1) * 16 * TOPK)
                for k in range(TOPK):
                    last = mm(kv_bank[:, 0:P], got[:, h % NGB, k, :], diag[:, h % 2, k, :], start=k == 0, stop=k == TOPK - 1)
                last.then_inc(s_kv_ps, 1)
                pe.wait_ge(s_q, n + 1)
                pe.wait_ge(s_kv, n + 1)
                mm(sc_bank[:, 0:P], qt[:, :], kvt[0:D, :], start=True, stop=True)
                mm(kv_bank[:, P:P + D], kvt[D:P, :], ffn_wo[D:P, h, :], start=True, stop=True).then_inc(s_score, 1)

            def head_out(b, h):
                n = b * HEADS + h
                pe.wait_ge(s_prob, n + 1)
                tr(sc_bank[:, 256:384], prob[:, :], const("ident")).then_inc(s_prob_ps, 1)
                pe.wait_ge(s_prob_t, n + 1)
                pe.wait_ge(s_vw, n + 1)
                if h == 0 and (not isinstance(b, int) or b > 0):
                    pe.wait_ge(s_out, b)
                mm(y_bank[:, 0:D], prob_t[:, :], vw[:, :], start=h == 0, stop=h == HEADS - 1).then_inc(s_y, 1)

            pipeline(pe, tokenizer, mixer, nothing, head, head_out, nothing, nothing)

        @block.scalar
        def _(act):
            a = nc.scalar.activation
            act.wait_ge(s_setup_done, 1)

            def sq0(b, r):
                act.wait_ge(s_conv0, b * 4 + r + 1)
                if r >= 2:
                    act.wait_ge(s_var0, b * 4 + r - 1)
                a(square[:, r % 2, :], conv_bank[r % 2][:, :], ACT.Square, bias=cbias[:, 0:1]).then_inc(s_sq0, 1)

            def relu0(b, r):
                act.wait_ge(s_norm0, b * 4 + r + 1)
                u = int(r < 2)
                a(h0[:, r, u:u + T1], normed[:, r % 2, :], ACT.Relu, scale=chan[:, 4:5], bias=chan[:, 9:10]).then_inc(s_h0, 1)

            def norm(b, n, dst):
                w, ps = LEN[n], level_bank(n)[:, 0:LEN[n]]
                act.wait_ge(s_conv, b * 4 + n + 1)
                a(square[:, n % 2, 0:w], ps, ACT.Square, bias=cbias[:, n + 1:n + 2] if n < 3 else 0.0).then_inc(s_sq, 1)
                act.wait_ge(s_var, b * 4 + n + 1)
                if n:
                    act.wait_ge(s_rstd, b * 4 + n)
                else:
                    act.wait_ge(s_rstd0, b * 4 + 4)
                a(logv[:, 0:w], var_bank[:, 0:w], ACT.Ln, bias=eps[:, 0:1]).then_inc(s_log, 1)
                act.wait_ge(s_log, b * 4 + n + 1)
                a(rstd[:, n % 2, 0:w], logv[:, 0:w], ACT.Exp, scale=-0.5).then_inc(s_rstd, 1)
                act.wait_ge(s_norm, b * 4 + n + 1)
                a(dst, normed[:, n % 2, 0:w], ACT.Relu, scale=chan[:, 5 + n:6 + n], bias=chan[:, 10 + n:11 + n]).then_inc(s_h, 1)

            def tokenizer(b, part):
                if part == 0:
                    act.wait_ge(s_window_ps, b + 1)
                    a(window_t[:, :], var_bank[0:WIN, 0:P], ACT.Copy).then_inc(s_window_t, 1)
                    sq0(b, 0)
                    for r in range(4):
                        if r < 3:
                            sq0(b, r + 1)
                        act.wait_ge(s_var0, b * 4 + r + 1)
                        if r >= 2:
                            act.wait_ge(s_norm0, b * 4 + r - 1)
                        if r or not isinstance(b, int) or b > 0:
                            act.wait_ge(s_rstd0, b * 4 + r)
                        a(logv[:, :], var_bank[:, :], ACT.Ln, bias=eps[:, 0:1]).then_inc(s_log0, 1)
                        act.wait_ge(s_log0, b * 4 + r + 1)
                        a(rstd[:, r % 2, :], logv[:, :], ACT.Exp, scale=-0.5).then_inc(s_rstd0, 1)
                        if r >= 1:
                            relu0(b, r - 1)
                    relu0(b, 3)
                elif part == 1:
                    norm(b, 0, h1[:, 1:T1 + 1])
                elif part == 2:
                    norm(b, 1, h2[:, 1:T2 + 1])
                elif part == 3:
                    norm(b, 2, h3[:, :])
                elif part == 4:
                    act.wait_ge(s_z1p, b + 1)
                    for m in range(MC):
                        last = a(z1[:, m, :], conv_bank[1][:, m * P:(m + 1) * P], ACT.Gelu, bias=mlpb[:, m:m + 1])
                    last.then_inc(s_z1, 1)
                    act.wait_ge(s_z2p, b + 1)
                    for m in range(MC):
                        last = a(z2[:, m, :], conv_bank[0][:, m * P:(m + 1) * P], ACT.Gelu, bias=mlpb[:, MC + m:MC + m + 1])
                    last.then_inc(s_z2, 1)
                    act.wait_ge(s_feat_ps, b + 1)
                    a(feat[:, :], conv_bank[1][:, 0:P], ACT.Copy).then_inc(s_feat, 1)
                    act.wait_ge(s_z3p, b + 1)
                    a(imp[:, 0:1], var_bank[:, 0:1], ACT.Tanh, scale=0.5, bias=half_b3[:, :]).then_inc(s_imp_t, 1)
                else:
                    if not isinstance(b, int) or b > 0:
                        act.wait_ge(s_mdve, (b - 1) * NV + V["res"])
                    norm(b, 3, tok[:, :])

            def mixer(b, part):
                dve = lambda k: act.wait_ge(s_mdve, b * NV + V[k])
                mpe = lambda k: act.wait_ge(s_mpe, b * NE + E[k])
                own = lambda k: act.wait_ge(s_mact, b * NA + A[k])
                if part == 0:
                    dve("mean")
                    a(mlog[:, :], mv[:, 1:2], ACT.Ln, bias=eps[:, 0:1]).then_inc(s_mact, 1)
                    own("log")
                    a(mrstd[:, :], mlog[:, :], ACT.Exp, scale=-0.5).then_inc(s_mact, 1)
                    mpe("xd")
                    a(xd[:, :], mx[:, 0:P], ACT.Copy).then_inc(s_mact, 1)
                    mpe("proj")
                    a(tanh_w[:, :], my[0:D, 2 * P:3 * P], ACT.Tanh).then_inc(s_mact, 1)
                    a(lin_a[:, :], my[0:D, 3 * P:4 * P], ACT.Copy).then_inc(s_mact, 1)
                    a(sig_g[:, :], mx[:, P:2 * P], ACT.Tanh, scale=0.5).then_inc(s_mact, 1)
                    mpe("lora")
                    a(sig_wa[:, 0, :], mx[0:D, 0:P], ACT.Tanh, scale=0.5, bias=v64h[:, 0:1]).then_inc(s_mact, 1)
                    a(sig_wa[:, 1, :], mx[0:D, 320:448], ACT.Tanh, scale=0.5, bias=v64h[:, 1:2]).then_inc(s_mact, 1)
                    a(gate[:, :], mx[:, 448:512], ACT.Copy).then_inc(s_mact, 1)
                    dve("mid")
                    a(dec_up[:, :], cdec[:, :], ACT.Exp, scale=DECAY, bias=mid[:, 0:1]).then_inc(s_mact, 1)
                    a(dec_dn[:, :], cdec[:, 1:P + 1], ACT.Exp, scale=-DECAY, bias=mid[:, 1:2]).then_inc(s_mact, 1)
                    mpe("ss")
                    a(kkn[:, :], my[0:D, 384:512], ACT.Sqrt).then_inc(s_mact, 1)
                elif part == 3:
                    dve("omean")
                    a(mlog[:, :], mv[:, 1:2], ACT.Ln, bias=eps[:, 1:2]).then_inc(s_mact, 1)
                    own("olog")
                    a(mrstd[:, :], mlog[:, :], ACT.Exp, scale=-0.5).then_inc(s_mact, 1)
                elif part == 4:
                    mpe("og_t")
                    a(og_t[:, :], my[0:D, 256:384], ACT.Copy).then_inc(s_mact, 1)
                    dve("mean2")
                    a(mlog[:, :], mv[:, 1:2], ACT.Ln, bias=eps[:, 0:1]).then_inc(s_mact, 1)
                    own("log2")
                    a(mrstd[:, :], mlog[:, :], ACT.Exp, scale=-0.5).then_inc(s_mact, 1)
                    mpe("x2")
                    if not isinstance(b, int) or b > 0:
                        act.wait_ge(s_handed, b)
                    a(x2[:, :], mx[0:D, 0:P], ACT.Copy).then_inc(s_mact, 1)
                    mpe("sims")
                    sm = sims[:, :, :, :].rearrange("p h s k -> p (h s k)")
                    if not isinstance(b, int) or b > 0:
                        act.wait_ge(s_route, (b - 1) * NROUTE + R["idx_1"])
                    a(sm[:, 0:512], my[:, :], ACT.Copy).then_inc(s_simcp, 1)
                    a(sm[:, 512:1024], mx[:, :], ACT.Copy).then_inc(s_simcp, 1)

            def route(b, part):
                if part == 3:
                    act.wait_ge(s_route, b * NROUTE + R["shift"])
                    a(fexp[:, :, :], fexp[:, :, :], ACT.Exp).then_inc(s_fexp, 1)

            def head(b, h):
                n = b * HEADS + h
                act.wait_ge(s_q_ps, n + 1)
                a(qt[:, :], sc_bank[0:D, 384:512], ACT.Copy, scale=-(D ** -0.5)).then_inc(s_q, 1)
                act.wait_ge(s_kv_ps, n + 1)
                a(kvt[:, :], kv_bank[:, 0:P], ACT.Copy).then_inc(s_kv, 1)
                act.wait_ge(s_score, n + 1)
                if h or not isinstance(b, int):
                    act.wait_ge(s_y, n)
                elif b:
                    act.wait_ge(s_y, n)
                a(vw[:, :], kv_bank[:, P:P + D], ACT.Copy).then_inc(s_vw, 1)

            def head_out(b, h):
                n = b * HEADS + h
                act.wait_ge(s_neg, n + 1)
                a(ex[:, :], neg[:, :], ACT.Exp, scale=-1.0, bias=nmax[:, :], accum_out=esum[:, :]).then_inc(s_exp, 1)
                act.wait_ge(s_prob_ps, n + 1)
                a(prob_t[:, :], sc_bank[:, 256:384], ACT.Copy).then_inc(s_prob_t, 1)

            pipeline(act, tokenizer, mixer, route, head, head_out, nothing, nothing)

        @block.vector
        def _(vec):
            v = nc.vector
            tt, ts, stt, cp = v.tensor_tensor, v.tensor_scalar, v.scalar_tensor_tensor, v.tensor_copy
            count = [0]

            def done(ins):
                count[0] += 1
                ins.then_inc(s_centred, 1)
                vec.wait_ge(s_centred, count[0])

            v.memset(eps[:, 0:1], EPS)
            v.memset(eps[:, 1:2], GN_EPS)
            v.memset(ramp[:, :, :], 0.0)
            done(v.memset(cdec[:, :], 0.0))
            vec.wait_ge(s_loaded, 16 * NLOADS)
            for w, n in ((conv0_w, FR), (conv_w[1], 8), (conv_w[2], 4), (conv_w[3], 4)):
                wr = WIN if w is conv0_w else C
                done(v.tensor_reduce(wmean[0:wr, 0:n], w[:, :, :], AX.X, ALU.add))
                done(ts(wmean[0:wr, 0:n], wmean[0:wr, 0:n], 1.0 / C, None, ALU.mult))
                done(tt(w[:, :, :], w[:, :, :], wmean[0:wr, 0:n].unsqueeze(2).broadcast_to([wr, n, C]), ALU.subtract))
            for k, (at, w, row) in STACK.items():
                done(ts(proj[D:P, at:at + w], proj[D:P, at:at + w], mixc[D:P, row:row + 1], None, ALU.mult))
            done(ts(half_b3[:, :], mlpb[:, 2 * MC:], 0.5, None, ALU.mult))
            done(ts(v64h[:, 0:2], v64[:, 0:2], 0.5, None, ALU.mult))
            done(ts(v64h[:, 2:3], v64[:, 3:4], -1.0, 1.0, ALU.mult, ALU.add))
            vec.wait_ge(s_setup_pe, 2)
            done(cp(cbias[:, :], mx[:, 0:4]))
            rw = route_w[:, :, :, :].rearrange("p h s k -> p (h s k)")
            done(cp(rw[:, 0:512], conv_bank[0][0:D, :]))
            cp(rw[:, 512:1024], conv_bank[1][0:D, :]).then_inc(s_setup_done, 1)

            def norm(b, n):
                vec.wait_ge(s_rstd, b * 4 + n + 1)
                ps, w = level_bank(n)[:, 0:LEN[n]], LEN[n]
                stt(normed[:, n % 2, 0:w], ps, cbias[:, n + 1:n + 2] if n < 3 else 0.0, rstd[:, n % 2, 0:w],
                    ALU.add, ALU.mult).then_inc(s_norm, 1)

            def tokenizer(b, part):
                if part == 0:
                    for r in range(4):
                        vec.wait_ge(s_rstd0, b * 4 + r + 1)
                        if r >= 2:
                            vec.wait_ge(s_h0, b * 4 + r - 1)
                        stt(normed[:, r % 2, :], conv_bank[r % 2][:, :], cbias[:, 0:1], rstd[:, r % 2, :],
                            ALU.add, ALU.mult).then_inc(s_norm0, 1)
                    vec.wait_ge(s_h0, b * 4 + 4)
                    cp(h0[:, 0, 0:1], h0[:, 0, 1:2])
                    cp(h0[:, 1, 0:1], h0[:, 3, 0:1])
                    cp(h0[:, 2, T1:T1 + 1], h0[:, 0, T1:T1 + 1])
                    cp(h0[:, 3, T1:T1 + 1], h0[:, 3, T1 - 1:T1]).then_inc(s_pad, 1)
                elif part <= 2:
                    h, w = (h1, T1) if part == 1 else (h2, T2)
                    norm(b, part - 1)
                    vec.wait_ge(s_h, b * 4 + part)
                    cp(h[:, 0:1], h[:, 2:3])
                    cp(h[:, w + 1:w + 2], h[:, w - 1:w]).then_inc(s_pad, 1)
                elif part == 3:
                    norm(b, 2)
                elif part == 4:
                    vec.wait_ge(s_imp_t, b + 1)
                    ts(imp[:, 1:2], imp[:, 0:1], 0.5, 0.5 + 1e-5, ALU.mult, ALU.add).then_inc(s_imp, 1)
                else:
                    vec.wait_ge(s_cums, b + 1)
                    v.reciprocal(total[:, :], var_bank[:, 3:4]).then_inc(s_ramp, 1)
                    vec.wait_ge(s_ramp, b * 6 + 1)
                    ts(cums[:, :], var_bank[:, 1:3], total[:, :], float(D), ALU.mult, ALU.mult).then_inc(s_ramp, 1)
                    vec.wait_ge(s_ramp, b * 6 + 2)
                    ts(ramp[:, 0, 0:D], const("neg_iota"), cums[:, 0:1], 0.0, ALU.add, ALU.max).then_inc(s_ramp, 1)
                    ts(ramp[:, 1, 0:D], const("neg_iota"), cums[:, 1:2], 0.0, ALU.add, ALU.max).then_inc(s_ramp, 1)
                    vec.wait_ge(s_ramp, b * 6 + 4)
                    tt(dramp[:, :], ramp[:, 0, :], ramp[:, 1, :], ALU.subtract).then_inc(s_ramp, 1)
                    vec.wait_ge(s_ramp, b * 6 + 5)
                    tt(wmat[:, :], dramp[:, 0:D], dramp[:, 1:D + 1], ALU.subtract).then_inc(s_ramp, 1)
                    norm(b, 3)

            def mixer(b, part):
                def step(key, ins):
                    ins.then_inc(s_mdve, 1)
                    wait = wait_apart if "stats" in key else type(vec).wait_ge
                    wait(vec, s_mdve, b * NV + V[key])

                act = lambda k: vec.wait_ge(s_mact, b * NA + A[k])
                mpe = lambda k: vec.wait_ge(s_mpe, b * NE + E[k])
                inv2 = inv[:, :, :].rearrange("p a t -> p (a t)")

                def levels(a, z):
                    for lv in range(a, z):
                        mpe(f"p{lv}")
                        step(f"p{lv}", cp(prod[:, :], my[:, 256:384]))
                        mpe(f"t{lv}")
                        step(f"t{lv}", tt(inv2, mx[:, 0:256], inv2, ALU.add))

                if part == 0:
                    vec.wait_ge(s_h, b * 4 + 4)
                    step("stats", v.bn_stats(stats[:, :], tok[:, :]))
                    step("mean", v.bn_aggr(mv[:, :], stats[:, :]))
                    act("rstd")
                    step("ln", ts(ln[:, :], tok[:, :], mv[:, 0:1], mrstd[:, :], ALU.subtract, ALU.mult))
                    act("tanh_g")
                    step("rk", cp(rk[:, :, :].rearrange("p a t -> p (a t)"), my[0:D, 0:2 * P]))
                    step("val", cp(val[:, :], mx[:, 2 * P:2 * P + D]))
                    step("sig_g", ts(sig_g[:, :], sig_g[:, :], 0.5, 0.5, ALU.mult, ALU.add))
                    act("tanh_sa")
                    step("sig_wa", ts(sig_wa[:, :, :], sig_wa[:, :, :], 0.5, 0.5, ALU.mult, ALU.add))
                    step("cdec", v.tensor_tensor_scan(cdec[:, 1:P + 1], const("ones", rows=D), sig_wa[:, 0, :], 0.0, ALU.mult, ALU.add))
                    ts(mid[:, 0:1], cdec[:, P:P + 1], -0.5 * DECAY, None, ALU.mult)
                    step("mid", ts(mid[:, 1:2], cdec[:, P:P + 1], 0.5 * DECAY, None, ALU.mult))
                    step("kkr", ts(kkr[:, :], rk[:, 1, :], v64[:, 2:3], None, ALU.mult))
                    step("kks", tt(kks[:, :], kkr[:, :], kkr[:, :], ALU.mult))
                    act("nrm")
                    step("nrm", ts(kkn[:, :], kkn[:, :], 1e-12, None, ALU.max))
                    step("rnrm", v.reciprocal(kkn[:, :], kkn[:, :]))
                    step("kk", tt(kk[:, :], kkr[:, :], kkn[:, :], ALU.mult))
                    step("kb", tt(kb[:, :], kk[:, :], sig_wa[:, 1, :], ALU.mult))
                    step("kfac", ts(kfac[:, :], sig_wa[:, 1, :], v64[:, 3:4], v64h[:, 2:3], ALU.mult, ALU.add))
                    step("k2", tt(k2[:, :], rk[:, 1, :], kfac[:, :], ALU.mult))
                    step("left_k", tt(left[:, 0, :], kk[:, :], dec_up[:, 0:P], ALU.mult))
                    step("left_r", tt(left[:, 1, :], rk[:, 0, :], dec_up[:, 1:P + 1], ALU.mult))
                    step("right_b", tt(right[:, 0, :], kb[:, :], dec_dn[:, :], ALU.mult))
                    step("right_k", tt(right[:, 1, :], k2[:, :], dec_dn[:, :], ALU.mult))
                    step("rk2", tt(rk2[:, :], rk[:, 0, :], k2[:, :], ALU.mult))
                elif part == 1:
                    mpe("tri")
                    step("tri", tt(tri[:, :, :].rearrange("p a t -> p (a t)"), mx[:, :], const("tri"), ALU.mult))
                    step("inv0", tt(inv[:, 0, :], my[:, 0:P], const("pair"), ALU.mult))
                    step("inv0b", tt(inv[:, 0, :], inv[:, 0, :], const("ident"), ALU.add))
                    step("invt0", tt(inv[:, 1, :], tri[:, 0, :], const("pair_t"), ALU.mult))
                    step("invt0b", tt(inv[:, 1, :], inv[:, 1, :], const("ident"), ALU.add))
                    step("offs", tt(offs[:, :, :], const("merge_t").rearrange("p (l t) -> p l t", l=LEVELS),
                                    tri[:, 0:1, :].broadcast_to([P, LEVELS, P]), ALU.mult))
                    step("bonus", cp(bonus[:, :], my[:, P:P + 1]))
                    levels(0, 2)
                elif part == 2:
                    levels(2, 4)
                elif part == 3:
                    levels(4, 5)
                    mpe("rhs0")
                    step("rhs0", cp(rhs0[:, :], my[:, 384:448]))
                    mpe("sol1")
                    step("sol1", cp(sol1[:, :], my[:, 448:512]))
                    mpe("offsol")
                    step("offsol", cp(offsol[:, :], mx[:, 256:320]))
                    mpe("sol2")
                    step("sa", tt(sa[:, :], mx[:, 320:384], sol1[:, :], ALU.add))
                    mpe("o")
                    step("ostats", v.bn_stats(stats[:, :], mx[:, 384:448]))
                    step("omean", v.bn_aggr(mv[:, :], stats[:, :]))
                else:
                    act("orstd")
                    step("on", ts(og[:, 0, :], mx[:, 384:448], mv[:, 0:1], mrstd[:, :], ALU.subtract, ALU.mult))
                    step("ow", tt(og[:, 0, :], og[:, 0, :], gnb[:, 0, :], ALU.mult))
                    step("ob", tt(og[:, 0, :], og[:, 0, :], gnb[:, 1, :], ALU.add))
                    step("obonus", stt(og[:, 0, :], val[:, :], bonus[:, :], og[:, 0, :], ALU.mult, ALU.add))
                    step("og", tt(og[:, 1, :], og[:, 0, :], gate[:, :], ALU.mult))
                    mpe("wo")
                    step("res", tt(res[:, :], my[:, 384:448], tok[:, :], ALU.add))
                    step("stats2", v.bn_stats(stats[:, :], res[:, :]))
                    step("mean2", v.bn_aggr(mv[:, :], stats[:, :]))
                    act("rstd2")
                    step("ln2", ts(ln[:, :], res[:, :], mv[:, 0:1], mrstd[:, :], ALU.subtract, ALU.mult))

            def route(b, part):
                def step(key, ins):
                    ins.then_inc(s_route, 1)
                    wait_apart(vec, s_route, b * NROUTE + R[key])

                if part < 2:
                    wait_apart(vec, s_simcp, b * 2 + part + 1)
                    lists = [(h, s) for h in range(4 * part, 4 * part + 4) for s in range(2)]
                    for h, s in lists:
                        last = v.max(top[:, 0, h, s, 0:8], sims[:, h, s, :])
                    step(f"top8_{part}", last)
                    for h, s in lists:
                        v.max_index(topi[:, h, s, 0:8], top[:, 0, h, s, 0:8], sims[:, h, s, :])
                    for h, s in lists:
                        last = v.match_replace(sims[:, h, s, :], top[:, 0, h, s, 0:8], sims[:, h, s, :], LOWEST)
                    step(f"rep_{part}", last)
                    for h, s in lists:
                        last = v.max(top[:, 0, h, s, 8:16], sims[:, h, s, :])
                    step(f"top16_{part}", last)
                    for h, s in lists:
                        last = v.max_index(topi[:, h, s, 8:16], top[:, 0, h, s, 8:16], sims[:, h, s, :])
                    step(f"idx_{part}", last)
                elif part == 2:
                    cp(top[:, 1, :, 0, :], topi[:, :, 0, :])
                    step("keys", ts(top[:, 1, :, 1, :], topi[:, :, 1, :], float(NKEY), None, ALU.mult))
                    tv = top[:, :, :, :, :].rearrange("p c h s r -> p (c h) s r")
                    cv = cand[:, :, :, :].rearrange("p c h n -> p (c h) n")
                    off = 0
                    for i0, i1, nj in RECTS:
                        ni = i1 - i0
                        last = tt(cv[:, :, off:off + ni * nj].rearrange("p c (i j) -> p c i j", i=ni),
                                  tv[:, :, 0, i0:i1].unsqueeze(3).broadcast_to([P, 2 * HEADS, ni, nj]),
                                  tv[:, :, 1, 0:nj].unsqueeze(2).broadcast_to([P, 2 * HEADS, ni, nj]), ALU.add)
                        off += ni * nj
                    step("cands", last)
                    for h in range(HEADS):
                        last = v.max(fin[:, h, 0:8], cand[:, 0, h, :])
                    step("fin8", last)
                    for h in range(HEADS):
                        v.max_index(finp[:, h, 0:8], fin[:, h, 0:8], cand[:, 0, h, :])
                    for h in range(HEADS):
                        last = v.match_replace(cand[:, 0, h, :], fin[:, h, 0:8], cand[:, 0, h, :], LOWEST)
                    step("rep_f", last)
                    for h in range(HEADS):
                        last = v.max(fin[:, h, 8:16], cand[:, 0, h, :])
                    step("fin16", last)
                    for h in range(HEADS):
                        last = v.max_index(finp[:, h, 8:16], fin[:, h, 8:16], cand[:, 0, h, :])
                    step("fidx", last)
                else:
                    full = [P, HEADS, TOPK, NCAND]
                    step("shift", tt(fexp[:, :, :], fin[:, :, :], fin[:, :, 0:1].broadcast_to([P, HEADS, TOPK]), ALU.subtract))
                    step("pick", tt(pick[:, :, :, :].rearrange("p h r n -> p (h r) n"),
                                    finp[:, :, :].rearrange("p h r -> p (h r)").unsqueeze(2).broadcast_to([P, HEADS * TOPK, NCAND]),
                                    const("cand_iota").unsqueeze(1).broadcast_to([P, HEADS * TOPK, NCAND]), ALU.is_equal))
                    step("rowsel", tt(pick[:, :, :, :], pick[:, :, :, :], cand[:, 1, :, :].unsqueeze(2).broadcast_to(full), ALU.mult))
                    step("rowf", v.tensor_reduce(rowf[:, :], pick[:, :, :, :].rearrange("p h r n -> p (h r) n"), AX.X, ALU.add))
                    step("i_next", tt(i_next[:, :], rowf[:, :], const("head_base"), ALU.add))
                    vec.wait_ge(s_fexp, b + 1)
                    step("fsum", v.tensor_reduce(fsum[:, :], fexp[:, :, :], AX.X, ALU.add))
                    step("frec", v.reciprocal(fsum[:, :], fsum[:, :]))
                    step("w_next", tt(w_next[:, :, :], fexp[:, :, :], fsum[:, :].unsqueeze(2).broadcast_to([P, HEADS, TOPK]), ALU.mult))

            def hand_rows(b):
                if not isinstance(b, int) or b > 0:
                    for g in range(NGB):
                        vec.wait_ge(s_got[g], b * (HEADS // NGB) * 16 * TOPK)
                cp(rows[:, :], i_next[:, :]).then_inc(s_rows, 1)

            def hand_rest(b):
                if not isinstance(b, int) or b > 0:
                    vec.wait_ge(s_q_ps, b * HEADS)
                    vec.wait_ge(s_out, b)
                cp(weight[:, :, :], w_next[:, :, :])
                cp(res_h[:, :], res[:, :])
                cp(x2_h[:, :], x2[:, :]).then_inc(s_handed, 1)
                vec.wait_ge(s_handed, b + 1)

            def head(b, h):
                n = b * HEADS + h
                if h >= 2 or not isinstance(b, int) or b > 0:
                    vec.wait_ge(s_kv_ps, n - 1)
                tt(diag[:, h % 2, :, :], const("ident").unsqueeze(1).broadcast_to([P, TOPK, P]),
                   weight[:, h, :].unsqueeze(2).broadcast_to([P, TOPK, P]), ALU.mult).then_inc(s_diag, 1)
                if h or not isinstance(b, int) or b > 0:
                    vec.wait_ge(s_exp, n)
                wait_apart(vec, s_score, n + 1)
                v.tensor_tensor_reduce(out=neg[:, :], in0=sc_bank[:, 0:P], in1=const("future"), scale=1.0, scalar=FUTURE,
                                       op0=ALU.add, op1=ALU.min, accum_out=nmax[:, :]).then_inc(s_neg, 1)

            def head_out(b, h):
                n = b * HEADS + h
                vec.wait_ge(s_exp, n + 1)
                v.reciprocal(erec[:, :], esum[:, :]).then_inc(s_erec, 1)
                vec.wait_ge(s_erec, n + 1)
                ts(prob[:, :], ex[:, :], erec[:, :], None, ALU.mult).then_inc(s_prob, 1)
                if h == HEADS - 1:
                    vec.wait_ge(s_y, n + 1)
                    if not isinstance(b, int) or b > 0:
                        vec.wait_ge(s_stored, b * 16)
                    tt(res_o[:, :], y_bank[:, 0:D], res_h[:, :], ALU.add).then_inc(s_out, 1)

            pipeline(vec, tokenizer, mixer, route, head, head_out, hand_rows, hand_rest)


_OUT = (BATCH, C, D)


def kernel(**inputs):
    import numpy as np
    import concourse.bacc as bacc
    from concourse.bass_utils import run_bass_kernel_spmd

    nc = bacc.Bacc("TRN2", target_bir_lowering=False, num_devices=1)
    t = {k[3:]: np.asarray(v) for k, v in inputs.items() if k != "x"}
    wave = np.pad(np.asarray(inputs["x"])[:, 0, :], ((0, 0), (PAD0, PAD0)), mode="reflect")
    wave = np.concatenate([wave, np.zeros((BATCH, (P + 1) * S0 * FR - wave.shape[1]), np.float32)], 1)
    conv = lambda n: np.transpose(t[f"tok_conv{n}_w"], (1, 2, 0))
    arrays = {
        "x": wave, "consts": constants(),
        "w0": np.transpose(t["tok_conv0_w"][:, 0, :]), "w1": conv(1), "w2": conv(2), "w3": conv(3),
        "cvec": np.stack([t[f"tok_conv{n}_b"] for n in range(4)] + [t[f"tok_n{n}_w"] for n in range(5)]
                         + [t[f"tok_n{n}_b"] for n in range(5)], 1),
        "mw1": t["tok_mlp_w1"], "mw2": t["tok_mlp_w2"], "mw3": np.transpose(t["tok_mlp_w3"].reshape(MC, P)),
        "mb12": np.transpose(np.concatenate([t["tok_mlp_b1"], t["tok_mlp_b2"]]).reshape(2 * MC, P)),
        "mb3": t["tok_mlp_b3"].reshape(1, 1),
        "stack": np.concatenate([t["attn_W_r"], t["attn_W_k"], t["attn_A_w"], t["attn_A_a"], t["attn_W_v"], t["attn_A_g"]], 1),
        "mix": np.transpose(t["attn_x_mix"]),
        "bw": t["attn_B_w"], "ba": t["attn_B_a"], "bg": t["attn_B_g"],
        "vec64": np.stack([t["attn_b_w"], t["attn_b_a"], t["attn_k_k"], t["attn_k_a"], t["attn_r_k"]], 1),
        "wo_attn": t["attn_W_o"], "gn": np.stack([t["attn_gn_w"], t["attn_gn_b"]]),
        "wqpk": np.transpose(t["ffn_Wq_pk"].reshape(D, 2, HEADS, 32), (3, 1, 2, 0)),
        "keys": np.transpose(t["ffn_pk_keys"], (3, 0, 2, 1)),
        "wq": t["ffn_Wq"], "table": np.concatenate([t["ffn_keys_table"], t["ffn_values_table"]], 1), "wo_ffn": t["ffn_Wo"],
    }
    arrays = {k: np.ascontiguousarray(a) for k, a in arrays.items()}
    aps = {k: nc.dram_tensor(f"in_{k}", a.shape, mybir.dt.from_np(a.dtype), kind="ExternalInput").ap() for k, a in arrays.items()}
    out = nc.dram_tensor("out_h", _OUT, F32, kind="ExternalOutput").ap()
    tower(nc, out=out, **aps)
    r = run_bass_kernel_spmd(nc, [{f"in_{k}": a for k, a in arrays.items()}], core_ids=[0])
    return r.results[0]["out_h"]
```

```python
import math

import concourse.bass as bass
from concourse import mybir
from contextlib import ExitStack

F32 = mybir.dt.float32
U32 = mybir.dt.uint32
ALU = mybir.AluOpType
ACT = mybir.ActivationFunctionType
AX = mybir.AxisListType

BATCH = 32
WAVE = 10240
C = 128
P = 128
D = 64
T0, T1, T2, T3 = 2048, 512, 256, 128
K0, S0, PAD0 = 10, 5, 3
FR = T0 // P
WIN = S0 * (FR - 1) + K0
MLP = 512
MC = MLP // P
HEADS = 8
NKEY = 64
TOPK = 16
LORA = 64
DECAY = -0.6065306597126334
RECTS = [(0, 1, 16), (1, 2, 8), (2, 4, 5), (4, 8, 3), (8, 16, 1)]
NCAND = sum((b - a) * n for a, b, n in RECTS)
EARLY_RECTS = [(0, 1, 8), (1, 2, 4), (2, 4, 2), (4, 8, 1)]
NEARLY = sum((b - a) * n for a, b, n in EARLY_RECTS)
RECT_AT = [sum((b - a) * n for a, b, n in RECTS[:k]) for k in range(len(RECTS))]
EARLY_PLACE = [at + i * nj + j for at, (_, _, nj), (a, b, n) in zip(RECT_AT, RECTS, EARLY_RECTS)
               for i in range(b - a) for j in range(n)]
LEVELS = 6
NGB = 4
EPS = 1e-5
GN_EPS = D * 1e-5
NORM_MIN = 1e-12
LN_SCALE = 2.0 ** 30
LOWEST = -3.0e38
FUTURE = 1.0e30

CONST = {}
_at = 0
for _name, _n in (("ident", P), ("mean_sq", P), ("ones", P), ("center", P), ("upto", P), ("before", P),
                  ("shift_diff", P), ("neg_iota", D), ("cand_iota", NCAND), ("early_place", NEARLY), ("head_base", HEADS * TOPK),
                  ("tri", 4 * P), ("pair", P), ("pair_t", P), ("merge_t", LEVELS * P), ("future", P)):
    CONST[_name] = (_at, _n)
    _at += _n
NCONST = _at

STACK = {"r": (0, 64, 0), "k": (64, 64, 2), "w": (128, 64, 1), "a": (192, 64, 4), "v": (256, 64, 3), "g": (320, 128, 5)}
NSTACK = 448


def constants():
    import numpy as np
    s, t = np.arange(P)[:, None], np.arange(P)[None, :]
    out = np.zeros((P, NCONST), np.float32)

    def put(name, a):
        at, n = CONST[name]
        out[:, at:at + n] = np.reshape(a, (a.shape[0], n)) if a.ndim > 1 else a

    put("ident", (s == t) * 1.0)
    put("mean_sq", np.full((P, P), 1.0 / (C - 1)))
    put("ones", np.ones((P, P)))
    put("center", (s == t) - 1.0 / C)
    put("upto", (s <= t) * 1.0)
    put("before", (s < t) * 1.0)
    put("shift_diff", (s == t - 1) * 1.0 - (s == t))
    put("neg_iota", -np.arange(D) * 1.0)
    put("cand_iota", np.arange(NCAND) * 1.0)
    put("early_place", np.array(EARLY_PLACE) * 1.0)
    put("head_base", np.repeat(np.arange(HEADS) * NKEY * NKEY, TOPK) * 1.0)
    put("tri", np.concatenate([-1.0 * (s < t), 1.0 * (s <= t), -1.0 * (s < t), 1.0 * (s <= t)], 1))
    put("pair", -1.0 * ((s % 2 == 1) & (t == s - 1)))
    put("pair_t", 1.0 * ((t % 2 == 1) & (s == t - 1)))
    merges = []
    for lv in range(1, LEVELS + 1):
        half = 2 ** lv
        merges.append(1.0 * ((s // (2 * half) == t // (2 * half)) & (t % (2 * half) >= half) & (s % (2 * half) < half)))
    put("merge_t", np.concatenate(merges, 1))
    put("future", FUTURE * (t > s))
    return out


def tower(nc, x, consts, w0, w1, w2, w3, cvec, mw1, mw2, mw3, mb12, mb3, stack, mix, bw, ba, bg, vec64,
          wo_attn, gn, wqpk, keys, wq, table, wo_ffn, out):
    ctx = ExitStack()
    with ctx:
        def sb(name, shape, dt=F32):
            return ctx.enter_context(nc.sbuf_tensor(name, shape, dt))

        def sem(name):
            return ctx.enter_context(nc.semaphore(name))

        cst = sb("cst", [P, NCONST])

        def const(name, a=0, b=None, rows=P):
            at, n = CONST[name]
            return cst[0:rows, at + a:at + (n if b is None else b)]

        conv0_w = sb("conv0_w", [WIN, FR, C])
        conv_w = {1: sb("conv1_w", [C, 8, C]), 2: sb("conv2_w", [C, 4, C]), 3: sb("conv3_w", [C, 4, C])}
        wmean = sb("wmean", [P, FR])
        chan = sb("chan", [C, 14])
        cbias = sb("cbias", [C, 4])
        mlp1 = sb("mlp1", [C, MLP])
        mlp2 = sb("mlp2", [P, MC, MLP])
        mlp3 = sb("mlp3", [P, MC])
        mlpb = sb("mlpb", [P, 2 * MC + 1])
        half_b3 = sb("half_b3", [P, 1])
        proj = sb("proj", [P, NSTACK])
        mixc = sb("mixc", [P, 6])
        lora_w = sb("lora_w", [LORA, D])
        lora_a = sb("lora_a", [LORA, D])
        lora_g = sb("lora_g", [P, D])
        v64 = sb("v64", [D, 5])
        v64h = sb("v64h", [D, 3])
        attn_wo = sb("attn_wo", [D, D])
        gnb = sb("gnb", [P, 2, D])
        qpk = sb("qpk", [32, 2, HEADS, D])
        pkk = sb("pkk", [32, 2, HEADS, NKEY])
        route_w = sb("route_w", [D, HEADS, 2, NKEY])
        ffn_wq = sb("ffn_wq", [D, HEADS * D])
        ffn_wo = sb("ffn_wo", [P, HEADS, D])
        eps = sb("eps", [P, 3])

        window = sb("window", [P, WIN])
        window_t = sb("window_t", [WIN, P])
        square = sb("square", [P, 2, 512])
        logv = sb("logv", [P, 512])
        rstd = sb("rstd", [P, 2, 512])
        normed = sb("normed", [P, 2, 512])
        h0 = sb("h0", [C, 4, T1 + 1])
        h1 = sb("h1", [C, T1 + 2])
        h2 = sb("h2", [C, T2 + 2])
        h3 = sb("h3", [C, T3])
        z1 = sb("z1", [P, MC, T3])
        z2 = sb("z2", [P, MC, T3])
        imp = sb("imp", [P, 2])
        total = sb("total", [P, 1])
        cums = sb("cums", [P, 2])
        ramp = sb("ramp", [P, 2, D + 1])
        dramp = sb("dramp", [P, D + 1])
        wmat = sb("wmat", [P, D])
        feat = sb("feat", [P, C])
        tok = sb("tok", [C, D])

        res = sb("res", [P, D])
        stats = sb("stats", [P, 6])
        mv = sb("mv", [P, 2])
        mlog = sb("mlog", [P, 1])
        mrstd = sb("mrstd", [P, 1])
        ln = sb("ln", [P, D])
        xd = sb("xd", [P, P])
        rk = sb("rk", [D, 2, P])
        val = sb("val", [P, D])
        tanh_w = sb("tanh_w", [LORA, P])
        lin_a = sb("lin_a", [LORA, P])
        sig_g = sb("sig_g", [P, P])
        sig_wa = sb("sig_wa", [D, 2, P])
        gate = sb("gate", [P, D])
        cdec = sb("cdec", [D, P + 1])
        mid = sb("mid", [D, 2])
        dec_up = sb("dec_up", [D, P + 1])
        dec_dn = sb("dec_dn", [D, P])
        kkr = sb("kkr", [D, P])
        kks = sb("kks", [D, P])
        kklog = sb("kklog", [D, P])
        kkn = sb("kkn", [D, P])
        kk = sb("kk", [D, P])
        kb = sb("kb", [D, P])
        kfac = sb("kfac", [D, P])
        k2 = sb("k2", [D, P])
        rk2 = sb("rk2", [D, P])
        left = sb("left", [D, 2, P])
        right = sb("right", [D, 2, P])
        tri = sb("tri", [P, 4, P])
        offs = sb("offs", [P, LEVELS, P])
        inv = sb("inv", [P, 2, P])
        prod = sb("prod", [P, P])
        rhs0 = sb("rhs0", [P, D])
        sol1 = sb("sol1", [P, D])
        offsol = sb("offsol", [P, D])
        sa = sb("sa", [P, D])
        bonus = sb("bonus", [P, 1])
        og = sb("og", [P, 2, D])
        og_t = sb("og_t", [D, P])
        x2 = sb("x2", [D, P])

        sims = sb("sims", [P, HEADS, 2, NKEY])
        top = sb("top", [P, 2, HEADS, 2, TOPK])
        topi = sb("topi", [P, HEADS, 2, TOPK], U32)
        cand = sb("cand", [P, 2, HEADS, NCAND])
        fin = sb("fin", [P, HEADS, TOPK])
        finp = sb("finp", [P, HEADS, TOPK], U32)
        early = sb("early", [P, HEADS, NEARLY])
        pick_e = sb("pick_e", [P, HEADS, 8, NEARLY])
        pick = sb("pick", [P, HEADS, 8, NCAND])
        rowf = sb("rowf", [P, HEADS, TOPK])
        fexp = sb("fexp", [P, HEADS, TOPK])
        fsum = sb("fsum", [P, HEADS])
        w_next = sb("w_next", [P, HEADS, TOPK])
        i_next = sb("i_next", [P, HEADS * TOPK], U32)

        rows = sb("rows", [P, HEADS * TOPK], U32)
        weight = sb("weight", [P, HEADS, TOPK])
        res_h = sb("res_h", [P, D])
        x2_h = sb("x2_h", [D, P])
        got = sb("got", [P, NGB, TOPK, P])
        kv = sb("kv", [P, 2, P])
        qt = sb("qt", [D, P])
        kvt = sb("kvt", [P, P])
        vw = sb("vw", [P, D])
        neg = sb("neg", [P, P])
        nmax = sb("nmax", [P, 1])
        ex = sb("ex", [P, P])
        esum = sb("esum", [P, 1])
        erec = sb("erec", [P, 1])
        prob = sb("prob", [P, P])
        prob_t = sb("prob_t", [P, P])
        res_o = sb("res_o", [P, D])

        bank = [ctx.enter_context(nc.psum_tensor(f"bank{i}", [P, 512], F32)) for i in range(8)]
        conv_bank, var_bank = (bank[0], bank[1]), bank[2]
        mx, my = bank[3], bank[4]
        kv_bank, sc_bank, y_bank = bank[5], bank[6], bank[7]

        s_loaded = sem("s_loaded")
        s_cleared = sem("s_cleared")
        s_centred = sem("s_centred")
        s_setup_pe = sem("s_setup_pe")
        s_setup_done = sem("s_setup_done")
        s_wave = sem("s_wave")
        s_window_ps = sem("s_window_ps")
        s_window_t = sem("s_window_t")
        s_conv0 = sem("s_conv0")
        s_sq0 = sem("s_sq0")
        s_var0 = sem("s_var0")
        s_log0 = sem("s_log0")
        s_rstd0 = sem("s_rstd0")
        s_norm0 = sem("s_norm0")
        s_h0 = sem("s_h0")
        s_pad = sem("s_pad")
        s_conv = sem("s_conv")
        s_sq = sem("s_sq")
        s_var = sem("s_var")
        s_log = sem("s_log")
        s_rstd = sem("s_rstd")
        s_norm = sem("s_norm")
        s_h = sem("s_h")
        s_z1p, s_z1, s_z2p, s_z2 = sem("s_z1p"), sem("s_z1"), sem("s_z2p"), sem("s_z2")
        s_z3p, s_imp_t, s_imp = sem("s_z3p"), sem("s_imp_t"), sem("s_imp")
        s_cums = sem("s_cums")
        s_ramp = sem("s_ramp")
        s_feat_ps, s_feat = sem("s_feat_ps"), sem("s_feat")
        s_mdve = sem("s_mdve")
        s_mact = sem("s_mact")
        s_mpe = sem("s_mpe")
        s_route = sem("s_route")
        s_simcp = sem("s_simcp")
        s_fexp = sem("s_fexp")
        s_rows = sem("s_rows")
        s_handed = sem("s_handed")
        s_got = [sem(f"s_got{i}") for i in range(NGB)]
        s_scaled = sem("s_scaled")
        s_sum = sem("s_sum")
        s_q_ps = sem("s_q_ps")
        s_q = sem("s_q")
        s_kv_ps = sem("s_kv_ps")
        s_kv = sem("s_kv")
        s_score = sem("s_score")
        s_vw = sem("s_vw")
        s_neg = sem("s_neg")
        s_exp = sem("s_exp")
        s_erec = sem("s_erec")
        s_prob = sem("s_prob")
        s_prob_ps = sem("s_prob_ps")
        s_prob_t = sem("s_prob_t")
        s_y = sem("s_y")
        s_waited = sem("s_waited")
        s_out = sem("s_out")
        s_stored = sem("s_stored")

        block = ctx.enter_context(nc.Block())

        def wait_apart(eng, sem, value):
            eng.wait_ge(sem, value)
            if not isinstance(value, int):
                eng.sem_inc(s_waited, 1)

        def level_bank(n):
            return conv_bank[(0, 1, 0, 0)[n]]

        LEN = (T1, T2, T3, D)
        V = {}
        for n, k in enumerate(("stats", "mean", "ln", "rk", "val", "sig_g", "sig_wa", "cdec", "mid", "kkr", "kks",
                               "nmax", "kk", "kb", "kfac", "k2", "left_k", "left_r", "right_b", "right_k", "rk2", "tri",
                               "inv0", "inv0b", "invt0", "invt0b", "offs", "bonus",
                               "p0", "t0", "p1", "t1", "p2", "t2", "p3", "t3", "p4", "t4",
                               "rhs0", "sol1", "offsol", "sa", "ostats", "omean", "on", "ow", "ob", "obonus", "og",
                               "res", "stats2", "mean2", "ln2"), 1):
            V[k] = n
        A = {}
        for n, k in enumerate(("log", "rstd", "xd", "tanh_w", "lin_a", "tanh_g", "tanh_sw", "tanh_sa", "gate",
                               "dec_up", "dec_dn", "nlog", "nrm", "olog", "orstd", "og_t", "log2", "rstd2", "x2"), 1):
            A[k] = n
        E = {}
        for n, k in enumerate(("xd", "proj", "lora", "ss", "tri", "p0", "t0", "p1", "t1", "p2", "t2", "p3", "t3", "p4", "t4",
                               "rhs0", "sol1", "offsol", "sol2", "o", "og_t", "wo", "x2", "sims"), 1):
            E[k] = n
        NV, NA, NE = len(V), len(A), len(E)
        R = {k: n for n, k in enumerate((
            "top8_0", "rep_0", "top16_0", "idx_0", "top8_1", "rep_1", "top16_1", "idx_1", "keys", "cands",
            "fin8", "rep_f", "fin16", "fidx", "shift", "early", "pick_e", "sel_e", "row_e", "pick_l", "sel_l", "row_l",
            "i_next", "fsum", "frec", "w_next"), 1)}
        NROUTE = len(R)
        def quarter(r):
            return [(f"v{r}", 1.2), (f"e{r}", 1.2), (f"n{r}", 1.0), (f"c{r + 2}", 1.6)]

        def layer(n):
            return [(f"k{n}", (6.8, 2, 1, 0.5)[n - 1]), (f"s{n}", 0.7), (f"w{n}", 1.0), (f"x{n}", 1.2), (f"y{n}", 0.8), (f"h{n}", 0.8)]

        def level(lv):
            return [(f"p{lv}", 0.7), (f"pc{lv}", 0.5), (f"t{lv}", 1.0), (f"tc{lv}", 0.6)]

        def head_hops(h):
            return [(f"a{h}", 2.2), (f"aa{h}", 2.2), (f"b{h}", 2.4), (f"d{h}", 1.2), (f"f{h}", 0.6), (f"g{h}", 1.5), (f"i{h}", 0.8),
                    (f"j{h}", 1.0), (f"k{h}", 1.0), (f"l{h}", 1.0), (f"m{h}", 0.6), (f"y{h}", 1.0)]

        T_HOPS = ([("win", 1.0), ("win_t", 0.6), ("c0", 1.6), ("c1", 1.6)] + quarter(0) + quarter(1) + quarter(2) + quarter(3)
                  + [("pad0", 0.6)] + layer(1) + [("pad1", 0.5)] + layer(2) + [("pad2", 0.5)] + layer(3)
                  + [("z1p", 1.6), ("z1", 2.4), ("z2p", 6.5), ("z2", 2.6), ("z3p", 1.0), ("imp_t", 1.0), ("imp", 0.5), ("cums", 1.0),
                     ("ramp", 1.6), ("pool", 0.7)] + layer(4)[1:])
        M_HOPS = ([("stats", 0.6), ("log", 0.8), ("ln", 0.6), ("xd", 1.0), ("xd_t", 0.6), ("proj", 2.7), ("tanh", 1.8), ("rk", 1.5),
                   ("lora", 1.4), ("tanh2", 1.6), ("wa", 1.6), ("ss", 0.7), ("dec", 0.9), ("nmax", 0.5), ("nrm", 0.7), ("kk", 3.0),
                   ("tri", 3.0), ("trim", 3.2)] + [x for lv in range(LEVELS - 1) for x in level(lv)]
                  + [(k, 0.7) for k in ("rhs0", "rhs0c", "sol1", "sol1c", "offsol", "offsolc", "sol2", "sa", "o", "ostats", "olog")]
                  + [("og", 1.6), ("og_t", 0.7), ("og_tc", 0.6), ("wo", 0.7), ("res", 1.0), ("log2", 0.8), ("ln2", 0.6), ("x2", 0.7),
                     ("x2c", 0.6), ("sims", 3.6), ("simcp", 1.2)]
                  + [(f"r{k}", t) for k, t in enumerate((1.2, 1.2, 2.2, 1.2, 1.2) * 2)]
                  + [("keys", 0.7), ("cands", 1.8), ("fin8", 1.2), ("finx", 1.2), ("repf", 2.0), ("fin16", 1.2), ("fidx", 1.2), ("shift", 0.3),
                     ("early", 0.5), ("e0", 1.5), ("e1", 1.5), ("e2", 1.5), ("l0", 3.8), ("l1", 3.8), ("l2", 3.8), ("i_next", 0.3),
                     ("w_next", 0.8)])

        def h_hops(prev, cur):
            return ((head_hops(HEADS - 1) + [("out", 0.5)] if prev else []) + ([("hand", 0.6)] if cur else [])
                    + [x for h in range(HEADS - 1) if cur for x in head_hops(h)])

        def merged(*stages):
            order = []
            for stage, hops in enumerate(stages):
                total, at = sum(t for _, t in hops), 0.0
                for name, t in hops:
                    order.append(((at + t / 2) / total, stage, name))
                    at += t
            return [(stage, name) for _, stage, name in sorted(order)]

        def pipeline(eng, tokenizer, mixer, heads, hand_rows):
            def step(tb, mb, prev, cur):
                stages = (T_HOPS if tb is not None else [], M_HOPS if mb is not None else [], h_hops(prev is not None, cur is not None))
                shares = [tokenizer(tb) if tb is not None else iter(()), mixer(mb) if mb is not None else iter(()), heads(prev, cur)]
                nxt = [next(g, None) for g in shares]
                for stage, name in merged(*stages):
                    if nxt[stage] == name:
                        nxt[stage] = next(shares[stage], None)
                assert nxt == [None] * 3, nxt
                if mb is not None:
                    hand_rows(mb)

            step(0, None, None, None)
            step(None, 0, None, None)
            step(1, None, None, None)
            step(2, 1, None, 0)
            with eng.Fori(1, BATCH - 2) as b:
                step(b + 2, b + 1, b - 1, b)
            step(None, BATCH - 1, BATCH - 3, BATCH - 2)
            step(None, None, BATCH - 2, BATCH - 1)
            step(None, None, BATCH - 1, None)

        def in_turn(head, hand, out):
            def heads(prev, cur):
                if prev is not None:
                    yield from head(prev, HEADS - 1)
                    yield from out(prev)
                if cur is not None:
                    yield from hand(cur)
                    for h in range(HEADS - 1):
                        yield from head(cur, h)
            return heads

        def nothing(b=None):
            return iter(())

        LOADS = [(cst[:, :], consts), (chan[:, :], cvec), (mlp1[:, :], mw1),
                 (mlp2[:, :, :], mw2.rearrange("(k p) n -> p k n", p=P)),
                 (mlp3[:, :], mw3), (mlpb[:, 0:2 * MC], mb12), (mlpb[:, 2 * MC:], mb3.broadcast_to([P, 1])),
                 (proj[0:D, :], stack), (proj[D:P, :], stack),
                 (lora_w[:, :], bw), (lora_a[:, :], ba), (lora_g[:, :], bg), (v64[:, :], vec64),
                 (attn_wo[:, :], wo_attn), (gnb[:, :, :], gn.rearrange("(o a) d -> o a d", o=1).broadcast_to([P, 2, D])),
                 (qpk[:, :, :, :], wqpk), (pkk[:, :, :, :], keys), (ffn_wq[:, :], wq),
                 (ffn_wo[D:P, :, :], wo_ffn.rearrange("(h d) n -> d h n", d=D)),
                 (conv_w[1][:, :, :], w1), (conv_w[2][:, :, :], w2), (conv_w[3][:, :, :], w3)]
        NLOADS = len(LOADS) + FR + 1

        @block.sync
        def _(sp):
            for dst, src in LOADS:
                sp.dma_start(dst, src).then_inc(s_loaded, 16)
            sp.wait_ge(s_cleared, 2)
            for j in range(FR):
                sp.dma_start(conv0_w[S0 * j:S0 * j + K0, j, :], w0).then_inc(s_loaded, 16)
            sp.dma_start(mixc[D:P, :], mix).then_inc(s_loaded, 16)

            def load_wave(b):
                n = S0 * FR
                sp.dma_start(window[:, 0:n], x[bass.ds(b, 1), 0:P * n].rearrange("o (p n) -> (o p) n", p=P)).then_inc(s_wave, 16)
                sp.dma_start(window[:, n:WIN], x[bass.ds(b, 1), n:(P + 1) * n].rearrange("o (p n) -> (o p) n", p=P)[:, 0:WIN - n]).then_inc(s_wave, 16)

            def store(b):
                sp.wait_ge(s_out, b + 1)
                sp.dma_start(out[bass.ds(b, 1), :, :].rearrange("o c d -> (o c) d"), res_o[:, :]).then_inc(s_stored, 16)

            load_wave(0)
            sp.wait_ge(s_window_ps, 1)
            load_wave(1)
            sp.wait_ge(s_window_ps, 2)
            load_wave(2)
            with sp.Fori(0, BATCH - 3) as b:
                sp.wait_ge(s_window_ps, b + 3)
                load_wave(b + 3)
                store(b)
            for b in range(BATCH - 3, BATCH):
                store(b)
            sp.wait_ge(s_stored, 16 * BATCH)

        @block.gpsimd
        def _(pool):
            nc.gpsimd.memset(conv0_w[:, :, :], 0.0).then_inc(s_cleared, 1)
            nc.gpsimd.memset(mixc[:, :], 1.0).then_inc(s_cleared, 1)

            def gathers(b):
                wait_apart(pool, s_rows, b + 1)
                for h in range(HEADS):
                    g = h % NGB
                    if h >= NGB or not isinstance(b, int):
                        wait_apart(pool, s_sum, b * HEADS + h - NGB + 1)
                    for k in range(TOPK):
                        pool.indirect_dma_start(got[:, g, k, :], None, table,
                                                bass.IndirectOffsetOnAxis(ap=rows[:, h * TOPK + k:h * TOPK + k + 1], axis=0)
                                                ).then_inc(s_got[g], 16)

            gathers(0)
            with pool.Fori(1, BATCH) as b:
                gathers(b)

        @block.tensor
        def _(pe):
            mm, tr = nc.tensor.matmul, nc.tensor.transpose
            pe.wait_ge(s_loaded, 16 * NLOADS)
            mm(mx[:, 0:4], const("center"), chan[:, 0:4], start=True, stop=True).then_inc(s_setup_pe, 1)
            for n in range(2 * HEADS):
                h, p = n // 2, n % 2
                last = mm(conv_bank[n // 8][0:D, (n % 8) * NKEY:(n % 8 + 1) * NKEY], qpk[:, p, h, :], pkk[:, p, h, :], start=True, stop=True)
            last.then_inc(s_setup_pe, 1)
            pe.wait_ge(s_setup_done, 1)

            def variance(b, n):
                pe.wait_ge(s_sq, b * 4 + n + 1)
                mm(var_bank[:, 0:LEN[n]], const("mean_sq"), square[:, n % 2, 0:LEN[n]], start=True, stop=True).then_inc(s_var, 1)

            def tokenizer(b):
                yield "win"
                pe.wait_ge(s_wave, 32 * (b + 1))
                if not isinstance(b, int) or b > 0:
                    pe.wait_ge(s_log, b * 4)
                tr(var_bank[0:WIN, 0:P], window[:, :], const("ident")).then_inc(s_window_ps, 1)
                yield "c0"
                pe.wait_ge(s_window_t, b + 1)
                conv0(b, 0)
                yield "c1"
                conv0(b, 1)
                for r in range(4):
                    yield f"v{r}"
                    pe.wait_ge(s_sq0, b * 4 + r + 1)
                    if r >= 1:
                        pe.wait_ge(s_log0, b * 4 + r)
                    mm(var_bank[:, :], const("mean_sq"), square[:, r % 2, :], start=True, stop=True).then_inc(s_var0, 1)
                    if r < 2:
                        yield f"c{r + 2}"
                        pe.wait_ge(s_norm0, b * 4 + r + 1)
                        conv0(b, r + 2)
                for n in (1, 2, 3):
                    yield f"k{n}"
                    pe.wait_ge(s_pad, b * 3 + n)
                    taps = 8 if n == 1 else 4
                    for k in range(taps):
                        if n == 1:
                            rhs = h0[:, k % 4, k // 4:k // 4 + T1]
                        else:
                            rhs = (h1 if n == 2 else h2)[:, k:k + 2 * LEN[n - 1] - 1:2]
                        last = mm(level_bank(n - 1)[:, 0:LEN[n - 1]], conv_w[n][:, k, :], rhs, start=k == 0, stop=k == taps - 1)
                    last.then_inc(s_conv, 1)
                    yield f"w{n}"
                    variance(b, n - 1)
                yield "z1p"
                pe.wait_ge(s_h, b * 4 + 3)
                for m in range(MC):
                    last = mm(conv_bank[1][:, m * P:(m + 1) * P], mlp1[:, m * P:(m + 1) * P], h3[:, :], start=True, stop=True)
                last.then_inc(s_z1p, 1)
                yield "z2p"
                pe.wait_ge(s_z1, b + 1)
                for m in range(MC):
                    for k in range(MC):
                        last = mm(conv_bank[0][:, m * P:(m + 1) * P], mlp2[:, k, m * P:(m + 1) * P], z1[:, k, :], start=k == 0, stop=k == MC - 1)
                last.then_inc(s_z2p, 1)
                mm(conv_bank[1][:, 0:P], h3[:, :], const("center"), start=True, stop=True).then_inc(s_feat_ps, 1)
                yield "z3p"
                pe.wait_ge(s_z2, b + 1)
                for k in range(MC):
                    last = mm(var_bank[:, 0:1], z2[:, k, :], mlp3[:, k:k + 1], start=k == 0, stop=k == MC - 1)
                last.then_inc(s_z3p, 1)
                yield "cums"
                pe.wait_ge(s_imp, b + 1)
                mm(var_bank[:, 1:2], const("upto"), imp[:, 1:2], start=True, stop=True)
                mm(var_bank[:, 2:3], const("before"), imp[:, 1:2], start=True, stop=True)
                mm(var_bank[:, 3:4], const("ones"), imp[:, 1:2], start=True, stop=True).then_inc(s_cums, 1)
                yield "pool"
                pe.wait_ge(s_feat, b + 1)
                pe.wait_ge(s_ramp, b * 6 + 6)
                mm(conv_bank[0][:, 0:D], feat[:, :], wmat[:, :], start=True, stop=True).then_inc(s_conv, 1)
                yield "w4"
                variance(b, 3)

            def conv0(b, r):
                for q in range(4):
                    j = 4 * (q + (r < 2)) + r - 2
                    last = mm(conv_bank[r % 2][:, q:512:4], conv0_w[:, j, :], window_t[:, :], start=True, stop=True)
                last.then_inc(s_conv0, 1)

            def mixer(b):
                dve = lambda k: pe.wait_ge(s_mdve, b * NV + V[k])
                act = lambda k: pe.wait_ge(s_mact, b * NA + A[k])
                yield "xd"
                dve("ln")
                mm(mx[0:D, 0:P], ln[:, :], const("ident"), start=True, stop=True)
                mm(mx[D:P, 0:P], ln[:, :], const("shift_diff"), start=True, stop=True).then_inc(s_mpe, 1)
                yield "proj"
                act("xd")
                for n, k in enumerate("rkwa"):
                    at, w, _ = STACK[k]
                    mm(my[0:D, n * P:(n + 1) * P], proj[:, at:at + w], xd[:, :], start=True, stop=True)
                at, w, _ = STACK["g"]
                mm(mx[:, P:2 * P], proj[:, at:at + w], xd[:, :], start=True, stop=True)
                at, w, _ = STACK["v"]
                mm(mx[:, 2 * P:2 * P + D], xd[:, :], proj[:, at:at + w], start=True, stop=True).then_inc(s_mpe, 1)
                yield "lora"
                wait_apart(pe, s_mdve, b * NV + V["sig_g"])
                mm(mx[0:D, 0:P], lora_w[:, :], tanh_w[:, :], start=True, stop=True)
                mm(mx[0:D, 320:448], lora_a[:, :], lin_a[:, :], start=True, stop=True)
                mm(mx[:, 448:512], sig_g[:, :], lora_g[:, :], start=True, stop=True).then_inc(s_mpe, 1)
                yield "ss"
                wait_apart(pe, s_mdve, b * NV + V["kks"])
                mm(my[0:D, 384:512], const("ones", 0, D, rows=D), kks[:, :], start=True, stop=True).then_inc(s_mpe, 1)
                yield "tri"
                dve("rk2")
                act("gate")
                mm(mx[:, 0:256], right[:, 0, :], left[:, :, :].rearrange("p a t -> p (a t)"), start=True, stop=True)
                mm(mx[:, 256:512], right[:, 1, :], left[:, :, :].rearrange("p a t -> p (a t)"), start=True, stop=True)
                mm(my[:, 0:P], left[:, 0, :], right[:, 0, :], start=True, stop=True)
                mm(my[:, P:P + 1], rk2[:, :], v64[:, 4:5], start=True, stop=True).then_inc(s_mpe, 1)
                for lv in range(LEVELS - 1):
                    yield f"p{lv}"
                    dve("bonus" if lv == 0 else f"t{lv - 1}")
                    mm(my[:, 256:384], offs[:, lv, :], inv[:, 0, :], start=True, stop=True).then_inc(s_mpe, 1)
                    yield f"t{lv}"
                    dve(f"p{lv}")
                    mm(mx[:, 0:P], inv[:, 1, :], prod[:, :], start=True, stop=True)
                    mm(mx[:, P:2 * P], prod[:, :], inv[:, 1, :], start=True, stop=True).then_inc(s_mpe, 1)
                yield "rhs0"
                mm(my[:, 384:448], tri[:, 2, :], val[:, :], start=True, stop=True).then_inc(s_mpe, 1)
                yield "sol1"
                dve("rhs0")
                mm(my[:, 448:512], inv[:, 1, :], rhs0[:, :], start=True, stop=True).then_inc(s_mpe, 1)
                yield "offsol"
                dve("sol1")
                mm(mx[:, 256:320], offs[:, LEVELS - 1, :], sol1[:, :], start=True, stop=True).then_inc(s_mpe, 1)
                yield "sol2"
                dve("offsol")
                mm(mx[:, 320:384], inv[:, 1, :], offsol[:, :], start=True, stop=True).then_inc(s_mpe, 1)
                yield "o"
                dve("sa")
                mm(mx[:, 384:448], tri[:, 1, :], sa[:, :], start=True, stop=False)
                mm(mx[:, 384:448], tri[:, 3, :], val[:, :], start=False, stop=True).then_inc(s_mpe, 1)
                yield "og_t"
                wait_apart(pe, s_mdve, b * NV + V["og"])
                tr(my[0:D, 256:384], og[:, 1, :], const("ident")).then_inc(s_mpe, 1)
                yield "wo"
                wait_apart(pe, s_mact, b * NA + A["og_t"])
                mm(my[:, 384:448], og_t[:, :], attn_wo[:, :], start=True, stop=True).then_inc(s_mpe, 1)
                yield "x2"
                wait_apart(pe, s_mdve, b * NV + V["ln2"])
                tr(mx[0:D, 0:P], ln[:, :], const("ident")).then_inc(s_mpe, 1)
                yield "sims"
                act("x2")
                rw = route_w[:, :, :, :].rearrange("p h s k -> p (h s k)")
                mm(my[:, :], x2[:, :], rw[:, 0:512], start=True, stop=True)
                mm(mx[:, :], x2[:, :], rw[:, 512:1024], start=True, stop=True).then_inc(s_mpe, 1)

            def head(b, h):
                n = b * HEADS + h
                yield f"b{h}"
                if h == 0:
                    wait_apart(pe, s_handed, b + 1)
                mm(sc_bank[0:D, 384:512], ffn_wq[:, h * D:(h + 1) * D], x2_h[:, :], start=True, stop=True).then_inc(s_q_ps, 1)
                yield f"d{h}"
                pe.wait_ge(s_sum, n + 1)
                tr(kv_bank[:, 0:P], kv[:, h % 2, :], const("ident")).then_inc(s_kv_ps, 1)
                yield f"g{h}"
                pe.wait_ge(s_q, n + 1)
                pe.wait_ge(s_kv, n + 1)
                mm(sc_bank[:, 0:P], qt[:, :], kvt[0:D, :], start=True, stop=True)
                mm(kv_bank[:, P:P + D], kvt[D:P, :], ffn_wo[D:P, h, :], start=True, stop=True).then_inc(s_score, 1)
                yield f"l{h}"
                pe.wait_ge(s_prob, n + 1)
                tr(sc_bank[:, 256:384], prob[:, :], const("ident")).then_inc(s_prob_ps, 1)
                yield f"y{h}"
                pe.wait_ge(s_prob_t, n + 1)
                pe.wait_ge(s_vw, n + 1)
                if h == 0 and (not isinstance(b, int) or b > 0):
                    pe.wait_ge(s_out, b)
                mm(y_bank[:, 0:D], prob_t[:, :], vw[:, :], start=h == 0, stop=h == HEADS - 1).then_inc(s_y, 1)

            pipeline(pe, tokenizer, mixer, in_turn(head, nothing, nothing), nothing)

        @block.scalar
        def _(act):
            a = nc.scalar.activation
            exp_and_ln = lambda: nc.scalar.preload_act_table_set("natural_log_exp_and_others")
            exp_and_ln()
            act.wait_ge(s_setup_done, 1)

            def sq0(b, r):
                act.wait_ge(s_conv0, b * 4 + r + 1)
                if r >= 2:
                    act.wait_ge(s_var0, b * 4 + r - 1)
                a(square[:, r % 2, :], conv_bank[r % 2][:, :], ACT.Square, bias=cbias[:, 0:1]).then_inc(s_sq0, 1)

            def tokenizer(b):
                yield "win_t"
                act.wait_ge(s_window_ps, b + 1)
                a(window_t[:, :], var_bank[0:WIN, 0:P], ACT.Copy).then_inc(s_window_t, 1)
                yield "c1"
                sq0(b, 0)
                for r in range(4):
                    if r < 3:
                        yield f"v{r}"
                        sq0(b, r + 1)
                    yield f"e{r}"
                    act.wait_ge(s_var0, b * 4 + r + 1)
                    if r >= 2:
                        act.wait_ge(s_norm0, b * 4 + r - 1)
                    if r or not isinstance(b, int) or b > 0:
                        act.wait_ge(s_rstd0, b * 4 + r)
                    a(logv[:, :], var_bank[:, :], ACT.Ln, bias=eps[:, 0:1]).then_inc(s_log0, 1)
                    act.wait_ge(s_log0, b * 4 + r + 1)
                    a(rstd[:, r % 2, :], logv[:, :], ACT.Exp, scale=-0.5).then_inc(s_rstd0, 1)
                    yield f"c{r + 2}"
                    act.wait_ge(s_norm0, b * 4 + r + 1)
                    u = int(r < 2)
                    a(h0[:, r, u:u + T1], normed[:, r % 2, :], ACT.Relu, scale=chan[:, 4:5], bias=chan[:, 9:10]).then_inc(s_h0, 1)
                yield from norm(b, 0, h1[:, 1:T1 + 1])
                yield from norm(b, 1, h2[:, 1:T2 + 1])
                yield from norm(b, 2, h3[:, :])
                yield "z1"
                act.wait_ge(s_z1p, b + 1)
                for m in range(MC):
                    last = a(z1[:, m, :], conv_bank[1][:, m * P:(m + 1) * P], ACT.Gelu, bias=mlpb[:, m:m + 1])
                last.then_inc(s_z1, 1)
                exp_and_ln()
                yield "z2"
                act.wait_ge(s_z2p, b + 1)
                for m in range(MC):
                    last = a(z2[:, m, :], conv_bank[0][:, m * P:(m + 1) * P], ACT.Gelu, bias=mlpb[:, MC + m:MC + m + 1])
                last.then_inc(s_z2, 1)
                exp_and_ln()
                act.wait_ge(s_feat_ps, b + 1)
                a(feat[:, :], conv_bank[1][:, 0:P], ACT.Copy).then_inc(s_feat, 1)
                yield "imp_t"
                act.wait_ge(s_z3p, b + 1)
                a(imp[:, 0:1], var_bank[:, 0:1], ACT.Tanh, scale=0.5, bias=half_b3[:, :]).then_inc(s_imp_t, 1)
                exp_and_ln()
                yield from norm(b, 3, tok[:, :])

            def norm(b, n, dst):
                w, ps = LEN[n], level_bank(n)[:, 0:LEN[n]]
                yield f"s{n + 1}"
                act.wait_ge(s_conv, b * 4 + n + 1)
                a(square[:, n % 2, 0:w], ps, ACT.Square, bias=cbias[:, n + 1:n + 2] if n < 3 else 0.0).then_inc(s_sq, 1)
                yield f"x{n + 1}"
                act.wait_ge(s_var, b * 4 + n + 1)
                if n:
                    act.wait_ge(s_rstd, b * 4 + n)
                else:
                    act.wait_ge(s_rstd0, b * 4 + 4)
                a(logv[:, 0:w], var_bank[:, 0:w], ACT.Ln, bias=eps[:, 0:1]).then_inc(s_log, 1)
                act.wait_ge(s_log, b * 4 + n + 1)
                a(rstd[:, n % 2, 0:w], logv[:, 0:w], ACT.Exp, scale=-0.5).then_inc(s_rstd, 1)
                yield f"h{n + 1}"
                act.wait_ge(s_norm, b * 4 + n + 1)
                if n == 3 and (not isinstance(b, int) or b > 0):
                    act.wait_ge(s_mdve, (b - 1) * NV + V["res"])
                a(dst, normed[:, n % 2, 0:w], ACT.Relu, scale=chan[:, 5 + n:6 + n], bias=chan[:, 10 + n:11 + n]).then_inc(s_h, 1)

            def mixer(b):
                dve = lambda k: act.wait_ge(s_mdve, b * NV + V[k])
                mpe = lambda k: act.wait_ge(s_mpe, b * NE + E[k])
                own = lambda k: act.wait_ge(s_mact, b * NA + A[k])
                later = not isinstance(b, int) or b > 0
                yield "log"
                dve("mean")
                a(mlog[:, :], mv[:, 1:2], ACT.Ln, bias=eps[:, 0:1]).then_inc(s_mact, 1)
                own("log")
                a(mrstd[:, :], mlog[:, :], ACT.Exp, scale=-0.5).then_inc(s_mact, 1)
                yield "xd_t"
                mpe("xd")
                a(xd[:, :], mx[:, 0:P], ACT.Copy).then_inc(s_mact, 1)
                yield "tanh"
                mpe("proj")
                a(tanh_w[:, :], my[0:D, 2 * P:3 * P], ACT.Tanh).then_inc(s_mact, 1)
                a(lin_a[:, :], my[0:D, 3 * P:4 * P], ACT.Copy).then_inc(s_mact, 1)
                a(sig_g[:, :], mx[:, P:2 * P], ACT.Tanh, scale=0.5).then_inc(s_mact, 1)
                exp_and_ln()
                yield "tanh2"
                mpe("lora")
                a(sig_wa[:, 0, :], mx[0:D, 0:P], ACT.Tanh, scale=0.5, bias=v64h[:, 0:1]).then_inc(s_mact, 1)
                a(sig_wa[:, 1, :], mx[0:D, 320:448], ACT.Tanh, scale=0.5, bias=v64h[:, 1:2]).then_inc(s_mact, 1)
                a(gate[:, :], mx[:, 448:512], ACT.Copy).then_inc(s_mact, 1)
                exp_and_ln()
                yield "dec"
                dve("mid")
                a(dec_up[:, :], cdec[:, :], ACT.Exp, scale=DECAY, bias=mid[:, 0:1]).then_inc(s_mact, 1)
                a(dec_dn[:, :], cdec[:, 1:P + 1], ACT.Exp, scale=-DECAY, bias=mid[:, 1:2]).then_inc(s_mact, 1)
                yield "nrm"
                dve("nmax")
                a(kklog[:, :], kkn[:, :], ACT.Ln, scale=LN_SCALE).then_inc(s_mact, 1)
                own("nlog")
                a(kkn[:, :], kklog[:, :], ACT.Exp, scale=-0.5, bias=eps[0:D, 2:3]).then_inc(s_mact, 1)
                yield "olog"
                dve("omean")
                a(mlog[:, :], mv[:, 1:2], ACT.Ln, bias=eps[:, 1:2]).then_inc(s_mact, 1)
                own("olog")
                a(mrstd[:, :], mlog[:, :], ACT.Exp, scale=-0.5).then_inc(s_mact, 1)
                yield "og_tc"
                mpe("og_t")
                a(og_t[:, :], my[0:D, 256:384], ACT.Copy).then_inc(s_mact, 1)
                yield "log2"
                dve("mean2")
                a(mlog[:, :], mv[:, 1:2], ACT.Ln, bias=eps[:, 0:1]).then_inc(s_mact, 1)
                own("log2")
                a(mrstd[:, :], mlog[:, :], ACT.Exp, scale=-0.5).then_inc(s_mact, 1)
                yield "x2c"
                mpe("x2")
                if later:
                    act.wait_ge(s_handed, b)
                a(x2[:, :], mx[0:D, 0:P], ACT.Copy).then_inc(s_mact, 1)
                yield "simcp"
                mpe("sims")
                sm = sims[:, :, :, :].rearrange("p h s k -> p (h s k)")
                if later:
                    act.wait_ge(s_route, (b - 1) * NROUTE + R["idx_1"])
                a(sm[:, 0:512], my[:, :], ACT.Copy).then_inc(s_simcp, 1)
                a(sm[:, 512:1024], mx[:, :], ACT.Copy).then_inc(s_simcp, 1)
                yield "e0"
                act.wait_ge(s_route, b * NROUTE + R["shift"])
                a(fexp[:, :, :], fexp[:, :, :], ACT.Exp).then_inc(s_fexp, 1)

            def head(b, h):
                n = b * HEADS + h
                yield f"a{h}"
                act.wait_ge(s_got[h % NGB], (b * (HEADS // NGB) + h // NGB + 1) * 16 * TOPK)
                if h == 0:
                    act.wait_ge(s_handed, b + 1)
                for k in range(TOPK // 2):
                    a(got[:, h % NGB, k, :], got[:, h % NGB, k, :], ACT.Copy, scale=weight[:, h, k:k + 1])
                yield f"aa{h}"
                for k in range(TOPK // 2, TOPK):
                    last = a(got[:, h % NGB, k, :], got[:, h % NGB, k, :], ACT.Copy, scale=weight[:, h, k:k + 1])
                last.then_inc(s_scaled, 1)
                yield f"d{h}"
                act.wait_ge(s_q_ps, n + 1)
                a(qt[:, :], sc_bank[0:D, 384:512], ACT.Copy, scale=-(D ** -0.5)).then_inc(s_q, 1)
                yield f"f{h}"
                act.wait_ge(s_kv_ps, n + 1)
                a(kvt[:, :], kv_bank[:, 0:P], ACT.Copy).then_inc(s_kv, 1)
                yield f"i{h}"
                act.wait_ge(s_score, n + 1)
                if not isinstance(b, int) or n > 0:
                    act.wait_ge(s_y, n)
                a(vw[:, :], kv_bank[:, P:P + D], ACT.Copy).then_inc(s_vw, 1)
                yield f"j{h}"
                act.wait_ge(s_neg, n + 1)
                a(ex[:, :], neg[:, :], ACT.Exp, scale=-1.0, bias=nmax[:, :], accum_out=esum[:, :]).then_inc(s_exp, 1)
                yield f"m{h}"
                act.wait_ge(s_prob_ps, n + 1)
                a(prob_t[:, :], sc_bank[:, 256:384], ACT.Copy).then_inc(s_prob_t, 1)

            pipeline(act, tokenizer, mixer, in_turn(head, nothing, nothing), nothing)

        @block.vector
        def _(vec):
            v = nc.vector
            tt, ts, stt, cp = v.tensor_tensor, v.tensor_scalar, v.scalar_tensor_tensor, v.tensor_copy
            count = [0]

            def done(ins):
                count[0] += 1
                ins.then_inc(s_centred, 1)
                vec.wait_ge(s_centred, count[0])

            v.memset(eps[:, 0:1], EPS)
            v.memset(eps[:, 1:2], GN_EPS)
            v.memset(eps[:, 2:3], 0.5 * math.log(LN_SCALE))
            v.memset(ramp[:, :, :], 0.0)
            done(v.memset(cdec[:, :], 0.0))
            vec.wait_ge(s_loaded, 16 * NLOADS)
            for w, n in ((conv0_w, FR), (conv_w[1], 8), (conv_w[2], 4), (conv_w[3], 4)):
                wr = WIN if w is conv0_w else C
                done(v.tensor_reduce(wmean[0:wr, 0:n], w[:, :, :], AX.X, ALU.add))
                done(ts(wmean[0:wr, 0:n], wmean[0:wr, 0:n], 1.0 / C, None, ALU.mult))
                done(tt(w[:, :, :], w[:, :, :], wmean[0:wr, 0:n].unsqueeze(2).broadcast_to([wr, n, C]), ALU.subtract))
            for k, (at, w, row) in STACK.items():
                done(ts(proj[D:P, at:at + w], proj[D:P, at:at + w], mixc[D:P, row:row + 1], None, ALU.mult))
            done(ts(half_b3[:, :], mlpb[:, 2 * MC:], 0.5, None, ALU.mult))
            done(ts(v64h[:, 0:2], v64[:, 0:2], 0.5, None, ALU.mult))
            done(ts(v64h[:, 2:3], v64[:, 3:4], -1.0, 1.0, ALU.mult, ALU.add))
            vec.wait_ge(s_setup_pe, 2)
            done(cp(cbias[:, :], mx[:, 0:4]))
            rw = route_w[:, :, :, :].rearrange("p h s k -> p (h s k)")
            done(cp(rw[:, 0:512], conv_bank[0][0:D, :]))
            cp(rw[:, 512:1024], conv_bank[1][0:D, :]).then_inc(s_setup_done, 1)

            def norm(b, n):
                yield f"y{n + 1}"
                vec.wait_ge(s_rstd, b * 4 + n + 1)
                ps, w = level_bank(n)[:, 0:LEN[n]], LEN[n]
                stt(normed[:, n % 2, 0:w], ps, cbias[:, n + 1:n + 2] if n < 3 else 0.0, rstd[:, n % 2, 0:w],
                    ALU.add, ALU.mult).then_inc(s_norm, 1)

            def tokenizer(b):
                for r in range(4):
                    yield f"n{r}"
                    vec.wait_ge(s_rstd0, b * 4 + r + 1)
                    if r >= 2:
                        vec.wait_ge(s_h0, b * 4 + r - 1)
                    stt(normed[:, r % 2, :], conv_bank[r % 2][:, :], cbias[:, 0:1], rstd[:, r % 2, :],
                        ALU.add, ALU.mult).then_inc(s_norm0, 1)
                yield "pad0"
                vec.wait_ge(s_h0, b * 4 + 4)
                cp(h0[:, 0, 0:1], h0[:, 0, 1:2])
                cp(h0[:, 1, 0:1], h0[:, 3, 0:1])
                cp(h0[:, 2, T1:T1 + 1], h0[:, 0, T1:T1 + 1])
                cp(h0[:, 3, T1:T1 + 1], h0[:, 3, T1 - 1:T1]).then_inc(s_pad, 1)
                for n, (h, w) in enumerate(((h1, T1), (h2, T2))):
                    yield from norm(b, n)
                    yield f"pad{n + 1}"
                    vec.wait_ge(s_h, b * 4 + n + 1)
                    cp(h[:, 0:1], h[:, 2:3])
                    cp(h[:, w + 1:w + 2], h[:, w - 1:w]).then_inc(s_pad, 1)
                yield from norm(b, 2)
                yield "imp"
                vec.wait_ge(s_imp_t, b + 1)
                ts(imp[:, 1:2], imp[:, 0:1], 0.5, 0.5 + 1e-5, ALU.mult, ALU.add).then_inc(s_imp, 1)
                yield "ramp"
                vec.wait_ge(s_cums, b + 1)
                v.reciprocal(total[:, :], var_bank[:, 3:4]).then_inc(s_ramp, 1)
                vec.wait_ge(s_ramp, b * 6 + 1)
                ts(cums[:, :], var_bank[:, 1:3], total[:, :], float(D), ALU.mult, ALU.mult).then_inc(s_ramp, 1)
                vec.wait_ge(s_ramp, b * 6 + 2)
                ts(ramp[:, 0, 0:D], const("neg_iota"), cums[:, 0:1], 0.0, ALU.add, ALU.max).then_inc(s_ramp, 1)
                ts(ramp[:, 1, 0:D], const("neg_iota"), cums[:, 1:2], 0.0, ALU.add, ALU.max).then_inc(s_ramp, 1)
                vec.wait_ge(s_ramp, b * 6 + 4)
                tt(dramp[:, :], ramp[:, 0, :], ramp[:, 1, :], ALU.subtract).then_inc(s_ramp, 1)
                vec.wait_ge(s_ramp, b * 6 + 5)
                tt(wmat[:, :], dramp[:, 0:D], dramp[:, 1:D + 1], ALU.subtract).then_inc(s_ramp, 1)
                yield from norm(b, 3)

            def mixer(b):
                def step(key, ins):
                    ins.then_inc(s_mdve, 1)
                    wait = wait_apart if "stats" in key else type(vec).wait_ge
                    wait(vec, s_mdve, b * NV + V[key])

                act = lambda k: vec.wait_ge(s_mact, b * NA + A[k])
                mpe = lambda k: vec.wait_ge(s_mpe, b * NE + E[k])
                inv2 = inv[:, :, :].rearrange("p a t -> p (a t)")

                yield "stats"
                vec.wait_ge(s_h, b * 4 + 4)
                step("stats", v.bn_stats(stats[:, :], tok[:, :]))
                step("mean", v.bn_aggr(mv[:, :], stats[:, :]))
                yield "ln"
                act("rstd")
                step("ln", ts(ln[:, :], tok[:, :], mv[:, 0:1], mrstd[:, :], ALU.subtract, ALU.mult))
                yield "rk"
                act("tanh_g")
                step("rk", cp(rk[:, :, :].rearrange("p a t -> p (a t)"), my[0:D, 0:2 * P]))
                step("val", cp(val[:, :], mx[:, 2 * P:2 * P + D]))
                step("sig_g", ts(sig_g[:, :], sig_g[:, :], 0.5, 0.5, ALU.mult, ALU.add))
                yield "wa"
                act("tanh_sa")
                step("sig_wa", ts(sig_wa[:, :, :], sig_wa[:, :, :], 0.5, 0.5, ALU.mult, ALU.add))
                step("cdec", v.tensor_tensor_scan(cdec[:, 1:P + 1], const("ones", rows=D), sig_wa[:, 0, :], 0.0, ALU.mult, ALU.add))
                ts(mid[:, 0:1], cdec[:, P:P + 1], -0.5 * DECAY, None, ALU.mult)
                step("mid", ts(mid[:, 1:2], cdec[:, P:P + 1], 0.5 * DECAY, None, ALU.mult))
                step("kkr", ts(kkr[:, :], rk[:, 1, :], v64[:, 2:3], None, ALU.mult))
                step("kks", tt(kks[:, :], kkr[:, :], kkr[:, :], ALU.mult))
                yield "nmax"
                mpe("ss")
                step("nmax", ts(kkn[:, :], my[0:D, 384:512], NORM_MIN ** 2, None, ALU.max))
                yield "kk"
                act("nrm")
                step("kk", tt(kk[:, :], kkr[:, :], kkn[:, :], ALU.mult))
                step("kb", tt(kb[:, :], kk[:, :], sig_wa[:, 1, :], ALU.mult))
                step("kfac", ts(kfac[:, :], sig_wa[:, 1, :], v64[:, 3:4], v64h[:, 2:3], ALU.mult, ALU.add))
                step("k2", tt(k2[:, :], rk[:, 1, :], kfac[:, :], ALU.mult))
                step("left_k", tt(left[:, 0, :], kk[:, :], dec_up[:, 0:P], ALU.mult))
                step("left_r", tt(left[:, 1, :], rk[:, 0, :], dec_up[:, 1:P + 1], ALU.mult))
                step("right_b", tt(right[:, 0, :], kb[:, :], dec_dn[:, :], ALU.mult))
                step("right_k", tt(right[:, 1, :], k2[:, :], dec_dn[:, :], ALU.mult))
                step("rk2", tt(rk2[:, :], rk[:, 0, :], k2[:, :], ALU.mult))
                yield "trim"
                mpe("tri")
                step("tri", tt(tri[:, :, :].rearrange("p a t -> p (a t)"), mx[:, :], const("tri"), ALU.mult))
                step("inv0", tt(inv[:, 0, :], my[:, 0:P], const("pair"), ALU.mult))
                step("inv0b", tt(inv[:, 0, :], inv[:, 0, :], const("ident"), ALU.add))
                step("invt0", tt(inv[:, 1, :], tri[:, 0, :], const("pair_t"), ALU.mult))
                step("invt0b", tt(inv[:, 1, :], inv[:, 1, :], const("ident"), ALU.add))
                step("offs", tt(offs[:, :, :], const("merge_t").rearrange("p (l t) -> p l t", l=LEVELS),
                                tri[:, 0:1, :].broadcast_to([P, LEVELS, P]), ALU.mult))
                step("bonus", cp(bonus[:, :], my[:, P:P + 1]))
                for lv in range(LEVELS - 1):
                    yield f"pc{lv}"
                    mpe(f"p{lv}")
                    step(f"p{lv}", cp(prod[:, :], my[:, 256:384]))
                    yield f"tc{lv}"
                    mpe(f"t{lv}")
                    step(f"t{lv}", tt(inv2, mx[:, 0:256], inv2, ALU.add))
                yield "rhs0c"
                mpe("rhs0")
                step("rhs0", cp(rhs0[:, :], my[:, 384:448]))
                yield "sol1c"
                mpe("sol1")
                step("sol1", cp(sol1[:, :], my[:, 448:512]))
                yield "offsolc"
                mpe("offsol")
                step("offsol", cp(offsol[:, :], mx[:, 256:320]))
                yield "sa"
                mpe("sol2")
                step("sa", tt(sa[:, :], mx[:, 320:384], sol1[:, :], ALU.add))
                yield "ostats"
                mpe("o")
                step("ostats", v.bn_stats(stats[:, :], mx[:, 384:448]))
                step("omean", v.bn_aggr(mv[:, :], stats[:, :]))
                yield "og"
                act("orstd")
                step("on", ts(og[:, 0, :], mx[:, 384:448], mv[:, 0:1], mrstd[:, :], ALU.subtract, ALU.mult))
                step("ow", tt(og[:, 0, :], og[:, 0, :], gnb[:, 0, :], ALU.mult))
                step("ob", tt(og[:, 0, :], og[:, 0, :], gnb[:, 1, :], ALU.add))
                step("obonus", stt(og[:, 0, :], val[:, :], bonus[:, :], og[:, 0, :], ALU.mult, ALU.add))
                step("og", tt(og[:, 1, :], og[:, 0, :], gate[:, :], ALU.mult))
                yield "res"
                mpe("wo")
                step("res", tt(res[:, :], my[:, 384:448], tok[:, :], ALU.add))
                step("stats2", v.bn_stats(stats[:, :], res[:, :]))
                step("mean2", v.bn_aggr(mv[:, :], stats[:, :]))
                yield "ln2"
                act("rstd2")
                step("ln2", ts(ln[:, :], res[:, :], mv[:, 0:1], mrstd[:, :], ALU.subtract, ALU.mult))

            def route(b):
                def step(key, ins):
                    ins.then_inc(s_route, 1)
                    wait_apart(vec, s_route, b * NROUTE + R[key])

                for part in range(2):
                    yield f"r{5 * part}"
                    wait_apart(vec, s_simcp, b * 2 + part + 1)
                    lists = [(h, s) for h in range(4 * part, 4 * part + 4) for s in range(2)]
                    for h, s in lists:
                        last = v.max(top[:, 0, h, s, 0:8], sims[:, h, s, :])
                    step(f"top8_{part}", last)
                    yield f"r{5 * part + 1}"
                    for h, s in lists:
                        v.max_index(topi[:, h, s, 0:8], top[:, 0, h, s, 0:8], sims[:, h, s, :])
                    yield f"r{5 * part + 2}"
                    for h, s in lists:
                        last = v.match_replace(sims[:, h, s, :], top[:, 0, h, s, 0:8], sims[:, h, s, :], LOWEST)
                    step(f"rep_{part}", last)
                    yield f"r{5 * part + 3}"
                    for h, s in lists:
                        last = v.max(top[:, 0, h, s, 8:16], sims[:, h, s, :])
                    step(f"top16_{part}", last)
                    yield f"r{5 * part + 4}"
                    for h, s in lists:
                        last = v.max_index(topi[:, h, s, 8:16], top[:, 0, h, s, 8:16], sims[:, h, s, :])
                    step(f"idx_{part}", last)
                yield "keys"
                cp(top[:, 1, :, 0, :], topi[:, :, 0, :])
                step("keys", ts(top[:, 1, :, 1, :], topi[:, :, 1, :], float(NKEY), None, ALU.mult))
                yield "cands"
                tv = top[:, :, :, :, :].rearrange("p c h s r -> p (c h) s r")
                cv = cand[:, :, :, :].rearrange("p c h n -> p (c h) n")
                off = 0
                for i0, i1, nj in RECTS:
                    ni = i1 - i0
                    last = tt(cv[:, :, off:off + ni * nj].rearrange("p c (i j) -> p c i j", i=ni),
                              tv[:, :, 0, i0:i1].unsqueeze(3).broadcast_to([P, 2 * HEADS, ni, nj]),
                              tv[:, :, 1, 0:nj].unsqueeze(2).broadcast_to([P, 2 * HEADS, ni, nj]), ALU.add)
                    off += ni * nj
                step("cands", last)
                yield "fin8"
                for h in range(HEADS):
                    last = v.max(fin[:, h, 0:8], cand[:, 0, h, :])
                step("fin8", last)
                yield "finx"
                for h in range(HEADS):
                    v.max_index(finp[:, h, 0:8], fin[:, h, 0:8], cand[:, 0, h, :])
                yield "repf"
                for h in range(HEADS):
                    last = v.match_replace(cand[:, 0, h, :], fin[:, h, 0:8], cand[:, 0, h, :], LOWEST)
                step("rep_f", last)
                yield "fin16"
                for h in range(HEADS):
                    last = v.max(fin[:, h, 8:16], cand[:, 0, h, :])
                step("fin16", last)
                yield "fidx"
                for h in range(HEADS):
                    last = v.max_index(finp[:, h, 8:16], fin[:, h, 8:16], cand[:, 0, h, :])
                step("fidx", last)
                yield "shift"
                step("shift", tt(fexp[:, :, :], fin[:, :, :], fin[:, :, 0:1].broadcast_to([P, HEADS, TOPK]), ALU.subtract))
                yield "early"
                at = 0
                for start, (_, _, nj), (i0, i1, n) in zip(RECT_AT, RECTS, EARLY_RECTS):
                    ni = i1 - i0
                    last = cp(early[:, :, at:at + ni * n].rearrange("p h (i j) -> p h i j", i=ni),
                              cand[:, 1, :, start:start + ni * nj].rearrange("p h (i j) -> p h i j", i=ni)[:, :, :, 0:n])
                    at += ni * n
                step("early", last)
                for key, r0, places, numbers, tile, n in (("e", 0, "early_place", early[:, :, :], pick_e, NEARLY),
                                                          ("l", 8, "cand_iota", cand[:, 1, :, :], pick, NCAND)):
                    full = [P, HEADS, 8, n]
                    yield key + "0"
                    step("pick_" + key, tt(tile[:, :, :, :], finp[:, :, r0:r0 + 8].unsqueeze(3).broadcast_to(full),
                                           const(places).unsqueeze(1).unsqueeze(1).broadcast_to(full), ALU.is_equal))
                    yield key + "1"
                    step("sel_" + key, tt(tile[:, :, :, :], tile[:, :, :, :], numbers.unsqueeze(2).broadcast_to(full), ALU.mult))
                    yield key + "2"
                    step("row_" + key, v.tensor_reduce(rowf[:, :, r0:r0 + 8], tile[:, :, :, :], AX.X, ALU.add))
                yield "i_next"
                step("i_next", tt(i_next[:, :], rowf[:, :, :].rearrange("p h r -> p (h r)"), const("head_base"), ALU.add))
                yield "w_next"
                vec.wait_ge(s_fexp, b + 1)
                step("fsum", v.tensor_reduce(fsum[:, :], fexp[:, :, :], AX.X, ALU.add))
                step("frec", v.reciprocal(fsum[:, :], fsum[:, :]))
                step("w_next", tt(w_next[:, :, :], fexp[:, :, :], fsum[:, :].unsqueeze(2).broadcast_to([P, HEADS, TOPK]), ALU.mult))

            def hand_rows(b):
                if not isinstance(b, int) or b > 0:
                    for g in range(NGB):
                        vec.wait_ge(s_got[g], b * (HEADS // NGB) * 16 * TOPK)
                cp(rows[:, :], i_next[:, :]).then_inc(s_rows, 1)

            def head(b, h):
                n = b * HEADS + h
                later = not isinstance(b, int) or b > 0
                yield f"b{h}"
                vec.wait_ge(s_scaled, n + 1)
                if h >= 2 or later:
                    vec.wait_ge(s_kv_ps, n - 1)
                v.tensor_reduce(kv[:, h % 2, :], got[:, h % NGB, :, :].rearrange("p k d -> p d k"), AX.X, ALU.add).then_inc(s_sum, 1)
                yield f"i{h}"
                if h or later:
                    vec.wait_ge(s_exp, n)
                wait_apart(vec, s_score, n + 1)
                v.tensor_tensor_reduce(out=neg[:, :], in0=sc_bank[:, 0:P], in1=const("future"), scale=1.0, scalar=FUTURE,
                                       op0=ALU.add, op1=ALU.min, accum_out=nmax[:, :]).then_inc(s_neg, 1)
                yield f"k{h}"
                vec.wait_ge(s_exp, n + 1)
                v.reciprocal(erec[:, :], esum[:, :]).then_inc(s_erec, 1)
                vec.wait_ge(s_erec, n + 1)
                ts(prob[:, :], ex[:, :], erec[:, :], None, ALU.mult).then_inc(s_prob, 1)

            def out_of(b):
                yield "out"
                vec.wait_ge(s_y, b * HEADS + HEADS)
                if not isinstance(b, int) or b > 0:
                    vec.wait_ge(s_stored, b * 16)
                tt(res_o[:, :], y_bank[:, 0:D], res_h[:, :], ALU.add).then_inc(s_out, 1)

            def hand(b):
                yield "hand"
                if not isinstance(b, int) or b > 0:
                    vec.wait_ge(s_q_ps, b * HEADS)
                    vec.wait_ge(s_out, b)
                cp(weight[:, :, :], w_next[:, :, :])
                cp(res_h[:, :], res[:, :])
                cp(x2_h[:, :], x2[:, :]).then_inc(s_handed, 1)
                vec.wait_ge(s_handed, b + 1)

            def mixer_and_route(b):
                yield from mixer(b)
                yield from route(b)

            pipeline(vec, tokenizer, mixer_and_route, in_turn(head, hand, out_of), hand_rows)


_OUT = (BATCH, C, D)


def kernel(**inputs):
    import numpy as np
    import concourse.bacc as bacc
    from concourse.bass_utils import run_bass_kernel_spmd

    nc = bacc.Bacc("TRN2", target_bir_lowering=False, num_devices=1)
    t = {k[3:]: np.asarray(v) for k, v in inputs.items() if k != "x"}
    wave = np.pad(np.asarray(inputs["x"])[:, 0, :], ((0, 0), (PAD0, PAD0)), mode="reflect")
    wave = np.concatenate([wave, np.zeros((BATCH, (P + 1) * S0 * FR - wave.shape[1]), np.float32)], 1)
    conv = lambda n: np.transpose(t[f"tok_conv{n}_w"], (1, 2, 0))
    arrays = {
        "x": wave, "consts": constants(),
        "w0": np.transpose(t["tok_conv0_w"][:, 0, :]), "w1": conv(1), "w2": conv(2), "w3": conv(3),
        "cvec": np.stack([t[f"tok_conv{n}_b"] for n in range(4)] + [t[f"tok_n{n}_w"] for n in range(5)]
                         + [t[f"tok_n{n}_b"] for n in range(5)], 1),
        "mw1": t["tok_mlp_w1"], "mw2": t["tok_mlp_w2"], "mw3": np.transpose(t["tok_mlp_w3"].reshape(MC, P)),
        "mb12": np.transpose(np.concatenate([t["tok_mlp_b1"], t["tok_mlp_b2"]]).reshape(2 * MC, P)),
        "mb3": t["tok_mlp_b3"].reshape(1, 1),
        "stack": np.concatenate([t["attn_W_r"], t["attn_W_k"], t["attn_A_w"], t["attn_A_a"], t["attn_W_v"], t["attn_A_g"]], 1),
        "mix": np.transpose(t["attn_x_mix"]),
        "bw": t["attn_B_w"], "ba": t["attn_B_a"], "bg": t["attn_B_g"],
        "vec64": np.stack([t["attn_b_w"], t["attn_b_a"], t["attn_k_k"], t["attn_k_a"], t["attn_r_k"]], 1),
        "wo_attn": t["attn_W_o"], "gn": np.stack([t["attn_gn_w"], t["attn_gn_b"]]),
        "wqpk": np.transpose(t["ffn_Wq_pk"].reshape(D, 2, HEADS, 32), (3, 1, 2, 0)),
        "keys": np.transpose(t["ffn_pk_keys"], (3, 0, 2, 1)),
        "wq": t["ffn_Wq"], "table": np.concatenate([t["ffn_keys_table"], t["ffn_values_table"]], 1), "wo_ffn": t["ffn_Wo"],
    }
    arrays = {k: np.ascontiguousarray(a) for k, a in arrays.items()}
    aps = {k: nc.dram_tensor(f"in_{k}", a.shape, mybir.dt.from_np(a.dtype), kind="ExternalInput").ap() for k, a in arrays.items()}
    out = nc.dram_tensor("out_h", _OUT, F32, kind="ExternalOutput").ap()
    tower(nc, out=out, **aps)
    r = run_bass_kernel_spmd(nc, [{f"in_{k}": a for k, a in arrays.items()}], core_ids=[0])
    return r.results[0]["out_h"]
```

```python
import math

import concourse.bass as bass
from concourse import mybir
from contextlib import ExitStack

F32 = mybir.dt.float32
U32 = mybir.dt.uint32
ALU = mybir.AluOpType
ACT = mybir.ActivationFunctionType
AX = mybir.AxisListType

BATCH = 32
WAVE = 10240
C = 128
P = 128
D = 64
T0, T1, T2, T3 = 2048, 512, 256, 128
K0, S0, PAD0 = 10, 5, 3
FR = T0 // P
WIN = S0 * (FR - 1) + K0
MLP = 512
MC = MLP // P
HEADS = 8
NKEY = 64
TOPK = 16
HALF = HEADS // 2
LORA = 64
DECAY = -0.6065306597126334
RECTS = [(0, 1, 16), (1, 2, 8), (2, 4, 5), (4, 8, 3), (8, 16, 1)]
NCAND = sum((b - a) * n for a, b, n in RECTS)
EARLY_RECTS = [(0, 1, 8), (1, 2, 4), (2, 4, 2), (4, 8, 1)]
NEARLY = sum((b - a) * n for a, b, n in EARLY_RECTS)
RECT_AT = [sum((b - a) * n for a, b, n in RECTS[:k]) for k in range(len(RECTS))]
EARLY_PLACE = [at + i * nj + j for at, (_, _, nj), (a, b, n) in zip(RECT_AT, RECTS, EARLY_RECTS)
               for i in range(b - a) for j in range(n)]
LEVELS = 6
SUMS_LATE = 2
SCORES_LATE = 3
NGB = 4
EPS = 1e-5
GN_EPS = D * 1e-5
NORM_MIN = 1e-12
LN_SCALE = 2.0 ** 30
LOWEST = -3.0e38
FUTURE = 1.0e30

CONST = {}
_at = 0
for _name, _n in (("ident", P), ("mean_sq", P), ("ones", P), ("center", P), ("upto", P), ("before", P),
                  ("shift_diff", P), ("neg_iota", D), ("cand_iota", NCAND), ("early_place", NEARLY), ("head_base", HEADS * TOPK),
                  ("tri", 4 * P), ("pair", P), ("pair_t", P), ("merge_t", LEVELS * P), ("future", P)):
    CONST[_name] = (_at, _n)
    _at += _n
NCONST = _at
CONST_FIRST = CONST["upto"][0]

STACK = {"r": (0, 64, 0), "k": (64, 64, 2), "w": (128, 64, 1), "a": (192, 64, 4), "v": (256, 64, 3), "g": (320, 128, 5)}
NSTACK = 448


def constants():
    import numpy as np
    s, t = np.arange(P)[:, None], np.arange(P)[None, :]
    out = np.zeros((P, NCONST), np.float32)

    def put(name, a):
        at, n = CONST[name]
        out[:, at:at + n] = np.reshape(a, (a.shape[0], n)) if a.ndim > 1 else a

    put("ident", (s == t) * 1.0)
    put("mean_sq", np.full((P, P), 1.0 / (C - 1)))
    put("ones", np.ones((P, P)))
    put("center", (s == t) - 1.0 / C)
    put("upto", (s <= t) * 1.0)
    put("before", (s < t) * 1.0)
    put("shift_diff", (s == t - 1) * 1.0 - (s == t))
    put("neg_iota", -np.arange(D) * 1.0)
    put("cand_iota", np.arange(NCAND) * 1.0)
    put("early_place", np.array(EARLY_PLACE) * 1.0)
    put("head_base", np.repeat(np.arange(HEADS) * NKEY * NKEY, TOPK) * 1.0)
    put("tri", np.concatenate([-1.0 * (s < t), 1.0 * (s <= t), -1.0 * (s < t), 1.0 * (s <= t)], 1))
    put("pair", -1.0 * ((s % 2 == 1) & (t == s - 1)))
    put("pair_t", 1.0 * ((t % 2 == 1) & (s == t - 1)))
    merges = []
    for lv in range(1, LEVELS + 1):
        half = 2 ** lv
        merges.append(1.0 * ((s // (2 * half) == t // (2 * half)) & (t % (2 * half) >= half) & (s % (2 * half) < half)))
    put("merge_t", np.concatenate(merges, 1))
    put("future", FUTURE * (t > s))
    return out


def tower(nc, x, consts, w0, w1, w2, w3, cvec, mw1, mw2, mw3, mb12, mb3, stack, mix, bw, ba, bg, vec64,
          wo_attn, gn, wqpk, keys, wq, table, wo_ffn, out):
    ctx = ExitStack()
    with ctx:
        def sb(name, shape, dt=F32):
            return ctx.enter_context(nc.sbuf_tensor(name, shape, dt))

        def sem(name):
            return ctx.enter_context(nc.semaphore(name))

        cst = sb("cst", [P, NCONST])

        def const(name, a=0, b=None, rows=P):
            at, n = CONST[name]
            return cst[0:rows, at + a:at + (n if b is None else b)]

        conv0_w = sb("conv0_w", [WIN, FR, C])
        conv_w = {1: sb("conv1_w", [C, 8, C]), 2: sb("conv2_w", [C, 4, C]), 3: sb("conv3_w", [C, 4, C])}
        wmean = sb("wmean", [P, FR])
        chan = sb("chan", [C, 14])
        cbias = sb("cbias", [C, 4])
        mlp1 = sb("mlp1", [C, MLP])
        mlp2 = sb("mlp2", [P, MC, MLP])
        mlp3 = sb("mlp3", [P, MC])
        mlpb = sb("mlpb", [P, 2 * MC + 1])
        half_b3 = sb("half_b3", [P, 1])
        proj = sb("proj", [P, NSTACK])
        mixc = sb("mixc", [P, 6])
        lora_w = sb("lora_w", [LORA, D])
        lora_a = sb("lora_a", [LORA, D])
        lora_g = sb("lora_g", [P, D])
        v64 = sb("v64", [D, 5])
        v64h = sb("v64h", [D, 3])
        attn_wo = sb("attn_wo", [D, D])
        gnb = sb("gnb", [P, 2, D])
        qpk = sb("qpk", [32, 2, HEADS, D])
        pkk = sb("pkk", [32, 2, HEADS, NKEY])
        route_w = sb("route_w", [D, HEADS, 2, NKEY])
        ffn_wq = sb("ffn_wq", [D, HEADS * D])
        ffn_wo = sb("ffn_wo", [P, HEADS, D])
        eps = sb("eps", [P, 3])

        window = sb("window", [P, WIN])
        window_t = sb("window_t", [WIN, P])
        square = sb("square", [P, 2, 512])
        logv = sb("logv", [P, 512])
        rstd = sb("rstd", [P, 2, 512])
        normed = sb("normed", [P, 2, 512])
        h0 = sb("h0", [C, 4, T1 + 1])
        h1 = sb("h1", [C, T1 + 2])
        h2 = sb("h2", [C, T2 + 2])
        h3 = sb("h3", [C, T3])
        z1 = sb("z1", [P, MC, T3])
        z2 = sb("z2", [P, MC, T3])
        imp = sb("imp", [P, 2])
        total = sb("total", [P, 1])
        cums = sb("cums", [P, 2])
        ramp = sb("ramp", [P, 2, D + 1])
        dramp = sb("dramp", [P, D + 1])
        wmat = sb("wmat", [P, D])
        feat = sb("feat", [P, C])
        tok = sb("tok", [C, D])

        res = sb("res", [P, D])
        stats = sb("stats", [P, 6])
        mv = sb("mv", [P, 2])
        mlog = sb("mlog", [P, 1])
        mrstd = sb("mrstd", [P, 1])
        ln = sb("ln", [P, D])
        xd = sb("xd", [P, P])
        rk = sb("rk", [D, 2, P])
        val = sb("val", [P, D])
        tanh_w = sb("tanh_w", [LORA, P])
        lin_a = sb("lin_a", [LORA, P])
        sig_g = sb("sig_g", [P, P])
        sig_wa = sb("sig_wa", [D, 2, P])
        gate = sb("gate", [P, D])
        cdec = sb("cdec", [D, P + 1])
        mid = sb("mid", [D, 2])
        dec_up = sb("dec_up", [D, P + 1])
        dec_dn = sb("dec_dn", [D, P])
        kkr = sb("kkr", [D, P])
        kks = sb("kks", [D, P])
        kklog = sb("kklog", [D, P])
        kkn = sb("kkn", [D, P])
        kk = sb("kk", [D, P])
        kb = sb("kb", [D, P])
        kfac = sb("kfac", [D, P])
        k2 = sb("k2", [D, P])
        rk2 = sb("rk2", [D, P])
        left = sb("left", [D, 2, P])
        right = sb("right", [D, 2, P])
        tri = sb("tri", [P, 4, P])
        offs = sb("offs", [P, LEVELS, P])
        inv = sb("inv", [P, 2, P])
        prod = sb("prod", [P, P])
        rhs0 = sb("rhs0", [P, D])
        sol1 = sb("sol1", [P, D])
        offsol = sb("offsol", [P, D])
        sa = sb("sa", [P, D])
        bonus = sb("bonus", [P, 1])
        og = sb("og", [P, 2, D])
        og_t = sb("og_t", [D, P])
        x2 = sb("x2", [D, P])

        sims = sb("sims", [P, HEADS, 2, NKEY])
        top = sb("top", [P, 2, HEADS, 2, TOPK])
        topi = sb("topi", [P, HEADS, 2, TOPK], U32)
        cand = sb("cand", [P, 2, HEADS, NCAND])
        fin = sb("fin", [P, HEADS, TOPK])
        finp = sb("finp", [P, HEADS, TOPK], U32)
        early = sb("early", [P, HEADS, NEARLY])
        pick_e = sb("pick_e", [P, HEADS, 8, NEARLY])
        pick = sb("pick", [P, HEADS, 8, NCAND])
        rowf = sb("rowf", [P, HEADS, TOPK])
        fexp = sb("fexp", [P, HEADS, TOPK])
        fsum = sb("fsum", [P, HEADS])
        w_next = sb("w_next", [P, HEADS, TOPK])

        rows = sb("rows", [P, HEADS * TOPK], U32)
        weight = sb("weight", [P, HEADS, TOPK])
        res_h = sb("res_h", [P, D])
        x2_h = sb("x2_h", [D, P])
        got = sb("got", [P, NGB, TOPK, P])
        kv = sb("kv", [P, 2, P])
        qt = sb("qt", [D, P])
        kvt = sb("kvt", [P, P])
        vw = sb("vw", [P, D])
        neg = sb("neg", [P, P])
        nmax = sb("nmax", [P, 1])
        ex = sb("ex", [P, P])
        esum = sb("esum", [P, 1])
        erec = sb("erec", [P, 1])
        prob = sb("prob", [P, P])
        prob_t = sb("prob_t", [P, P])
        res_o = sb("res_o", [P, D])

        bank = [ctx.enter_context(nc.psum_tensor(f"bank{i}", [P, 512], F32)) for i in range(8)]
        conv_bank, var_bank = (bank[0], bank[1]), bank[2]
        mx, my = bank[3], bank[4]
        kv_bank, sc_bank, y_bank = bank[5], bank[6], bank[7]

        s_loaded_0 = sem("s_loaded_0")
        s_loaded_1 = sem("s_loaded_1")
        s_loaded_2 = sem("s_loaded_2")
        s_cleared = sem("s_cleared")
        s_centred = sem("s_centred")
        s_bias_ps = sem("s_bias_ps")
        s_conv0_ready = sem("s_conv0_ready")
        s_convs_ready = sem("s_convs_ready")
        s_rest_ready = sem("s_rest_ready")
        s_route_ps = sem("s_route_ps")
        s_route_w = sem("s_route_w")
        s_wave = sem("s_wave")
        s_window_ps = sem("s_window_ps")
        s_window_t = sem("s_window_t")
        s_conv0 = sem("s_conv0")
        s_sq0 = sem("s_sq0")
        s_var0 = sem("s_var0")
        s_log0 = sem("s_log0")
        s_rstd0 = sem("s_rstd0")
        s_norm0 = sem("s_norm0")
        s_h0 = sem("s_h0")
        s_pad = sem("s_pad")
        s_conv = sem("s_conv")
        s_sq = sem("s_sq")
        s_var = sem("s_var")
        s_log = sem("s_log")
        s_rstd = sem("s_rstd")
        s_norm = sem("s_norm")
        s_h = sem("s_h")
        s_z1p, s_z1, s_z2p, s_z2 = sem("s_z1p"), sem("s_z1"), sem("s_z2p"), sem("s_z2")
        s_z3p, s_imp_t, s_imp = sem("s_z3p"), sem("s_imp_t"), sem("s_imp")
        s_cums = sem("s_cums")
        s_ramp = sem("s_ramp")
        s_feat_ps, s_feat = sem("s_feat_ps"), sem("s_feat")
        s_mdve = sem("s_mdve")
        s_mact = sem("s_mact")
        s_mpe = sem("s_mpe")
        s_route = sem("s_route")
        s_ahead = sem("s_ahead")
        s_simcp = sem("s_simcp")
        s_fexp = sem("s_fexp")
        s_rows = sem("s_rows")
        s_weight = sem("s_weight")
        s_handed = sem("s_handed")
        s_got = [sem(f"s_got{i}") for i in range(NGB)]
        s_scaled = sem("s_scaled")
        s_sum = sem("s_sum")
        s_q_ps = sem("s_q_ps")
        s_q = sem("s_q")
        s_kv_ps = sem("s_kv_ps")
        s_kv = sem("s_kv")
        s_score = sem("s_score")
        s_vw = sem("s_vw")
        s_neg = sem("s_neg")
        s_exp = sem("s_exp")
        s_erec = sem("s_erec")
        s_prob = sem("s_prob")
        s_prob_ps = sem("s_prob_ps")
        s_prob_t = sem("s_prob_t")
        s_y = sem("s_y")
        s_waited = sem("s_waited")
        s_out = sem("s_out")
        s_stored = sem("s_stored")

        block = ctx.enter_context(nc.Block())

        def wait_apart(eng, sem, value):
            eng.wait_ge(sem, value)
            if not isinstance(value, int):
                eng.sem_inc(s_waited, 1)

        def level_bank(n):
            return conv_bank[(0, 1, 0, 0)[n]]

        LEN = (T1, T2, T3, D)
        V = {}
        for n, k in enumerate(("stats", "mean", "ln", "rk", "val", "sig_g", "sig_wa", "cdec", "mid", "kkr", "kks",
                               "nmax", "kk", "kb", "kfac", "k2", "left_k", "left_r", "right_b", "right_k", "rk2", "tri",
                               "inv0", "inv0b", "invt0", "invt0b", "offs", "bonus",
                               "p0", "t0", "p1", "t1", "p2", "t2", "p3", "t3", "p4", "t4",
                               "rhs0", "sol1", "offsol", "sa", "ostats", "omean", "on", "ow", "ob", "obonus", "og",
                               "res", "stats2", "mean2", "ln2"), 1):
            V[k] = n
        A = {}
        for n, k in enumerate(("log", "rstd", "xd", "tanh_w", "lin_a", "tanh_g", "tanh_sw", "tanh_sa", "gate",
                               "dec_up", "dec_dn", "nlog", "nrm", "olog", "orstd", "og_t", "log2", "rstd2", "x2"), 1):
            A[k] = n
        E = {}
        for n, k in enumerate(("xd", "proj", "lora", "ss", "tri", "p0", "t0", "p1", "t1", "p2", "t2", "p3", "t3", "p4", "t4",
                               "rhs0", "sol1", "offsol", "sol2", "o", "og_t", "wo", "x2", "sims"), 1):
            E[k] = n
        NV, NA, NE = len(V), len(A), len(E)
        R = {k: n for n, k in enumerate((
            "top8_0", "rep_0", "top16_0", "idx_0", "top8_1", "rep_1", "top16_1", "idx_1", "keys", "cands",
            "fin8", "rep_f", "fin16", "fidx", "shift", "early", "pick_e", "sel_e", "row_e", "pick_l", "sel_l", "row_l",
            "fsum", "frec", "w_next"), 1)}
        NROUTE = len(R)
        SCALES = 4

        def quarter(r):
            return [(f"v{r}", 1.2), (f"e{r}", 1.2), (f"n{r}", 1.0), (f"c{r + 2}", 1.6)]

        def layer(n):
            return [(f"k{n}", (6.8, 2, 1, 0.5)[n - 1]), (f"s{n}", 0.7), (f"w{n}", 1.0), (f"x{n}", 1.2), (f"y{n}", 0.8), (f"h{n}", 0.8)]

        def level(lv):
            return [(f"p{lv}", 0.7), (f"pc{lv}", 0.5), (f"t{lv}", 1.0), (f"tc{lv}", 0.6)]

        def head_hops(h):
            return [(f"d{h}", 1.2), (f"f{h}", 0.6), (f"g{h}", 1.5), (f"i{h}", 0.8),
                    (f"j{h}", 1.0), (f"k{h}", 1.0), (f"l{h}", 1.0), (f"m{h}", 0.6), (f"y{h}", 1.0)]

        def sum_hops(h):
            return [(f"a{h}{k}", 1.5) for k in range(0, TOPK, SCALES)] + [(f"b{h}", 2.4)]

        T_HOPS = ([("win", 1.0), ("win_t", 0.6), ("c0", 1.6), ("c1", 1.6)] + quarter(0) + quarter(1) + quarter(2) + quarter(3)
                  + [("pad0", 0.6)] + layer(1) + [("pad1", 0.5)] + layer(2) + [("pad2", 0.5)] + layer(3)
                  + [("z1p", 1.6), ("z1", 2.4), ("z2p", 6.5), ("z2", 2.6), ("z3p", 1.0), ("imp_t", 1.0), ("imp", 0.5), ("cums", 1.0),
                     ("ramp", 1.6), ("pool", 0.7)] + layer(4)[1:])
        MIX_HOPS = ([("stats", 0.6), ("log", 0.8), ("ln", 0.6), ("xd", 1.0), ("xd_t", 0.6), ("proj", 2.7), ("tanh", 1.8), ("rk", 1.5),
                   ("lora", 1.4), ("tanh2", 1.6), ("wa", 1.6), ("ss", 0.7), ("dec", 0.9), ("nmax", 0.5), ("nrm", 0.7), ("kk", 3.0),
                   ("tri", 3.0), ("trim", 3.2)] + [x for lv in range(LEVELS - 1) for x in level(lv)]
                  + [(k, 0.7) for k in ("rhs0", "rhs0c", "sol1", "sol1c", "offsol", "offsolc", "sol2", "sa", "o", "ostats", "olog")]
                  + [("og", 1.6), ("og_t", 0.7), ("og_tc", 0.6), ("wo", 0.7), ("res", 1.0), ("log2", 0.8), ("ln2", 0.6), ("x2", 0.7),
                     ("x2c", 0.6), ("sims", 3.6), ("simcp", 1.2)])

        TOP_HOPS = [(f"r{k}", t) for k, t in enumerate((1.2, 1.2, 2.2, 1.2, 1.2) * 2)]
        CHOOSE_HOPS = [("keys", 0.7), ("cands", 1.8), ("fin8", 1.2), ("finx", 1.2), ("repf", 2.0), ("fin16", 1.2), ("fidx", 1.2), ("shift", 0.3),
                       ("early", 0.5), ("e0", 1.5), ("e1", 1.5), ("e2", 1.5), ("l0", 3.8), ("l1", 3.8), ("l2", 3.8), ("rows", 0.4)]
        M_HOPS_0 = (MIX_HOPS + TOP_HOPS[0:5] + [("h_" + k, t / 2) for k, t in CHOOSE_HOPS if k != "shift"]
                    + TOP_HOPS[5:] + [(k, t / 2) for k, t in CHOOSE_HOPS] + [("w_next", 0.8)])
        M_HOPS = MIX_HOPS + TOP_HOPS + CHOOSE_HOPS + [("w_next", 0.8)]

        def heads_hops(prev, cur, late, of_head, first, last):
            before = [x for h in range(HEADS - late, HEADS) for x in of_head(h)] + last
            now = first + [x for h in range(HEADS - late) for x in of_head(h)]
            return [(n if prev is not None else None, t) for n, t in before] + [(n if cur is not None else None, t) for n, t in now]

        def merged(stages, spans):
            order = []
            for stage, (hops, (start, end)) in enumerate(zip(stages, spans)):
                total, at = sum(t for _, t in hops), 0.0
                for name, t in hops:
                    if name:
                        order.append((start + (end - start) * (at + t / 2) / total, stage, name))
                    at += t
            return [(stage, name) for _, stage, name in sorted(order)]

        def pipeline(eng, tokenizer, mixer, sums, scores):
            def step(tb, mb, prev, cur, spans=[(0.0, 1.0)] * 4):
                stages = (T_HOPS if tb is not None else [], [] if mb is None else M_HOPS_0 if isinstance(mb, int) and mb == 0 else M_HOPS,
                          heads_hops(prev, cur, SUMS_LATE, sum_hops, [("hand_w", 0.6)], []),
                          heads_hops(prev, cur, SCORES_LATE, head_hops, [("hand_x", 0.4)], [("out", 0.5)]))
                shares = [tokenizer(tb) if tb is not None else iter(()), mixer(mb) if mb is not None else iter(()),
                          sums(prev, cur), scores(prev, cur)]
                nxt = [next(g, None) for g in shares]
                for stage, name in merged(stages, spans):
                    if nxt[stage] == name:
                        nxt[stage] = next(shares[stage], None)
                assert nxt == [None] * 4, nxt

            step(0, None, None, None)
            step(1, 0, None, None, [(0.5, 1.15), (0.0, 1.0), (0.0, 1.0), (0.0, 1.0)])
            step(2, 1, None, 0, [(0.1, 1.0), (0.0, 0.85), (-0.3, 1.0), (-0.3, 1.0)])
            with eng.Fori(1, BATCH - 2) as b:
                step(b + 2, b + 1, b - 1, b)
            step(None, BATCH - 1, BATCH - 3, BATCH - 2)
            step(None, None, BATCH - 2, BATCH - 1)
            step(None, None, BATCH - 1, None)

        def in_turn(late, head, first, last):
            def heads(prev, cur):
                if prev is not None:
                    for h in range(HEADS - late, HEADS):
                        yield from head(prev, h)
                    yield from last(prev)
                if cur is not None:
                    yield from first(cur)
                    for h in range(HEADS - late):
                        yield from head(cur, h)
            return heads

        def nothing(*_):
            return iter(())

        LOADS_0 = [(cst[:, 0:CONST_FIRST], consts[:, 0:CONST_FIRST]), (chan[:, :], cvec)]
        LOADS_1 = [(conv_w[1][:, :, :], w1), (conv_w[2][:, :, :], w2), (conv_w[3][:, :, :], w3)]
        LOADS_2 = [(mlp1[:, :], mw1), (cst[:, CONST_FIRST:], consts[:, CONST_FIRST:]),
                 (mlp2[:, :, :], mw2.rearrange("(k p) n -> p k n", p=P)),
                 (mlp3[:, :], mw3), (mlpb[:, 0:2 * MC], mb12), (mlpb[:, 2 * MC:], mb3.broadcast_to([P, 1])),
                 (proj[0:D, :], stack), (proj[D:P, :], stack),
                 (lora_w[:, :], bw), (lora_a[:, :], ba), (lora_g[:, :], bg), (v64[:, :], vec64),
                 (attn_wo[:, :], wo_attn), (gnb[:, :, :], gn.rearrange("(o a) d -> o a d", o=1).broadcast_to([P, 2, D])),
                 (qpk[:, :, :, :], wqpk), (pkk[:, :, :, :], keys), (ffn_wq[:, :], wq),
                 (ffn_wo[D:P, :, :], wo_ffn.rearrange("(h d) n -> d h n", d=D))]
        FIRST, CONVS, REST = 16 * (len(LOADS_0) + FR), 16 * len(LOADS_1), 16 * (len(LOADS_2) + 1)

        @block.sync
        def _(sp):
            def load_wave(b):
                n = S0 * FR
                sp.dma_start(window[:, 0:n], x[bass.ds(b, 1), 0:P * n].rearrange("o (p n) -> (o p) n", p=P)).then_inc(s_wave, 16)
                sp.dma_start(window[:, n:WIN], x[bass.ds(b, 1), n:(P + 1) * n].rearrange("o (p n) -> (o p) n", p=P)[:, 0:WIN - n]).then_inc(s_wave, 16)

            def store(b):
                sp.wait_ge(s_out, b + 1)
                sp.dma_start(out[bass.ds(b, 1), :, :].rearrange("o c d -> (o c) d"), res_o[:, :]).then_inc(s_stored, 16)

            for dst, src in LOADS_0:
                sp.dma_start(dst, src).then_inc(s_loaded_0, 16)
            sp.wait_ge(s_cleared, 1)
            for j in range(FR):
                sp.dma_start(conv0_w[S0 * j:S0 * j + K0, j, :], w0).then_inc(s_loaded_0, 16)
            load_wave(0)
            for dst, src in LOADS_1:
                sp.dma_start(dst, src).then_inc(s_loaded_1, 16)
            for dst, src in LOADS_2:
                sp.dma_start(dst, src).then_inc(s_loaded_2, 16)
            sp.wait_ge(s_cleared, 2)
            sp.dma_start(mixc[D:P, :], mix).then_inc(s_loaded_2, 16)
            sp.wait_ge(s_window_ps, 1)
            load_wave(1)
            sp.wait_ge(s_window_ps, 2)
            load_wave(2)
            with sp.Fori(0, BATCH - 3) as b:
                sp.wait_ge(s_window_ps, b + 3)
                load_wave(b + 3)
                store(b)
            for b in range(BATCH - 3, BATCH):
                store(b)
            sp.wait_ge(s_stored, 16 * BATCH)

        @block.gpsimd
        def _(pool):
            nc.gpsimd.memset(conv0_w[:, :, :], 0.0).then_inc(s_cleared, 1)
            nc.gpsimd.memset(mixc[:, :], 1.0).then_inc(s_cleared, 1)

            def gathers(b):
                for h in range(HEADS):
                    if h % HALF == 0:
                        wait_apart(pool, s_rows, b * 2 + h // HALF + 1)
                    g = h % NGB
                    if h >= NGB or not isinstance(b, int):
                        wait_apart(pool, s_sum, b * HEADS + h - NGB + 1)
                    for k in range(TOPK):
                        pool.indirect_dma_start(got[:, g, k, :], None, table,
                                                bass.IndirectOffsetOnAxis(ap=rows[:, h * TOPK + k:h * TOPK + k + 1], axis=0)
                                                ).then_inc(s_got[g], 16)

            gathers(0)
            with pool.Fori(1, BATCH) as b:
                gathers(b)

        @block.tensor
        def _(pe):
            mm, tr = nc.tensor.matmul, nc.tensor.transpose
            pe.wait_ge(s_loaded_0, FIRST)
            mm(mx[:, 0:4], const("center"), chan[:, 0:4], start=True, stop=True).then_inc(s_bias_ps, 1)
            pe.wait_ge(s_conv0_ready, 1)

            def routing_weights():
                pe.wait_ge(s_loaded_2, REST)
                for n in range(2 * HEADS):
                    h, p = n // 2, n % 2
                    last = mm((sc_bank, y_bank)[n // 8][0:D, (n % 8) * NKEY:(n % 8 + 1) * NKEY], qpk[:, p, h, :], pkk[:, p, h, :],
                              start=True, stop=True)
                last.then_inc(s_route_ps, 1)

            def variance(b, n):
                pe.wait_ge(s_sq, b * 4 + n + 1)
                mm(var_bank[:, 0:LEN[n]], const("mean_sq"), square[:, n % 2, 0:LEN[n]], start=True, stop=True).then_inc(s_var, 1)

            def tokenizer(b):
                yield "win"
                pe.wait_ge(s_wave, 32 * (b + 1))
                if not isinstance(b, int) or b > 0:
                    pe.wait_ge(s_log, b * 4)
                tr(var_bank[0:WIN, 0:P], window[:, :], const("ident")).then_inc(s_window_ps, 1)
                yield "c0"
                pe.wait_ge(s_window_t, b + 1)
                conv0(b, 0)
                yield "c1"
                conv0(b, 1)
                for r in range(4):
                    yield f"v{r}"
                    pe.wait_ge(s_sq0, b * 4 + r + 1)
                    if r >= 1:
                        pe.wait_ge(s_log0, b * 4 + r)
                    mm(var_bank[:, :], const("mean_sq"), square[:, r % 2, :], start=True, stop=True).then_inc(s_var0, 1)
                    if r < 2:
                        yield f"c{r + 2}"
                        pe.wait_ge(s_norm0, b * 4 + r + 1)
                        conv0(b, r + 2)
                for n in (1, 2, 3):
                    yield f"k{n}"
                    pe.wait_ge(s_pad, b * 3 + n)
                    if isinstance(b, int) and b == 0 and n == 1:
                        pe.wait_ge(s_convs_ready, 1)
                    taps = 8 if n == 1 else 4
                    for k in range(taps):
                        if n == 1:
                            rhs = h0[:, k % 4, k // 4:k // 4 + T1]
                        else:
                            rhs = (h1 if n == 2 else h2)[:, k:k + 2 * LEN[n - 1] - 1:2]
                        last = mm(level_bank(n - 1)[:, 0:LEN[n - 1]], conv_w[n][:, k, :], rhs, start=k == 0, stop=k == taps - 1)
                    last.then_inc(s_conv, 1)
                    yield f"w{n}"
                    variance(b, n - 1)
                yield "z1p"
                if isinstance(b, int) and b == 0:
                    routing_weights()
                pe.wait_ge(s_h, b * 4 + 3)
                for m in range(MC):
                    last = mm(conv_bank[1][:, m * P:(m + 1) * P], mlp1[:, m * P:(m + 1) * P], h3[:, :], start=True, stop=True)
                last.then_inc(s_z1p, 1)
                yield "z2p"
                pe.wait_ge(s_z1, b + 1)
                for m in range(MC):
                    for k in range(MC):
                        last = mm(conv_bank[0][:, m * P:(m + 1) * P], mlp2[:, k, m * P:(m + 1) * P], z1[:, k, :], start=k == 0, stop=k == MC - 1)
                last.then_inc(s_z2p, 1)
                mm(conv_bank[1][:, 0:P], h3[:, :], const("center"), start=True, stop=True).then_inc(s_feat_ps, 1)
                yield "z3p"
                pe.wait_ge(s_z2, b + 1)
                for k in range(MC):
                    last = mm(var_bank[:, 0:1], z2[:, k, :], mlp3[:, k:k + 1], start=k == 0, stop=k == MC - 1)
                last.then_inc(s_z3p, 1)
                yield "cums"
                pe.wait_ge(s_imp, b + 1)
                mm(var_bank[:, 1:2], const("upto"), imp[:, 1:2], start=True, stop=True)
                mm(var_bank[:, 2:3], const("before"), imp[:, 1:2], start=True, stop=True)
                mm(var_bank[:, 3:4], const("ones"), imp[:, 1:2], start=True, stop=True).then_inc(s_cums, 1)
                yield "pool"
                pe.wait_ge(s_feat, b + 1)
                pe.wait_ge(s_ramp, b * 6 + 6)
                mm(conv_bank[0][:, 0:D], feat[:, :], wmat[:, :], start=True, stop=True).then_inc(s_conv, 1)
                yield "w4"
                variance(b, 3)

            def conv0(b, r):
                for q in range(4):
                    j = 4 * (q + (r < 2)) + r - 2
                    last = mm(conv_bank[r % 2][:, q:512:4], conv0_w[:, j, :], window_t[:, :], start=True, stop=True)
                last.then_inc(s_conv0, 1)

            def mixer(b):
                dve = lambda k: pe.wait_ge(s_mdve, b * NV + V[k])
                act = lambda k: pe.wait_ge(s_mact, b * NA + A[k])
                yield "xd"
                dve("ln")
                mm(mx[0:D, 0:P], ln[:, :], const("ident"), start=True, stop=True)
                mm(mx[D:P, 0:P], ln[:, :], const("shift_diff"), start=True, stop=True).then_inc(s_mpe, 1)
                yield "proj"
                act("xd")
                for n, k in enumerate("rkwa"):
                    at, w, _ = STACK[k]
                    mm(my[0:D, n * P:(n + 1) * P], proj[:, at:at + w], xd[:, :], start=True, stop=True)
                at, w, _ = STACK["g"]
                mm(mx[:, P:2 * P], proj[:, at:at + w], xd[:, :], start=True, stop=True)
                at, w, _ = STACK["v"]
                mm(mx[:, 2 * P:2 * P + D], xd[:, :], proj[:, at:at + w], start=True, stop=True).then_inc(s_mpe, 1)
                yield "lora"
                wait_apart(pe, s_mdve, b * NV + V["sig_g"])
                mm(mx[0:D, 0:P], lora_w[:, :], tanh_w[:, :], start=True, stop=True)
                mm(mx[0:D, 320:448], lora_a[:, :], lin_a[:, :], start=True, stop=True)
                mm(mx[:, 448:512], sig_g[:, :], lora_g[:, :], start=True, stop=True).then_inc(s_mpe, 1)
                yield "ss"
                wait_apart(pe, s_mdve, b * NV + V["kks"])
                mm(my[0:D, 384:512], const("ones", 0, D, rows=D), kks[:, :], start=True, stop=True).then_inc(s_mpe, 1)
                yield "tri"
                dve("rk2")
                act("gate")
                mm(mx[:, 0:256], right[:, 0, :], left[:, :, :].rearrange("p a t -> p (a t)"), start=True, stop=True)
                mm(mx[:, 256:512], right[:, 1, :], left[:, :, :].rearrange("p a t -> p (a t)"), start=True, stop=True)
                mm(my[:, 0:P], left[:, 0, :], right[:, 0, :], start=True, stop=True)
                mm(my[:, P:P + 1], rk2[:, :], v64[:, 4:5], start=True, stop=True).then_inc(s_mpe, 1)
                for lv in range(LEVELS - 1):
                    yield f"p{lv}"
                    dve("bonus" if lv == 0 else f"t{lv - 1}")
                    mm(my[:, 256:384], offs[:, lv, :], inv[:, 0, :], start=True, stop=True).then_inc(s_mpe, 1)
                    yield f"t{lv}"
                    dve(f"p{lv}")
                    mm(mx[:, 0:P], inv[:, 1, :], prod[:, :], start=True, stop=True)
                    mm(mx[:, P:2 * P], prod[:, :], inv[:, 1, :], start=True, stop=True).then_inc(s_mpe, 1)
                yield "rhs0"
                mm(my[:, 384:448], tri[:, 2, :], val[:, :], start=True, stop=True).then_inc(s_mpe, 1)
                yield "sol1"
                dve("rhs0")
                mm(my[:, 448:512], inv[:, 1, :], rhs0[:, :], start=True, stop=True).then_inc(s_mpe, 1)
                yield "offsol"
                dve("sol1")
                mm(mx[:, 256:320], offs[:, LEVELS - 1, :], sol1[:, :], start=True, stop=True).then_inc(s_mpe, 1)
                yield "sol2"
                dve("offsol")
                mm(mx[:, 320:384], inv[:, 1, :], offsol[:, :], start=True, stop=True).then_inc(s_mpe, 1)
                yield "o"
                dve("sa")
                mm(mx[:, 384:448], tri[:, 1, :], sa[:, :], start=True, stop=False)
                mm(mx[:, 384:448], tri[:, 3, :], val[:, :], start=False, stop=True).then_inc(s_mpe, 1)
                yield "og_t"
                wait_apart(pe, s_mdve, b * NV + V["og"])
                tr(my[0:D, 256:384], og[:, 1, :], const("ident")).then_inc(s_mpe, 1)
                yield "wo"
                wait_apart(pe, s_mact, b * NA + A["og_t"])
                mm(my[:, 384:448], og_t[:, :], attn_wo[:, :], start=True, stop=True).then_inc(s_mpe, 1)
                yield "x2"
                wait_apart(pe, s_mdve, b * NV + V["ln2"])
                tr(mx[0:D, 0:P], ln[:, :], const("ident")).then_inc(s_mpe, 1)
                yield "sims"
                act("x2")
                if isinstance(b, int) and b == 0:
                    pe.wait_ge(s_route_w, 1)
                rw = route_w[:, :, :, :].rearrange("p h s k -> p (h s k)")
                mm(my[:, :], x2[:, :], rw[:, 0:512], start=True, stop=True)
                mm(mx[:, :], x2[:, :], rw[:, 512:1024], start=True, stop=True).then_inc(s_mpe, 1)

            def head(b, h):
                n = b * HEADS + h
                yield f"d{h}"
                if h == 0:
                    wait_apart(pe, s_handed, b + 1)
                mm(sc_bank[0:D, 384:512], ffn_wq[:, h * D:(h + 1) * D], x2_h[:, :], start=True, stop=True).then_inc(s_q_ps, 1)
                pe.wait_ge(s_sum, n + 1)
                tr(kv_bank[:, 0:P], kv[:, h % 2, :], const("ident")).then_inc(s_kv_ps, 1)
                yield f"g{h}"
                pe.wait_ge(s_q, n + 1)
                pe.wait_ge(s_kv, n + 1)
                mm(sc_bank[:, 0:P], qt[:, :], kvt[0:D, :], start=True, stop=True)
                mm(kv_bank[:, P:P + D], kvt[D:P, :], ffn_wo[D:P, h, :], start=True, stop=True).then_inc(s_score, 1)
                yield f"l{h}"
                pe.wait_ge(s_prob, n + 1)
                tr(sc_bank[:, 256:384], prob[:, :], const("ident")).then_inc(s_prob_ps, 1)
                yield f"y{h}"
                pe.wait_ge(s_prob_t, n + 1)
                pe.wait_ge(s_vw, n + 1)
                if h == 0 and (not isinstance(b, int) or b > 0):
                    pe.wait_ge(s_out, b)
                mm(y_bank[:, 0:D], prob_t[:, :], vw[:, :], start=h == 0, stop=h == HEADS - 1).then_inc(s_y, 1)

            pipeline(pe, tokenizer, mixer, nothing, in_turn(SCORES_LATE, head, nothing, nothing))

        @block.scalar
        def _(act):
            a = nc.scalar.activation
            exp_and_ln = lambda: nc.scalar.preload_act_table_set("natural_log_exp_and_others")
            exp_and_ln()
            act.wait_ge(s_conv0_ready, 1)

            def sq0(b, r):
                act.wait_ge(s_conv0, b * 4 + r + 1)
                if r >= 2:
                    act.wait_ge(s_var0, b * 4 + r - 1)
                a(square[:, r % 2, :], conv_bank[r % 2][:, :], ACT.Square, bias=cbias[:, 0:1]).then_inc(s_sq0, 1)

            def tokenizer(b):
                yield "win_t"
                act.wait_ge(s_window_ps, b + 1)
                a(window_t[:, :], var_bank[0:WIN, 0:P], ACT.Copy).then_inc(s_window_t, 1)
                yield "c1"
                sq0(b, 0)
                for r in range(4):
                    if r < 3:
                        yield f"v{r}"
                        sq0(b, r + 1)
                    yield f"e{r}"
                    act.wait_ge(s_var0, b * 4 + r + 1)
                    if r >= 2:
                        act.wait_ge(s_norm0, b * 4 + r - 1)
                    if r or not isinstance(b, int) or b > 0:
                        act.wait_ge(s_rstd0, b * 4 + r)
                    a(logv[:, :], var_bank[:, :], ACT.Ln, bias=eps[:, 0:1]).then_inc(s_log0, 1)
                    act.wait_ge(s_log0, b * 4 + r + 1)
                    a(rstd[:, r % 2, :], logv[:, :], ACT.Exp, scale=-0.5).then_inc(s_rstd0, 1)
                    yield f"c{r + 2}"
                    act.wait_ge(s_norm0, b * 4 + r + 1)
                    u = int(r < 2)
                    a(h0[:, r, u:u + T1], normed[:, r % 2, :], ACT.Relu, scale=chan[:, 4:5], bias=chan[:, 9:10]).then_inc(s_h0, 1)
                yield from norm(b, 0, h1[:, 1:T1 + 1])
                yield from norm(b, 1, h2[:, 1:T2 + 1])
                yield from norm(b, 2, h3[:, :])
                yield "z1"
                if isinstance(b, int) and b == 0:
                    act.wait_ge(s_loaded_2, REST)
                    act.wait_ge(s_rest_ready, 1)
                act.wait_ge(s_z1p, b + 1)
                for m in range(MC):
                    last = a(z1[:, m, :], conv_bank[1][:, m * P:(m + 1) * P], ACT.Gelu, bias=mlpb[:, m:m + 1])
                last.then_inc(s_z1, 1)
                exp_and_ln()
                yield "z2"
                act.wait_ge(s_z2p, b + 1)
                for m in range(MC):
                    last = a(z2[:, m, :], conv_bank[0][:, m * P:(m + 1) * P], ACT.Gelu, bias=mlpb[:, MC + m:MC + m + 1])
                last.then_inc(s_z2, 1)
                exp_and_ln()
                act.wait_ge(s_feat_ps, b + 1)
                a(feat[:, :], conv_bank[1][:, 0:P], ACT.Copy).then_inc(s_feat, 1)
                yield "imp_t"
                act.wait_ge(s_z3p, b + 1)
                a(imp[:, 0:1], var_bank[:, 0:1], ACT.Tanh, scale=0.5, bias=half_b3[:, :]).then_inc(s_imp_t, 1)
                exp_and_ln()
                yield from norm(b, 3, tok[:, :])

            def norm(b, n, dst):
                w, ps = LEN[n], level_bank(n)[:, 0:LEN[n]]
                yield f"s{n + 1}"
                act.wait_ge(s_conv, b * 4 + n + 1)
                a(square[:, n % 2, 0:w], ps, ACT.Square, bias=cbias[:, n + 1:n + 2] if n < 3 else 0.0).then_inc(s_sq, 1)
                yield f"x{n + 1}"
                act.wait_ge(s_var, b * 4 + n + 1)
                if n:
                    act.wait_ge(s_rstd, b * 4 + n)
                else:
                    act.wait_ge(s_rstd0, b * 4 + 4)
                a(logv[:, 0:w], var_bank[:, 0:w], ACT.Ln, bias=eps[:, 0:1]).then_inc(s_log, 1)
                act.wait_ge(s_log, b * 4 + n + 1)
                a(rstd[:, n % 2, 0:w], logv[:, 0:w], ACT.Exp, scale=-0.5).then_inc(s_rstd, 1)
                yield f"h{n + 1}"
                act.wait_ge(s_norm, b * 4 + n + 1)
                if n == 3 and (not isinstance(b, int) or b > 0):
                    act.wait_ge(s_mdve, (b - 1) * NV + V["res"])
                a(dst, normed[:, n % 2, 0:w], ACT.Relu, scale=chan[:, 5 + n:6 + n], bias=chan[:, 10 + n:11 + n]).then_inc(s_h, 1)

            def mixer(b):
                dve = lambda k: act.wait_ge(s_mdve, b * NV + V[k])
                mpe = lambda k: act.wait_ge(s_mpe, b * NE + E[k])
                own = lambda k: act.wait_ge(s_mact, b * NA + A[k])
                later = not isinstance(b, int) or b > 0
                yield "log"
                dve("mean")
                a(mlog[:, :], mv[:, 1:2], ACT.Ln, bias=eps[:, 0:1]).then_inc(s_mact, 1)
                own("log")
                a(mrstd[:, :], mlog[:, :], ACT.Exp, scale=-0.5).then_inc(s_mact, 1)
                yield "xd_t"
                mpe("xd")
                a(xd[:, :], mx[:, 0:P], ACT.Copy).then_inc(s_mact, 1)
                yield "tanh"
                mpe("proj")
                a(tanh_w[:, :], my[0:D, 2 * P:3 * P], ACT.Tanh).then_inc(s_mact, 1)
                a(lin_a[:, :], my[0:D, 3 * P:4 * P], ACT.Copy).then_inc(s_mact, 1)
                a(sig_g[:, :], mx[:, P:2 * P], ACT.Tanh, scale=0.5).then_inc(s_mact, 1)
                exp_and_ln()
                yield "tanh2"
                mpe("lora")
                a(sig_wa[:, 0, :], mx[0:D, 0:P], ACT.Tanh, scale=0.5, bias=v64h[:, 0:1]).then_inc(s_mact, 1)
                a(sig_wa[:, 1, :], mx[0:D, 320:448], ACT.Tanh, scale=0.5, bias=v64h[:, 1:2]).then_inc(s_mact, 1)
                a(gate[:, :], mx[:, 448:512], ACT.Copy).then_inc(s_mact, 1)
                exp_and_ln()
                yield "dec"
                dve("mid")
                a(dec_up[:, :], cdec[:, :], ACT.Exp, scale=DECAY, bias=mid[:, 0:1]).then_inc(s_mact, 1)
                a(dec_dn[:, :], cdec[:, 1:P + 1], ACT.Exp, scale=-DECAY, bias=mid[:, 1:2]).then_inc(s_mact, 1)
                yield "nrm"
                dve("nmax")
                a(kklog[:, :], kkn[:, :], ACT.Ln, scale=LN_SCALE).then_inc(s_mact, 1)
                own("nlog")
                a(kkn[:, :], kklog[:, :], ACT.Exp, scale=-0.5, bias=eps[0:D, 2:3]).then_inc(s_mact, 1)
                yield "olog"
                dve("omean")
                a(mlog[:, :], mv[:, 1:2], ACT.Ln, bias=eps[:, 1:2]).then_inc(s_mact, 1)
                own("olog")
                a(mrstd[:, :], mlog[:, :], ACT.Exp, scale=-0.5).then_inc(s_mact, 1)
                yield "og_tc"
                mpe("og_t")
                a(og_t[:, :], my[0:D, 256:384], ACT.Copy).then_inc(s_mact, 1)
                yield "log2"
                dve("mean2")
                a(mlog[:, :], mv[:, 1:2], ACT.Ln, bias=eps[:, 0:1]).then_inc(s_mact, 1)
                own("log2")
                a(mrstd[:, :], mlog[:, :], ACT.Exp, scale=-0.5).then_inc(s_mact, 1)
                yield "x2c"
                mpe("x2")
                if later:
                    act.wait_ge(s_handed, b)
                a(x2[:, :], mx[0:D, 0:P], ACT.Copy).then_inc(s_mact, 1)
                yield "simcp"
                mpe("sims")
                sm = sims[:, :, :, :].rearrange("p h s k -> p (h s k)")
                if later:
                    act.wait_ge(s_route, (b - 1) * NROUTE + R["idx_1"])
                a(sm[:, 0:512], my[:, :], ACT.Copy).then_inc(s_simcp, 1)
                a(sm[:, 512:1024], mx[:, :], ACT.Copy).then_inc(s_simcp, 1)
                yield "e0"
                act.wait_ge(s_route, b * NROUTE + R["shift"])
                a(fexp[:, :, :], fexp[:, :, :], ACT.Exp).then_inc(s_fexp, 1)

            def weighted(b, h):
                for k0 in range(0, TOPK, SCALES):
                    yield f"a{h}{k0}"
                    if k0 == 0:
                        act.wait_ge(s_got[h % NGB], (b * (HEADS // NGB) + h // NGB + 1) * 16 * TOPK)
                        if h == 0:
                            act.wait_ge(s_weight, b + 1)
                    for k in range(k0, k0 + SCALES):
                        last = a(got[:, h % NGB, k, :], got[:, h % NGB, k, :], ACT.Copy, scale=weight[:, h, k:k + 1])
                last.then_inc(s_scaled, 1)

            def head(b, h):
                n = b * HEADS + h
                yield f"d{h}"
                act.wait_ge(s_q_ps, n + 1)
                a(qt[:, :], sc_bank[0:D, 384:512], ACT.Copy, scale=-(D ** -0.5)).then_inc(s_q, 1)
                yield f"f{h}"
                act.wait_ge(s_kv_ps, n + 1)
                a(kvt[:, :], kv_bank[:, 0:P], ACT.Copy).then_inc(s_kv, 1)
                yield f"i{h}"
                act.wait_ge(s_score, n + 1)
                if not isinstance(b, int) or n > 0:
                    act.wait_ge(s_y, n)
                a(vw[:, :], kv_bank[:, P:P + D], ACT.Copy).then_inc(s_vw, 1)
                yield f"j{h}"
                act.wait_ge(s_neg, n + 1)
                a(ex[:, :], neg[:, :], ACT.Exp, scale=-1.0, bias=nmax[:, :], accum_out=esum[:, :]).then_inc(s_exp, 1)
                yield f"m{h}"
                act.wait_ge(s_prob_ps, n + 1)
                a(prob_t[:, :], sc_bank[:, 256:384], ACT.Copy).then_inc(s_prob_t, 1)

            pipeline(act, tokenizer, mixer, in_turn(SUMS_LATE, weighted, nothing, nothing), in_turn(SCORES_LATE, head, nothing, nothing))

        @block.vector
        def _(vec):
            v = nc.vector
            tt, ts, stt, cp = v.tensor_tensor, v.tensor_scalar, v.scalar_tensor_tensor, v.tensor_copy
            count = [0]

            def done(ins):
                count[0] += 1
                ins.then_inc(s_centred, 1)
                vec.wait_ge(s_centred, count[0])

            v.memset(eps[:, 0:1], EPS)
            v.memset(eps[:, 1:2], GN_EPS)
            v.memset(eps[:, 2:3], 0.5 * math.log(LN_SCALE))
            v.memset(ramp[:, :, :], 0.0)
            done(v.memset(cdec[:, :], 0.0))
            def centre(w, n):
                wr = WIN if w is conv0_w else C
                done(v.tensor_reduce(wmean[0:wr, 0:n], w[:, :, :], AX.X, ALU.add))
                done(ts(wmean[0:wr, 0:n], wmean[0:wr, 0:n], 1.0 / C, None, ALU.mult))
                return tt(w[:, :, :], w[:, :, :], wmean[0:wr, 0:n].unsqueeze(2).broadcast_to([wr, n, C]), ALU.subtract)

            vec.wait_ge(s_bias_ps, 1)
            done(cp(cbias[:, :], mx[:, 0:4]))
            vec.wait_ge(s_loaded_0, FIRST)
            centre(conv0_w, FR).then_inc(s_conv0_ready, 1)
            vec.wait_ge(s_conv0_ready, 1)
            vec.wait_ge(s_loaded_1, CONVS)
            done(centre(conv_w[1], 8))
            done(centre(conv_w[2], 4))
            centre(conv_w[3], 4).then_inc(s_convs_ready, 1)

            def rest_of_setup():
                vec.wait_ge(s_loaded_2, REST)
                for k, (at, w, row) in STACK.items():
                    ts(proj[D:P, at:at + w], proj[D:P, at:at + w], mixc[D:P, row:row + 1], None, ALU.mult)
                ts(half_b3[:, :], mlpb[:, 2 * MC:], 0.5, None, ALU.mult)
                ts(v64h[:, 0:2], v64[:, 0:2], 0.5, None, ALU.mult)
                ts(v64h[:, 2:3], v64[:, 3:4], -1.0, 1.0, ALU.mult, ALU.add).then_inc(s_rest_ready, 1)
                vec.wait_ge(s_rest_ready, 1)

            def copy_routing_weights():
                vec.wait_ge(s_route_ps, 1)
                rw = route_w[:, :, :, :].rearrange("p h s k -> p (h s k)")
                cp(rw[:, 0:512], sc_bank[0:D, :])
                cp(rw[:, 512:1024], y_bank[0:D, :]).then_inc(s_route_w, 1)

            def norm(b, n):
                yield f"y{n + 1}"
                vec.wait_ge(s_rstd, b * 4 + n + 1)
                ps, w = level_bank(n)[:, 0:LEN[n]], LEN[n]
                stt(normed[:, n % 2, 0:w], ps, cbias[:, n + 1:n + 2] if n < 3 else 0.0, rstd[:, n % 2, 0:w],
                    ALU.add, ALU.mult).then_inc(s_norm, 1)

            def tokenizer(b):
                for r in range(4):
                    yield f"n{r}"
                    vec.wait_ge(s_rstd0, b * 4 + r + 1)
                    if r >= 2:
                        vec.wait_ge(s_h0, b * 4 + r - 1)
                    stt(normed[:, r % 2, :], conv_bank[r % 2][:, :], cbias[:, 0:1], rstd[:, r % 2, :],
                        ALU.add, ALU.mult).then_inc(s_norm0, 1)
                yield "pad0"
                vec.wait_ge(s_h0, b * 4 + 4)
                cp(h0[:, 0, 0:1], h0[:, 0, 1:2])
                cp(h0[:, 1, 0:1], h0[:, 3, 0:1])
                cp(h0[:, 2, T1:T1 + 1], h0[:, 0, T1:T1 + 1])
                cp(h0[:, 3, T1:T1 + 1], h0[:, 3, T1 - 1:T1]).then_inc(s_pad, 1)
                if isinstance(b, int) and b == 0:
                    rest_of_setup()
                for n, (h, w) in enumerate(((h1, T1), (h2, T2))):
                    yield from norm(b, n)
                    yield f"pad{n + 1}"
                    vec.wait_ge(s_h, b * 4 + n + 1)
                    cp(h[:, 0:1], h[:, 2:3])
                    cp(h[:, w + 1:w + 2], h[:, w - 1:w]).then_inc(s_pad, 1)
                yield from norm(b, 2)
                yield "imp"
                vec.wait_ge(s_imp_t, b + 1)
                ts(imp[:, 1:2], imp[:, 0:1], 0.5, 0.5 + 1e-5, ALU.mult, ALU.add).then_inc(s_imp, 1)
                yield "ramp"
                vec.wait_ge(s_cums, b + 1)
                v.reciprocal(total[:, :], var_bank[:, 3:4]).then_inc(s_ramp, 1)
                vec.wait_ge(s_ramp, b * 6 + 1)
                ts(cums[:, :], var_bank[:, 1:3], total[:, :], float(D), ALU.mult, ALU.mult).then_inc(s_ramp, 1)
                vec.wait_ge(s_ramp, b * 6 + 2)
                ts(ramp[:, 0, 0:D], const("neg_iota"), cums[:, 0:1], 0.0, ALU.add, ALU.max).then_inc(s_ramp, 1)
                ts(ramp[:, 1, 0:D], const("neg_iota"), cums[:, 1:2], 0.0, ALU.add, ALU.max).then_inc(s_ramp, 1)
                vec.wait_ge(s_ramp, b * 6 + 4)
                tt(dramp[:, :], ramp[:, 0, :], ramp[:, 1, :], ALU.subtract).then_inc(s_ramp, 1)
                vec.wait_ge(s_ramp, b * 6 + 5)
                tt(wmat[:, :], dramp[:, 0:D], dramp[:, 1:D + 1], ALU.subtract).then_inc(s_ramp, 1)
                yield from norm(b, 3)

            def mixer(b):
                def step(key, ins):
                    ins.then_inc(s_mdve, 1)
                    wait = wait_apart if "stats" in key else type(vec).wait_ge
                    wait(vec, s_mdve, b * NV + V[key])

                act = lambda k: vec.wait_ge(s_mact, b * NA + A[k])
                mpe = lambda k: vec.wait_ge(s_mpe, b * NE + E[k])
                inv2 = inv[:, :, :].rearrange("p a t -> p (a t)")

                yield "stats"
                vec.wait_ge(s_h, b * 4 + 4)
                step("stats", v.bn_stats(stats[:, :], tok[:, :]))
                step("mean", v.bn_aggr(mv[:, :], stats[:, :]))
                yield "ln"
                act("rstd")
                step("ln", ts(ln[:, :], tok[:, :], mv[:, 0:1], mrstd[:, :], ALU.subtract, ALU.mult))
                yield "rk"
                if isinstance(b, int) and b == 0:
                    copy_routing_weights()
                act("tanh_g")
                step("rk", cp(rk[:, :, :].rearrange("p a t -> p (a t)"), my[0:D, 0:2 * P]))
                step("val", cp(val[:, :], mx[:, 2 * P:2 * P + D]))
                step("sig_g", ts(sig_g[:, :], sig_g[:, :], 0.5, 0.5, ALU.mult, ALU.add))
                yield "wa"
                act("tanh_sa")
                step("sig_wa", ts(sig_wa[:, :, :], sig_wa[:, :, :], 0.5, 0.5, ALU.mult, ALU.add))
                step("cdec", v.tensor_tensor_scan(cdec[:, 1:P + 1], const("ones", rows=D), sig_wa[:, 0, :], 0.0, ALU.mult, ALU.add))
                ts(mid[:, 0:1], cdec[:, P:P + 1], -0.5 * DECAY, None, ALU.mult)
                step("mid", ts(mid[:, 1:2], cdec[:, P:P + 1], 0.5 * DECAY, None, ALU.mult))
                step("kkr", ts(kkr[:, :], rk[:, 1, :], v64[:, 2:3], None, ALU.mult))
                step("kks", tt(kks[:, :], kkr[:, :], kkr[:, :], ALU.mult))
                yield "nmax"
                mpe("ss")
                step("nmax", ts(kkn[:, :], my[0:D, 384:512], NORM_MIN ** 2, None, ALU.max))
                yield "kk"
                act("nrm")
                step("kk", tt(kk[:, :], kkr[:, :], kkn[:, :], ALU.mult))
                step("kb", tt(kb[:, :], kk[:, :], sig_wa[:, 1, :], ALU.mult))
                step("kfac", ts(kfac[:, :], sig_wa[:, 1, :], v64[:, 3:4], v64h[:, 2:3], ALU.mult, ALU.add))
                step("k2", tt(k2[:, :], rk[:, 1, :], kfac[:, :], ALU.mult))
                step("left_k", tt(left[:, 0, :], kk[:, :], dec_up[:, 0:P], ALU.mult))
                step("left_r", tt(left[:, 1, :], rk[:, 0, :], dec_up[:, 1:P + 1], ALU.mult))
                step("right_b", tt(right[:, 0, :], kb[:, :], dec_dn[:, :], ALU.mult))
                step("right_k", tt(right[:, 1, :], k2[:, :], dec_dn[:, :], ALU.mult))
                step("rk2", tt(rk2[:, :], rk[:, 0, :], k2[:, :], ALU.mult))
                yield "trim"
                mpe("tri")
                step("tri", tt(tri[:, :, :].rearrange("p a t -> p (a t)"), mx[:, :], const("tri"), ALU.mult))
                step("inv0", tt(inv[:, 0, :], my[:, 0:P], const("pair"), ALU.mult))
                step("inv0b", tt(inv[:, 0, :], inv[:, 0, :], const("ident"), ALU.add))
                step("invt0", tt(inv[:, 1, :], tri[:, 0, :], const("pair_t"), ALU.mult))
                step("invt0b", tt(inv[:, 1, :], inv[:, 1, :], const("ident"), ALU.add))
                step("offs", tt(offs[:, :, :], const("merge_t").rearrange("p (l t) -> p l t", l=LEVELS),
                                tri[:, 0:1, :].broadcast_to([P, LEVELS, P]), ALU.mult))
                step("bonus", cp(bonus[:, :], my[:, P:P + 1]))
                for lv in range(LEVELS - 1):
                    yield f"pc{lv}"
                    mpe(f"p{lv}")
                    step(f"p{lv}", cp(prod[:, :], my[:, 256:384]))
                    yield f"tc{lv}"
                    mpe(f"t{lv}")
                    step(f"t{lv}", tt(inv2, mx[:, 0:256], inv2, ALU.add))
                yield "rhs0c"
                mpe("rhs0")
                step("rhs0", cp(rhs0[:, :], my[:, 384:448]))
                yield "sol1c"
                mpe("sol1")
                step("sol1", cp(sol1[:, :], my[:, 448:512]))
                yield "offsolc"
                mpe("offsol")
                step("offsol", cp(offsol[:, :], mx[:, 256:320]))
                yield "sa"
                mpe("sol2")
                step("sa", tt(sa[:, :], mx[:, 320:384], sol1[:, :], ALU.add))
                yield "ostats"
                mpe("o")
                step("ostats", v.bn_stats(stats[:, :], mx[:, 384:448]))
                step("omean", v.bn_aggr(mv[:, :], stats[:, :]))
                yield "og"
                act("orstd")
                step("on", ts(og[:, 0, :], mx[:, 384:448], mv[:, 0:1], mrstd[:, :], ALU.subtract, ALU.mult))
                step("ow", tt(og[:, 0, :], og[:, 0, :], gnb[:, 0, :], ALU.mult))
                step("ob", tt(og[:, 0, :], og[:, 0, :], gnb[:, 1, :], ALU.add))
                step("obonus", stt(og[:, 0, :], val[:, :], bonus[:, :], og[:, 0, :], ALU.mult, ALU.add))
                step("og", tt(og[:, 1, :], og[:, 0, :], gate[:, :], ALU.mult))
                yield "res"
                mpe("wo")
                step("res", tt(res[:, :], my[:, 384:448], tok[:, :], ALU.add))
                step("stats2", v.bn_stats(stats[:, :], res[:, :]))
                step("mean2", v.bn_aggr(mv[:, :], stats[:, :]))
                yield "ln2"
                act("rstd2")
                step("ln2", ts(ln[:, :], res[:, :], mv[:, 0:1], mrstd[:, :], ALU.subtract, ALU.mult))

            def rows_to_gpsimd(b, half):
                if not isinstance(b, int) or b > 0:
                    for h in range(half * HALF, (half + 1) * HALF):
                        vec.wait_ge(s_got[h % NGB], ((b - 1) * (HEADS // NGB) + h // NGB + 1) * 16 * TOPK)
                a, z = half * HALF * TOPK, (half + 1) * HALF * TOPK
                tt(rows[:, a:z], rowf[:, :, :].rearrange("p h r -> p (h r)")[:, a:z], const("head_base", a, z), ALU.add).then_inc(s_rows, 1)

            def route(b):
                def step(key, ins):
                    ins.then_inc(s_route, 1)
                    wait_apart(vec, s_route, b * NROUTE + R[key])

                first = isinstance(b, int) and b == 0
                for part in range(2):
                    yield f"r{5 * part}"
                    wait_apart(vec, s_simcp, b * 2 + part + 1)
                    lists = [(h, s) for h in range(4 * part, 4 * part + 4) for s in range(2)]
                    for h, s in lists:
                        last = v.max(top[:, 0, h, s, 0:8], sims[:, h, s, :])
                    step(f"top8_{part}", last)
                    yield f"r{5 * part + 1}"
                    for h, s in lists:
                        v.max_index(topi[:, h, s, 0:8], top[:, 0, h, s, 0:8], sims[:, h, s, :])
                    yield f"r{5 * part + 2}"
                    for h, s in lists:
                        last = v.match_replace(sims[:, h, s, :], top[:, 0, h, s, 0:8], sims[:, h, s, :], LOWEST)
                    step(f"rep_{part}", last)
                    yield f"r{5 * part + 3}"
                    for h, s in lists:
                        last = v.max(top[:, 0, h, s, 8:16], sims[:, h, s, :])
                    step(f"top16_{part}", last)
                    yield f"r{5 * part + 4}"
                    for h, s in lists:
                        last = v.max_index(topi[:, h, s, 8:16], top[:, 0, h, s, 8:16], sims[:, h, s, :])
                    step(f"idx_{part}", last)
                    if first and part == 0:
                        yield from choose(slice(0, HALF), "h_", step_ahead)
                        yield "h_rows"
                        rows_to_gpsimd(b, 0)
                yield from choose(slice(HALF, HEADS) if first else slice(0, HEADS), "", step)
                yield "rows"
                rows_to_gpsimd(b, int(first))
                yield "w_next"
                vec.wait_ge(s_fexp, b + 1)
                step("fsum", v.tensor_reduce(fsum[:, :], fexp[:, :, :], AX.X, ALU.add))
                step("frec", v.reciprocal(fsum[:, :], fsum[:, :]))
                step("w_next", tt(w_next[:, :, :], fexp[:, :, :], fsum[:, :].unsqueeze(2).broadcast_to([P, HEADS, TOPK]), ALU.mult))

            ahead = [0]

            def step_ahead(key, ins):
                ahead[0] += 1
                ins.then_inc(s_ahead, 1)
                vec.wait_ge(s_ahead, ahead[0])

            def choose(heads, name, step):
                some = range(HEADS)[heads]
                n_heads = len(some)
                yield name + "keys"
                cp(top[:, 1, heads, 0, :], topi[:, heads, 0, :])
                step("keys", ts(top[:, 1, heads, 1, :], topi[:, heads, 1, :], float(NKEY), None, ALU.mult))
                yield name + "cands"
                for c in range(2):
                    off = 0
                    for i0, i1, nj in RECTS:
                        ni = i1 - i0
                        full = [P, n_heads, ni, nj]
                        last = tt(cand[:, c, heads, off:off + ni * nj].rearrange("p h (i j) -> p h i j", i=ni),
                                  top[:, c, heads, 0, i0:i1].unsqueeze(3).broadcast_to(full),
                                  top[:, c, heads, 1, 0:nj].unsqueeze(2).broadcast_to(full), ALU.add)
                        off += ni * nj
                step("cands", last)
                yield name + "fin8"
                for h in some:
                    last = v.max(fin[:, h, 0:8], cand[:, 0, h, :])
                step("fin8", last)
                yield name + "finx"
                for h in some:
                    v.max_index(finp[:, h, 0:8], fin[:, h, 0:8], cand[:, 0, h, :])
                yield name + "repf"
                for h in some:
                    last = v.match_replace(cand[:, 0, h, :], fin[:, h, 0:8], cand[:, 0, h, :], LOWEST)
                step("rep_f", last)
                yield name + "fin16"
                for h in some:
                    last = v.max(fin[:, h, 8:16], cand[:, 0, h, :])
                step("fin16", last)
                yield name + "fidx"
                for h in some:
                    last = v.max_index(finp[:, h, 8:16], fin[:, h, 8:16], cand[:, 0, h, :])
                step("fidx", last)
                if name == "":
                    yield "shift"
                    step("shift", tt(fexp[:, :, :], fin[:, :, :], fin[:, :, 0:1].broadcast_to([P, HEADS, TOPK]), ALU.subtract))
                yield name + "early"
                at = 0
                for start, (_, _, nj), (i0, i1, n) in zip(RECT_AT, RECTS, EARLY_RECTS):
                    ni = i1 - i0
                    last = cp(early[:, heads, at:at + ni * n].rearrange("p h (i j) -> p h i j", i=ni),
                              cand[:, 1, heads, start:start + ni * nj].rearrange("p h (i j) -> p h i j", i=ni)[:, :, :, 0:n])
                    at += ni * n
                step("early", last)
                for key, r0, places, numbers, tile, n in (("e", 0, "early_place", early[:, heads, :], pick_e, NEARLY),
                                                          ("l", 8, "cand_iota", cand[:, 1, heads, :], pick, NCAND)):
                    full, tile = [P, n_heads, 8, n], tile[:, heads, :, :]
                    yield name + key + "0"
                    step("pick_" + key, tt(tile, finp[:, heads, r0:r0 + 8].unsqueeze(3).broadcast_to(full),
                                           const(places).unsqueeze(1).unsqueeze(1).broadcast_to(full), ALU.is_equal))
                    yield name + key + "1"
                    step("sel_" + key, tt(tile, tile, numbers.unsqueeze(2).broadcast_to(full), ALU.mult))
                    yield name + key + "2"
                    step("row_" + key, v.tensor_reduce(rowf[:, heads, r0:r0 + 8], tile, AX.X, ALU.add))

            def weighted(b, h):
                n = b * HEADS + h
                yield f"b{h}"
                vec.wait_ge(s_scaled, n + 1)
                if h >= 2 or not isinstance(b, int) or b > 0:
                    vec.wait_ge(s_kv_ps, n - 1)
                v.tensor_reduce(kv[:, h % 2, :], got[:, h % NGB, :, :].rearrange("p k d -> p d k"), AX.X, ALU.add).then_inc(s_sum, 1)

            def head(b, h):
                n = b * HEADS + h
                yield f"i{h}"
                if h or not isinstance(b, int) or b > 0:
                    vec.wait_ge(s_exp, n)
                wait_apart(vec, s_score, n + 1)
                v.tensor_tensor_reduce(out=neg[:, :], in0=sc_bank[:, 0:P], in1=const("future"), scale=1.0, scalar=FUTURE,
                                       op0=ALU.add, op1=ALU.min, accum_out=nmax[:, :]).then_inc(s_neg, 1)
                yield f"k{h}"
                vec.wait_ge(s_exp, n + 1)
                v.reciprocal(erec[:, :], esum[:, :]).then_inc(s_erec, 1)
                vec.wait_ge(s_erec, n + 1)
                ts(prob[:, :], ex[:, :], erec[:, :], None, ALU.mult).then_inc(s_prob, 1)

            def out_of(b):
                yield "out"
                vec.wait_ge(s_y, b * HEADS + HEADS)
                if not isinstance(b, int) or b > 0:
                    vec.wait_ge(s_stored, b * 16)
                tt(res_o[:, :], y_bank[:, 0:D], res_h[:, :], ALU.add).then_inc(s_out, 1)

            def hand_weights(b):
                yield "hand_w"
                if not isinstance(b, int) or b > 0:
                    rows_to_gpsimd(b, 1)
                    vec.wait_ge(s_scaled, b * HEADS)
                cp(weight[:, :, :], w_next[:, :, :]).then_inc(s_weight, 1)

            def hand_tokens(b):
                yield "hand_x"
                if not isinstance(b, int) or b > 0:
                    vec.wait_ge(s_q_ps, b * HEADS)
                    vec.wait_ge(s_out, b)
                cp(res_h[:, :], res[:, :])
                cp(x2_h[:, :], x2[:, :]).then_inc(s_handed, 1)
                vec.wait_ge(s_handed, b + 1)

            def mixer_and_route(b):
                yield from mixer(b)
                yield from route(b)

            pipeline(vec, tokenizer, mixer_and_route, in_turn(SUMS_LATE, weighted, hand_weights, nothing),
                     in_turn(SCORES_LATE, head, hand_tokens, out_of))


_OUT = (BATCH, C, D)


def kernel(**inputs):
    import numpy as np
    import concourse.bacc as bacc
    from concourse.bass_utils import run_bass_kernel_spmd

    nc = bacc.Bacc("TRN2", target_bir_lowering=False, num_devices=1)
    t = {k[3:]: np.asarray(v) for k, v in inputs.items() if k != "x"}
    wave = np.pad(np.asarray(inputs["x"])[:, 0, :], ((0, 0), (PAD0, PAD0)), mode="reflect")
    wave = np.concatenate([wave, np.zeros((BATCH, (P + 1) * S0 * FR - wave.shape[1]), np.float32)], 1)
    conv = lambda n: np.transpose(t[f"tok_conv{n}_w"], (1, 2, 0))
    arrays = {
        "x": wave, "consts": constants(),
        "w0": np.transpose(t["tok_conv0_w"][:, 0, :]), "w1": conv(1), "w2": conv(2), "w3": conv(3),
        "cvec": np.stack([t[f"tok_conv{n}_b"] for n in range(4)] + [t[f"tok_n{n}_w"] for n in range(5)]
                         + [t[f"tok_n{n}_b"] for n in range(5)], 1),
        "mw1": t["tok_mlp_w1"], "mw2": t["tok_mlp_w2"], "mw3": np.transpose(t["tok_mlp_w3"].reshape(MC, P)),
        "mb12": np.transpose(np.concatenate([t["tok_mlp_b1"], t["tok_mlp_b2"]]).reshape(2 * MC, P)),
        "mb3": t["tok_mlp_b3"].reshape(1, 1),
        "stack": np.concatenate([t["attn_W_r"], t["attn_W_k"], t["attn_A_w"], t["attn_A_a"], t["attn_W_v"], t["attn_A_g"]], 1),
        "mix": np.transpose(t["attn_x_mix"]),
        "bw": t["attn_B_w"], "ba": t["attn_B_a"], "bg": t["attn_B_g"],
        "vec64": np.stack([t["attn_b_w"], t["attn_b_a"], t["attn_k_k"], t["attn_k_a"], t["attn_r_k"]], 1),
        "wo_attn": t["attn_W_o"], "gn": np.stack([t["attn_gn_w"], t["attn_gn_b"]]),
        "wqpk": np.transpose(t["ffn_Wq_pk"].reshape(D, 2, HEADS, 32), (3, 1, 2, 0)),
        "keys": np.transpose(t["ffn_pk_keys"], (3, 0, 2, 1)),
        "wq": t["ffn_Wq"], "table": np.concatenate([t["ffn_keys_table"], t["ffn_values_table"]], 1), "wo_ffn": t["ffn_Wo"],
    }
    arrays = {k: np.ascontiguousarray(a) for k, a in arrays.items()}
    aps = {k: nc.dram_tensor(f"in_{k}", a.shape, mybir.dt.from_np(a.dtype), kind="ExternalInput").ap() for k, a in arrays.items()}
    out = nc.dram_tensor("out_h", _OUT, F32, kind="ExternalOutput").ap()
    tower(nc, out=out, **aps)
    r = run_bass_kernel_spmd(nc, [{f"in_{k}": a for k, a in arrays.items()}], core_ids=[0])
    return r.results[0]["out_h"]
```
